# Optimizing a Trainium2 kernel written in Bass

```python
import numpy as np
import jax
import jax.numpy as jnp

def _softmax(x, axis=-1):
    return jax.nn.softmax(x, axis=axis)

def _gelu(x):
    return jax.nn.gelu(x, approximate=True)

def _silu(x):
    return jax.nn.silu(x)

def _sigmoid(x):
    return jax.nn.sigmoid(x)

def _layernorm(x, axis=-1, eps=1e-05):
    m = jnp.mean(x, axis=axis, keepdims=True)
    v = jnp.var(x, axis=axis, keepdims=True)
    return (x - m) / jnp.sqrt(v + eps)

def _scatter_add(tgt, idx, src, axis=0):
    return tgt.at[idx].add(src)

def _segment_sum(src, seg, n):
    return jax.ops.segment_sum(src, seg, n)
kernel_name = 'mk_cond_seq_d1_seqx_r2_9217c8'

def setup_inputs(seed: int=0):
    np.random.seed(seed)
    _w = jnp.asarray

    def _rec_inputs():
        import jax
        import jax.numpy as jnp
        _rk = jax.random.key(seed)
        x = 1.648e-05 + 1 * jax.random.normal(jax.random.fold_in(_rk, 1), (2, 2048, 576), jnp.float32)
        _lenS = 2048 - jax.random.randint(jax.random.fold_in(_rk, 7), (2,), 0, max(1, 2048 // 4) + 1, jnp.int32)
        _lenS2 = 2048 - jax.random.randint(jax.random.fold_in(_rk, 8), (2,), 0, max(1, 2048 // 4) + 1, jnp.int32)
        cond_1152 = 0.00914911 + 1.00357 * jax.random.normal(jax.random.fold_in(_rk, 11), (2, 576), jnp.float32)
        return (x, cond_1152)
    x, cond_1152 = _rec_inputs()

    def _L0_cond_setup():
        import jax, jax.numpy as jnp
        import numpy as np
        DIM = 576
        HEADS = 16
        HEAD_DIM = DIM // HEADS
        HIDDEN = int(DIM * 4.0)
        EPS = 1e-12

        def rmsnorm(x, g, d):
            n = jnp.linalg.norm(x, axis=-1, keepdims=True)
            return x / jnp.maximum(n, EPS) * d ** 0.5 * g

        def modulate(x, scale, shift):
            return x * (1.0 + scale[:, None, :]) + shift[:, None, :]
        key = jax.random.key(seed)
        ks = jax.random.split(key, 12)
        B, N = (8, 512)
        s = 0.02
        return {'x': jax.random.normal(ks[0], (B, N, DIM), jnp.float32), 'c': jax.random.normal(ks[1], (B, DIM), jnp.float32), 'g1': jnp.ones((1,), jnp.float32), 'g2': jnp.ones((1,), jnp.float32), 'qkv_w': jax.random.normal(ks[2], (3 * DIM, DIM), jnp.float32) * s, 'qkv_b': jnp.zeros((3 * DIM,), jnp.float32), 'qg': jnp.ones((1,), jnp.float32), 'kg': jnp.ones((1,), jnp.float32), 'proj_w': jax.random.normal(ks[3], (DIM, DIM), jnp.float32) * s, 'proj_b': jnp.zeros((DIM,), jnp.float32), 'fc1_w': jax.random.normal(ks[4], (HIDDEN, DIM), jnp.float32) * s, 'fc1_b': jnp.zeros((HIDDEN,), jnp.float32), 'fc2_w': jax.random.normal(ks[5], (DIM, HIDDEN), jnp.float32) * s, 'fc2_b': jnp.zeros((DIM,), jnp.float32), 'ada_w': jax.random.normal(ks[6], (6 * DIM, DIM), jnp.float32) * s, 'ada_b': jnp.zeros((6 * DIM,), jnp.float32)}
    _L0_cond_all = _L0_cond_setup()
    _L0_cond_in = {k: v for k, v in _L0_cond_all.items() if k in ('g1', 'g2', 'qkv_w', 'qkv_b', 'qg', 'kg', 'proj_w', 'proj_b', 'fc1_w', 'fc1_b', 'fc2_w', 'fc2_b', 'ada_w', 'ada_b')}
    del _L0_cond_all
    return {'x': x, 'cond_1152': cond_1152, 'L0_cond_g1': _L0_cond_in['g1'], 'L0_cond_g2': _L0_cond_in['g2'], 'L0_cond_qkv_w': _L0_cond_in['qkv_w'], 'L0_cond_qkv_b': _L0_cond_in['qkv_b'], 'L0_cond_qg': _L0_cond_in['qg'], 'L0_cond_kg': _L0_cond_in['kg'], 'L0_cond_proj_w': _L0_cond_in['proj_w'], 'L0_cond_proj_b': _L0_cond_in['proj_b'], 'L0_cond_fc1_w': _L0_cond_in['fc1_w'], 'L0_cond_fc1_b': _L0_cond_in['fc1_b'], 'L0_cond_fc2_w': _L0_cond_in['fc2_w'], 'L0_cond_fc2_b': _L0_cond_in['fc2_b'], 'L0_cond_ada_w': _L0_cond_in['ada_w'], 'L0_cond_ada_b': _L0_cond_in['ada_b']}

def reference(x, cond_1152, L0_cond_g1, L0_cond_g2, L0_cond_qkv_w, L0_cond_qkv_b, L0_cond_qg, L0_cond_kg, L0_cond_proj_w, L0_cond_proj_b, L0_cond_fc1_w, L0_cond_fc1_b, L0_cond_fc2_w, L0_cond_fc2_b, L0_cond_ada_w, L0_cond_ada_b):
    import jax
    import jax.numpy as jnp

    def _L0_cond_ref(x, c, g1, g2, qkv_w, qkv_b, qg, kg, proj_w, proj_b, fc1_w, fc1_b, fc2_w, fc2_b, ada_w, ada_b):
        import jax, jax.numpy as jnp
        import numpy as np
        DIM = 576
        HEADS = 16
        HEAD_DIM = DIM // HEADS
        HIDDEN = int(DIM * 4.0)
        EPS = 1e-12

        def rmsnorm(x, g, d):
            n = jnp.linalg.norm(x, axis=-1, keepdims=True)
            return x / jnp.maximum(n, EPS) * d ** 0.5 * g

        def modulate(x, scale, shift):
            return x * (1.0 + scale[:, None, :]) + shift[:, None, :]
        B, N, D = x.shape
        mod = jax.nn.silu(c) @ ada_w.T + ada_b
        shift_msa, scale_msa, gate_msa, shift_mlp, scale_mlp, gate_mlp = jnp.split(mod, 6, axis=-1)
        gate_msa = jnp.tanh(gate_msa)
        gate_mlp = jnp.tanh(gate_mlp)
        h = modulate(rmsnorm(x, g1, D), scale_msa, shift_msa)
        qkv = h @ qkv_w.T + qkv_b
        qkv = qkv.reshape(B, N, 3, HEADS, HEAD_DIM).transpose(2, 0, 3, 1, 4)
        q, k, v = (qkv[0], qkv[1], qkv[2])
        q = rmsnorm(q, qg, HEAD_DIM)
        k = rmsnorm(k, kg, HEAD_DIM)
        q = q * HEAD_DIM ** (-0.5)
        attn = jax.nn.softmax(jnp.einsum('bhqd,bhkd->bhqk', q, k), axis=-1)
        o = jnp.einsum('bhqk,bhkd->bhqd', attn, v)
        o = o.transpose(0, 2, 1, 3).reshape(B, N, D)
        o = o @ proj_w.T + proj_b
        x = x + gate_msa[:, None, :] * o
        h2 = modulate(rmsnorm(x, g2, D), scale_mlp, shift_mlp)
        m = jax.nn.gelu(h2 @ fc1_w.T + fc1_b, approximate=True) @ fc2_w.T + fc2_b
        x = x + gate_mlp[:, None, :] * m
        return x
    x = _L0_cond_ref(x, cond_1152, L0_cond_g1, L0_cond_g2, L0_cond_qkv_w, L0_cond_qkv_b, L0_cond_qg, L0_cond_kg, L0_cond_proj_w, L0_cond_proj_b, L0_cond_fc1_w, L0_cond_fc1_b, L0_cond_fc2_w, L0_cond_fc2_b, L0_cond_ada_w, L0_cond_ada_b)
    return x

_drawn_inputs = setup_inputs


def setup_inputs(seed=0):
    import zlib

    import numpy as np

    out = dict(_drawn_inputs(seed))
    spreads = {'L0_cond_qkv_b': (0.0, 0.588),
     'L0_cond_proj_b': (0.0, 0.285),
     'L0_cond_fc1_b': (0.0, 0.498),
     'L0_cond_fc2_b': (0.0, 0.278),
     'L0_cond_ada_b': (0.0, 0.1)}
    factors = {'L0_cond_qkv_w': 3.176}
    for name, (base, spread) in spreads.items():
        noise = np.random.default_rng([zlib.crc32(name.encode()), seed]).standard_normal(out[name].shape)
        drawn = base * np.exp(spread * noise) if base else spread * noise
        out[name] = jnp.asarray(drawn.astype(out[name].dtype))
    for name, factor in factors.items():
        out[name] = (out[name] * factor).astype(out[name].dtype)
    return out
```

```python
from contextlib import ExitStack

import concourse.bass as bass
import numpy as np
from concourse import mybir

F32 = mybir.dt.float32
F32R = mybir.dt.float32r
ACT = mybir.ActivationFunctionType
ALU = mybir.AluOpType
AX = mybir.AxisListType

P = 128
B, N, D = 2, 2048, 576
H, HD = 16, 36
F = 4 * D
KC = 5
KR = 116
DP = KC * KR
BLK = 512
NIT = N // BLK
TPB = BLK // P
NT = N // P
FC = F // P
PAIRS = H // 2
PW = 3 * 2 * HD
QK = 2 * 2 * HD
PKW = 3 * HD + 2
PKS = 112
VW = 64 + HD + 1
EPS = 1e-12
EXP_ROOM = 60.0
SHIFT_MSA, SCALE_MSA, GATE_MSA, SHIFT_MLP, SCALE_MLP, GATE_MLP = range(6)


def wait(eng, sem, value):
    if isinstance(value, int) and value <= 0:
        return
    eng.wait_ge(sem, value)


def iterate(eng, count, body):
    body(0, True, False)
    with eng.Fori(1, count - 1) as it:
        body(it, False, False)
    body(count - 1, False, True)


def f32(ap):
    return ap.bitcast(F32)


def build(nc, xT, cT, ada, adab, wqkv, qkvb, wp, pb, w1, f1b, w2, f2b, gains, outT):
    qkv_s = nc.dram_tensor("qkv_scratch", (B * NT, P, PAIRS * PW), F32, kind="Internal").ap()
    o_s = nc.dram_tensor("o_scratch", (B * NT, P, D), F32, kind="Internal").ap()
    x1_s = nc.dram_tensor("x1_scratch", (KR, KC, B * N), F32, kind="Internal").ap()
    with ExitStack() as ctx:
        ps = ctx.enter_context(nc.psum_tensor("ps", [P, 8, 512], F32))

        def sb(stack, name, shape, dt=F32):
            return stack.enter_context(nc.sbuf_tensor(name, shape, dt))

        ident = sb(ctx, "ident", [P, P])
        ones = sb(ctx, "ones", [P, P], F32R)
        mod = sb(ctx, "mod", [KR, 6, KC, B])
        gate_b = sb(ctx, "gate_b", [KR, 2, KC, B])
        gain = sb(ctx, "gain", [P, 4])
        qscale = sb(ctx, "qscale", [P, 1])
        bound = sb(ctx, "bound", [P, 1])
        bound_hi = sb(ctx, "bound_hi", [P, 2], F32R)
        pb_t = sb(ctx, "pb_t", [KR, KC])
        f2b_t = sb(ctx, "f2b_t", [KR, KC])
        f1b_t = sb(ctx, "f1b_t", [P, FC])

        qkv_phase(nc, ctx, sb, ps, xT, cT, ada, adab, wqkv, qkvb, pb, f1b, f2b, gains, qkv_s,
                  ident, ones, mod, gate_b, gain, qscale, bound, bound_hi, pb_t, f2b_t, f1b_t)
        w2_hi = sb(ctx, "w2_hi", [P, FC, DP], F32R)
        w2_lo = sb(ctx, "w2_lo", [P, FC, DP], F32R)
        attention_phase(nc, ctx, sb, ps, qkv_s, o_s, w2, ident, bound, bound_hi, w2_hi, w2_lo)
        proj_phase(nc, ctx, sb, ps, o_s, xT, wp, x1_s, ident, mod, gate_b)
        mlp_phase(nc, ctx, sb, ps, x1_s, w1, outT, ones, mod, gate_b, gain, f1b_t, w2_hi, w2_lo)


def qkv_phase(nc, ctx, sb, ps, xT, cT, ada, adab, wqkv, qkvb, pb, f1b, f2b, gains, qkv_s,
              ident, ones, mod, gate_b, gain, qscale, bound, bound_hi, pb_t, f2b_t, f1b_t):
    PIECE = 2 * PW
    NP = PAIRS // 2
    with ExitStack() as st:
        def sem(name):
            return ctx.enter_context(nc.semaphore("a_" + name))

        aw = sb(st, "aw", [KR, 2, KC, DP])
        adab_t = sb(st, "adab_t", [KR, 6 * KC])
        c_t = sb(st, "c_t", [KR, KC, B])
        c_e = sb(st, "c_e", [KR, KC, B])
        c_s = sb(st, "c_s", [KR, KC, B])
        ones32 = sb(st, "ones32", [P, P])
        w_raw = sb(st, "w_raw", [KR, KC, PIECE])
        w_hi = sb(st, "w_hi", [KR, KC, NP * PIECE], F32R)
        w_lo = sb(st, "w_lo", [KR, KC, NP * PIECE], F32R)
        bias = sb(st, "bias", [P, NP * PIECE])
        xb = sb(st, "xb", [KR, 2, KC, BLK])
        tmp = sb(st, "tmp", [KR, KC, BLK])
        rb = sb(st, "rb", [P, BLK])
        h_hi = sb(st, "h_hi", [KR, 2, KC, BLK], F32R)
        h_lo = sb(st, "h_lo", [KR, 2, KC, BLK], F32R)
        stage = sb(st, "stage", [P, 2, PAIRS, PW])
        sqb = sb(st, "sqb", [P, PAIRS, QK])
        ssb = sb(st, "ssb", [P, PAIRS, 4])
        rt = sb(st, "rt", [P, PAIRS, 4])

        c_ld, small_ld, gain_ld, late_ld = sem("c_ld"), sem("small_ld"), sem("gain_ld"), sem("late_ld")
        aw_ld = [sem(f"aw_ld{j}") for j in range(2)]
        w_ld, bias_ld = sem("w_ld"), sem("bias_ld")
        x_ld = [sem(f"x_ld{j}") for j in range(2)]
        setup, ident_done, ones_done = sem("setup"), sem("ident_done"), sem("ones_done")
        c_exp, c_one, c_rec, c_silu = sem("c_exp"), sem("c_one"), sem("c_rec"), sem("c_silu")
        mod_mm, mod_add, mod_one, mod_done = sem("mod_mm"), sem("mod_add"), sem("mod_one"), sem("mod_done")
        gain_a, gain_c, gain_d = sem("gain_a"), sem("gain_c"), sem("gain_d")
        tanh_done = sem("tanh_done")
        whi_done, wlo_done = sem("whi_done"), sem("wlo_done")
        sq_done, sqlo_done, ss_done, nrm_done = sem("sq_done"), sem("sqlo_done"), sem("ss_done"), sem("nrm_done")
        r_max, r_rec, r_done, xr_done = sem("r_max"), sem("r_rec"), sem("r_done"), sem("xr_done")
        aff_done, hhi_done, hlo_done = sem("aff_done"), sem("hhi_done"), sem("hlo_done")
        qkv_mm, evac_done, sqt_done, red_done = sem("qkv_mm"), sem("evac_done"), sem("sqt_done"), sem("red_done")
        rt_done, t_max, t_rec, t_scl, scale_done = sem("rt_done"), sem("t_max"), sem("t_rec"), sem("t_scl"), sem("scale_done")
        st_dma = [sem(f"st_dma{j}") for j in range(2)]

        MODB, RB = ps[0:KR, 5, :], ps[0:KR, 4, :]

        with nc.Block() as block:
            @block.sync
            def _(sp):
                sp.dma_start(c_t[:], cT).then_inc(c_ld, 16)
                sp.dma_start(adab_t[:], adab).then_inc(small_ld, 16)
                for s in range(2):
                    sp.dma_start(aw[:, s], ada[:, s]).then_inc(aw_ld[s], 16)
                    sp.dma_start(xb[:, s], xT[:, :, s * N:s * N + BLK]).then_inc(x_ld[s], 16)
                for j in range(4):
                    sp.dma_start(gain[:, j:j + 1], gains[j].partition_broadcast(P)).then_inc(gain_ld, 16)
                for q in range(NP):
                    if q >= 1:
                        sp.wait_ge(whi_done, q)
                        sp.wait_ge(wlo_done, q)
                    sp.dma_start(w_raw[:], wqkv[:, :, q * PIECE:(q + 1) * PIECE]).then_inc(w_ld, 16)
                sp.dma_start(bias[:], qkvb.partition_broadcast(P)).then_inc(bias_ld, 16)
                sp.dma_start(pb_t[:], pb).then_inc(late_ld, 16)
                sp.dma_start(f2b_t[:], f2b).then_inc(late_ld, 16)
                sp.dma_start(f1b_t[:], f1b).then_inc(late_ld, 16)
                for s in range(2, 4):
                    sp.wait_ge(mod_mm, s - 1)
                    sp.dma_start(aw[:, s % 2], ada[:, s]).then_inc(aw_ld[s % 2], 16)

                def body(it, first, last):
                    for r in range(B):
                        if not last:
                            sp.wait_ge(xr_done, B * it + r + 1)
                            sp.dma_start(xb[:, r], xT[:, :, bass.ds(r * N + BLK * it + BLK, BLK)]).then_inc(x_ld[r], 16)
                        for t in range(TPB):
                            tt = TPB * (B * it + r) + t
                            sp.wait_ge(scale_done, tt + 1)
                            sp.dma_start(qkv_s[bass.ds(r * NT + TPB * it + t, 1)].rearrange("a p c -> (a p) c"),
                                         stage[:, t % 2].rearrange("p a c -> p (a c)")).then_inc(st_dma[t % 2], 16)
                iterate(sp, NIT, body)
                for s in range(4, 6):
                    sp.wait_ge(mod_mm, s - 1)
                    sp.dma_start(aw[:, s % 2], ada[:, s]).then_inc(aw_ld[s % 2], 16)
                for j in range(2):
                    sp.wait_ge(st_dma[j], 16 * B * N // P // 2)

            @block.gpsimd
            def _(pool):
                pool.memset(ident[:], 0.0).then_inc(setup, 1)
                pool.wait_ge(setup, 1)
                pool.affine_select(out=ident[:], in_=ident[:], compare_op=ALU.not_equal, fill=1.0, base=0,
                                   pattern=[[-1, P]], channel_multiplier=1).then_inc(ident_done, 1)

            def prep_act(act, i, r, part):
                if part == 0:
                    act.wait_ge(x_ld[r], 16 * (i // B + 1) if isinstance(i, int) else 8 * (i - r) + 16)
                    wait(act, hlo_done, i)
                    act.activation(tmp[:], xb[:, r], ACT.Square).then_inc(sq_done, 1)
                    wait(act, qkv_mm, 2 * TPB * (i - 1))
                    act.activation(h_hi[:, r], xb[:, r], ACT.Square).then_inc(sq_done, 1)
                elif part == 1:
                    act.wait_ge(ss_done, i + 1)
                    wait(act, xr_done, i)
                    act.activation(rb[0:KR, :], RB, ACT.Sqrt).then_inc(nrm_done, 1)
                else:
                    act.wait_ge(xr_done, i + 1)
                    if part == 3:
                        act.wait_ge(mod_one, 1)
                    for m in range(KC):
                        act.activation(tmp[:, m], tmp[:, m], ACT.Identity, bias=mod[:, SHIFT_MSA, m, r:r + 1],
                                       scale=mod[:, SCALE_MSA, m, r:r + 1]).then_inc(aff_done, 1)
                    act.wait_ge(aff_done, KC * (i + 1))
                    act.activation(h_hi[:, r], tmp[:], ACT.Copy).then_inc(hhi_done, 1)

            def prep_dve(dve, i, r, part):
                if part == 0:
                    dve.wait_ge(sq_done, 2 * (i + 1))
                    dve.tensor_tensor(h_lo[:, r], tmp[:], f32(h_hi[:, r]), ALU.subtract).then_inc(sqlo_done, 1)
                elif part == 1:
                    dve.wait_ge(nrm_done, i + 1)
                    dve.tensor_scalar(rb[0:KR], rb[0:KR], EPS, None, ALU.max).then_inc(r_max, 1)
                    dve.wait_ge(r_max, i + 1)
                    dve.reciprocal(rb[0:KR], rb[0:KR]).then_inc(r_rec, 1)
                    dve.wait_ge(r_rec, i + 1)
                    dve.tensor_scalar(rb[0:KR], rb[0:KR], float(D) ** 0.5, gain[0:KR, 0:1], ALU.mult,
                                      ALU.mult).then_inc(r_done, 1)
                    dve.wait_ge(r_done, i + 1)
                    dve.tensor_tensor(tmp[:], xb[:, r], rb[0:KR, :].unsqueeze(1).to_broadcast([KR, KC, BLK]),
                                      ALU.mult).then_inc(xr_done, 1)
                else:
                    dve.wait_ge(hhi_done, i + 1)
                    dve.tensor_tensor(h_lo[:, r], tmp[:], f32(h_hi[:, r]), ALU.subtract).then_inc(hlo_done, 1)

            @block.scalar
            def _(act):
                act.wait_ge(c_ld, 16)
                act.activation(c_e[:], c_t[:], ACT.Exp, scale=-1.0).then_inc(c_exp, 1)
                prep_act(act, 0, 0, 0)
                for q in range(NP):
                    act.wait_ge(w_ld, 16 * (q + 1))
                    act.activation(w_hi[:, :, q * PIECE:(q + 1) * PIECE], w_raw[:], ACT.Copy).then_inc(whi_done, 1)
                    if q == 0:
                        prep_act(act, 0, 0, 1)
                    if q == 1:
                        prep_act(act, 0, 0, 3)

                def tile(i, t):
                    tt = TPB * i + t
                    act.wait_ge(evac_done, 2 * tt + 2)
                    wait(act, red_done, tt)
                    act.activation(sqb[:], stage[:, t % 2, :, 0:QK], ACT.Square).then_inc(sqt_done, 1)
                    act.wait_ge(red_done, tt + 1)
                    act.activation(rt[:], ssb[:], ACT.Sqrt).then_inc(rt_done, 1)

                def body(it, first, last):
                    for r in range(B):
                        i = B * it + r
                        more = not (last and r == 1)
                        if more:
                            prep_act(act, i + 1, 1 - r, 0)
                        tile(i, 0)
                        if more:
                            prep_act(act, i + 1, 1 - r, 1)
                        tile(i, 1)
                        if more:
                            prep_act(act, i + 1, 1 - r, 2)
                        tile(i, 2)
                        tile(i, 3)
                iterate(act, NIT, body)
                act.wait_ge(mod_add, 2)
                for g in (GATE_MSA, GATE_MLP):
                    act.activation(mod[:, g], mod[:, g], ACT.Tanh).then_inc(tanh_done, 1)

            @block.vector
            def _(dve):
                dve.memset(ones32[:], 1.0).then_inc(ones_done, 1)
                dve.wait_ge(ones_done, 1)
                dve.tensor_copy(ones[:], ones32[:]).then_inc(ones_done, 1)
                dve.wait_ge(c_exp, 1)
                dve.tensor_scalar(c_e[:], c_e[:], 1.0, None, ALU.add).then_inc(c_one, 1)
                dve.wait_ge(c_one, 1)
                dve.reciprocal(c_e[:], c_e[:]).then_inc(c_rec, 1)
                dve.wait_ge(c_rec, 1)
                dve.tensor_tensor(c_s[:], c_t[:], c_e[:], ALU.mult).then_inc(c_silu, 1)
                prep_dve(dve, 0, 0, 0)
                dve.wait_ge(gain_ld, 64)
                dve.tensor_scalar(qscale[:], gain[:, 2:3], gain[:, 3:4], float(HD) ** 0.5, ALU.mult,
                                  ALU.mult).then_inc(gain_a, 1)
                dve.wait_ge(gain_a, 1)
                dve.tensor_scalar(bound[:], qscale[:], -1.0, qscale[:, 0:1], ALU.mult, ALU.min).then_inc(gain_c, 1)
                dve.wait_ge(gain_c, 1)
                dve.tensor_scalar(bound[:], bound[:], EXP_ROOM, 0.0, ALU.add, ALU.min).then_inc(gain_c, 1)
                dve.wait_ge(gain_c, 2)
                dve.tensor_copy(bound_hi[:, 0:1], bound[:]).then_inc(gain_d, 1)
                dve.wait_ge(gain_d, 1)
                dve.tensor_tensor(bound_hi[:, 1:2], bound[:], f32(bound_hi[:, 0:1]), ALU.subtract)

                def modulation(lo, hi, n):
                    dve.wait_ge(small_ld, 16)
                    dve.wait_ge(mod_mm, hi)
                    dve.tensor_tensor(mod[:, lo:hi].rearrange("p s m b -> p (s m) b"),
                                      MODB[:, lo * KC * B:hi * KC * B].rearrange("p (s b) -> p s b", b=B),
                                      adab_t[:, lo * KC:hi * KC].unsqueeze(2).to_broadcast([KR, (hi - lo) * KC, B]),
                                      ALU.add).then_inc(mod_add, 1)
                    dve.wait_ge(mod_add, n)
                    s = SCALE_MSA if n == 1 else SCALE_MLP
                    dve.tensor_scalar(mod[:, s], mod[:, s], 1.0, None, ALU.add).then_inc(mod_one, 1)

                for q in range(NP):
                    dve.wait_ge(whi_done, q + 1)
                    cols = slice(q * PIECE, (q + 1) * PIECE)
                    dve.tensor_tensor(w_lo[:, :, cols], w_raw[:], f32(w_hi[:, :, cols]), ALU.subtract).then_inc(wlo_done, 1)
                    if q == 0:
                        prep_dve(dve, 0, 0, 1)
                        modulation(0, 2, 1)
                    if q == 1:
                        prep_dve(dve, 0, 0, 2)
                dve.wait_ge(bias_ld, 16)

                def scale(tt, t):
                    dve.wait_ge(rt_done, tt + 1)
                    dve.tensor_scalar(rt[:], rt[:], EPS, None, ALU.max).then_inc(t_max, 1)
                    dve.wait_ge(t_max, tt + 1)
                    dve.reciprocal(rt[:], rt[:]).then_inc(t_rec, 1)
                    dve.wait_ge(t_rec, tt + 1)
                    dve.tensor_scalar(rt[:, :, 0:2], rt[:, :, 0:2], qscale[:, 0:1], None, ALU.mult).then_inc(t_scl, 1)
                    dve.wait_ge(t_scl, tt + 1)
                    qk = stage[:, t % 2, :, 0:QK].rearrange("p a (h d) -> p a h d", d=HD)
                    dve.tensor_tensor(qk, qk, rt[:].unsqueeze(3).to_broadcast([P, PAIRS, 4, HD]),
                                      ALU.mult).then_inc(scale_done, 1)

                def tile(it, i, r, t, first):
                    tt = TPB * i + t
                    for h in range(2):
                        dve.wait_ge(qkv_mm, 2 * tt + h + 1)
                        if not (first and r == 0 and t < 2):
                            dve.wait_ge(st_dma[t % 2], 16 * (2 * i + t // 2))
                        dve.tensor_tensor(stage[:, t % 2, 4 * h:4 * h + 4].rearrange("p (n a) c -> p n (a c)", a=2),
                                          ps[:, 2 * h:2 * h + 2, 0:PIECE],
                                          bias[:, 2 * h * PIECE:(2 * h + 2) * PIECE].rearrange("p (n c) -> p n c", n=2),
                                          ALU.add).then_inc(evac_done, 1)
                    if not (first and r == 0 and t == 0):
                        scale(tt - 1, t + 1)
                    dve.wait_ge(sqt_done, tt + 1)
                    dve.tensor_reduce(ssb[:], sqb[:].rearrange("p a (h d) -> p a h d", d=HD), AX.X, ALU.add).then_inc(red_done, 1)

                def body(it, first, last):
                    for r in range(B):
                        i = B * it + r
                        more = not (last and r == 1)
                        if more:
                            prep_dve(dve, i + 1, 1 - r, 0)
                        for t in range(TPB):
                            tile(it, i, r, t, first)
                            if more and t in (1, 2):
                                prep_dve(dve, i + 1, 1 - r, t)
                iterate(dve, NIT, body)
                scale(B * N // P - 1, 1)
                modulation(2, 6, 2)
                dve.wait_ge(late_ld, 48)
                dve.wait_ge(tanh_done, 2)
                for j, (g, b_t) in enumerate(((GATE_MSA, pb_t), (GATE_MLP, f2b_t))):
                    dve.tensor_tensor(gate_b[:, j], mod[:, g], b_t[:].unsqueeze(2).to_broadcast([KR, KC, B]),
                                      ALU.mult).then_inc(mod_done, 1)

            @block.tensor
            def _(pe):
                def modulate(s):
                    pe.wait_ge(aw_ld[s % 2], 16 * (s // 2 + 1))
                    for m in range(KC):
                        col = (s * KC + m) * B
                        for k in range(KC):
                            mm = pe.matmul(MODB[:, col:col + B], aw[:, s % 2, k, m * KR:(m + 1) * KR], c_s[:, k],
                                           start=k == 0, stop=k == KC - 1)
                    mm.then_inc(mod_mm, 1)

                def sum_squares(i, r):
                    pe.wait_ge(sqlo_done, i + 1)
                    wait(pe, nrm_done, i)
                    for k in range(KC):
                        for n, part in enumerate((h_hi, h_lo)):
                            mm = pe.matmul(RB, ones[0:KR, 0:KR], part[:, r, k], start=k == 0 and n == 0,
                                           stop=k == KC - 1 and n == 1)
                    mm.then_inc(ss_done, 1)

                pe.wait_ge(c_silu, 1)
                modulate(0)
                pe.wait_ge(ones_done, 2)
                sum_squares(0, 0)
                modulate(1)

                def tile(i, r, t, first):
                    tt = TPB * i + t
                    cols = slice(t * P, (t + 1) * P)
                    for h in range(2):
                        if first and r == 0 and t == 0:
                            pe.wait_ge(wlo_done, 2 * h + 2)
                        if not (first and r == 0 and t == 0):
                            pe.wait_ge(evac_done, 2 * tt + h - 1)
                        for k in range(KC):
                            for n, (a, w) in enumerate(((h_hi, w_hi), (h_hi, w_lo), (h_lo, w_hi))):
                                for q in (2 * h, 2 * h + 1):
                                    mm = pe.matmul(ps[:, q, 0:PIECE], a[:, r, k, cols], w[:, k, q * PIECE:(q + 1) * PIECE],
                                                   start=k == 0 and n == 0, stop=k == KC - 1 and n == 2)
                        mm.then_inc(qkv_mm, 1)

                def body(it, first, last):
                    for r in range(B):
                        i = B * it + r
                        pe.wait_ge(hlo_done, i + 1)
                        for t in range(TPB):
                            tile(i, r, t, first)
                            if t == 0 and not (last and r == 1):
                                sum_squares(i + 1, 1 - r)
                iterate(pe, NIT, body)
                for s in range(2, 6):
                    modulate(s)


def attention_phase(nc, ctx, sb, ps, qkv_s, o_s, w2, ident, bound, bound_hi, w2_hi, w2_lo):
    C = NIT
    with ExitStack() as st:
        def sem(name):
            return ctx.enter_context(nc.semaphore("b_" + name))

        pair = sb(st, "pair", [P, B, NT, PW])
        kT = sb(st, "kT", [PKW, B, 2, N], F32R)
        qT = sb(st, "qT", [PKW, 2, 2, BLK], F32R)
        vp = sb(st, "vp", [P, B, NT, VW])
        prob = sb(st, "prob", [P, 4, 2 * BLK])
        qpack = sb(st, "qpack", [P, TPB, 2, PKS], F32R)
        kpack = sb(st, "kpack", [P, TPB, 2, PKS], F32R)
        osb = sb(st, "osb", [VW, BLK])
        rl = sb(st, "rl", [P, TPB, 2])
        ofin = sb(st, "ofin", [P, 2, TPB, 2, HD])
        w2_raw = sb(st, "w2_raw", [P, 2, DP])
        cst = sb(st, "cst", [P, TPB, 2, 2])

        pair_ld = [sem(f"pair_ld{j}") for j in range(B)]
        w2_ld = [sem(f"w2_ld{j}") for j in range(2)]
        vzero, cst_done, rows_done = sem("vzero"), sem("cst_done"), sem("rows_done")
        q_hi, q_pack, k_hi, k_pack = sem("q_hi"), sem("q_pack"), sem("k_hi"), sem("k_pack")
        tp, qT_done, kT_done, v_done = sem("tp"), sem("qT_done"), sem("kT_done"), sem("v_done")
        s_mm, exp_done, pv_mm = sem("s_mm"), sem("exp_done"), sem("pv_mm")
        o_evac, ot_mm, rl_done, o_fin = sem("o_evac"), sem("ot_mm"), sem("rl_done"), sem("o_fin")
        o_dma = [sem(f"o_dma{j}") for j in range(2)]
        w2hi_done, w2lo_done = sem("w2hi_done"), sem("w2lo_done")

        TP, OT = ps[0:PKW, 6, :], ps[:, 7, :].rearrange("p (t c) -> p t c", t=TPB)
        NU = B * PAIRS * C

        with nc.Block() as block:
            @block.sync
            def _(sp):
                def load(it, r):
                    sp.dma_start(pair[:, r], qkv_s[r * NT:(r + 1) * NT, :, bass.ds(PW * it, PW)]
                                 .rearrange("t p c -> p t c")).then_inc(pair_ld[r], 16)

                def store(it, r, c):
                    u = C * (B * it + r) + c
                    sp.wait_ge(o_fin, u + 1)
                    sp.dma_start(o_s[r * NT + TPB * c:r * NT + TPB * (c + 1), :, bass.ds(2 * HD * it, 2 * HD)]
                                 .rearrange("t p c -> p t c"),
                                 ofin[:, c % 2].rearrange("p t h d -> p t (h d)")).then_inc(o_dma[c % 2], 16)

                load(0, 0)
                load(0, 1)

                def body(it, first, last):
                    for r in range(B):
                        g = B * it + r
                        for c in range(C):
                            if c == 2 and not last:
                                sp.wait_ge(q_pack, 4 * g + 4)
                                sp.wait_ge(v_done, 4 * g + 4)
                                load(it + 1, r)
                            store(it, r, c)
                iterate(sp, PAIRS, body)
                for j in range(2):
                    sp.wait_ge(o_dma[j], 16 * NU // 2)

            @block.gpsimd
            def _(pool):
                pool.memset(vp[:], 0.0).then_inc(vzero, 1)
                pool.wait_ge(vzero, 1)
                for r in range(B):
                    for h in range(2):
                        pool.memset(vp[:, r, :, 64 * h + HD:64 * h + HD + 1], 1.0).then_inc(vzero, 1)
                pool.wait_ge(vzero, 5)
                for k in range(2):
                    pool.dma_start(w2_raw[:, k], w2[:, k]).then_inc(w2_ld[k], 16)

                def take_v(it, r, first):
                    g = B * it + r
                    pool.wait_ge(pair_ld[r], 16 * (it + 1))
                    if not first:
                        pool.wait_ge(pv_mm, NT * C * (g - 1))
                    for h in range(2):
                        c = QK + h * HD
                        for half in (slice(0, NT // 2), slice(NT // 2, NT)):
                            pool.tensor_scalar(vp[:, r, half, 64 * h:64 * h + HD], pair[:, r, half, c:c + HD], 1.0, None,
                                               ALU.mult).then_inc(v_done, 1)

                take_v(0, 0, True)
                take_v(0, 1, True)
                for k in range(FC):
                    pool.wait_ge(w2_ld[k % 2], 16 * (k // 2 + 1))
                    pool.tensor_scalar(w2_hi[:, k], w2_raw[:, k % 2], 1.0, None, ALU.mult).then_inc(w2hi_done, 1)
                    pool.wait_ge(w2hi_done, k + 1)
                    pool.tensor_tensor(w2_lo[:, k], w2_raw[:, k % 2], f32(w2_hi[:, k]), ALU.subtract).then_inc(w2lo_done, 1)
                    if k + 2 < FC:
                        pool.wait_ge(w2lo_done, k + 1)
                        pool.dma_start(w2_raw[:, k % 2], w2[:, k + 2]).then_inc(w2_ld[k % 2], 16)
                for it in range(1, PAIRS):
                    for r in range(B):
                        take_v(it, r, False)

            @block.scalar
            def _(act):
                def body(it, first, last):
                    for r in range(B):
                        for c in range(C):
                            for kt in range(NT):
                                s = NT * (C * (B * it + r) + c) + kt
                                act.wait_ge(s_mm, s + 1)
                                if not (first and r == 0 and c == 0 and kt < 4):
                                    act.wait_ge(pv_mm, s - 3)
                                j = kt % 2
                                act.activation(prob[:, kt % 4], ps[:, 2 * j:2 * j + 2, :].rearrange("p a b -> p (a b)"),
                                               ACT.Exp).then_inc(exp_done, 1)
                iterate(act, PAIRS, body)

            @block.vector
            def _(dve):
                dve.memset(cst[:], 1.0).then_inc(cst_done, 1)
                dve.wait_ge(cst_done, 1)
                dve.tensor_copy(kpack[:, :, :, 3 * HD:PKW], cst[:]).then_inc(rows_done, 1)
                for j in range(2):
                    dve.tensor_scalar(qpack[:, :, :, 3 * HD + j:3 * HD + j + 1], cst[:, :, :, 0:1],
                                      f32(bound_hi[:, j:j + 1]), None, ALU.mult).then_inc(rows_done, 1)

                def pack_q(it, r, c):
                    n = C * (B * it + r) + c
                    dve.wait_ge(pair_ld[r], 16 * (it + 1))
                    src = pair[:, r, TPB * c:TPB * (c + 1), 0:2 * HD].rearrange("p t (h d) -> p t h d", d=HD)
                    dve.tensor_copy(qpack[:, :, :, 0:HD], src).then_inc(q_hi, 1)
                    dve.tensor_copy(qpack[:, :, :, HD:2 * HD], src)
                    dve.wait_ge(q_hi, n + 1)
                    dve.tensor_tensor(qpack[:, :, :, 2 * HD:3 * HD], src, f32(qpack[:, :, :, 0:HD]), ALU.subtract).then_inc(q_pack, 1)

                def pack_k(it, r, c):
                    n = C * (B * it + r) + c
                    dve.wait_ge(pair_ld[r], 16 * (it + 1))
                    src = pair[:, r, TPB * c:TPB * (c + 1), 2 * HD:4 * HD].rearrange("p t (h d) -> p t h d", d=HD)
                    dve.tensor_copy(kpack[:, :, :, 0:HD], src).then_inc(k_hi, 1)
                    dve.tensor_copy(kpack[:, :, :, 2 * HD:3 * HD], src)
                    dve.wait_ge(k_hi, n + 1)
                    dve.tensor_tensor(kpack[:, :, :, HD:2 * HD], src, f32(kpack[:, :, :, 0:HD]), ALU.subtract).then_inc(k_pack, 1)

                def q_out(slot, h, group):
                    dve.wait_ge(tp, group + 1)
                    dve.tensor_copy(qT[:, slot, h], TP).then_inc(qT_done, 1)

                def k_out(r, h, c, group):
                    dve.wait_ge(tp, group + 1)
                    dve.tensor_copy(kT[:, r, h, BLK * c:BLK * (c + 1)], TP).then_inc(kT_done, 1)

                def take_o(u, slot, early):
                    dve.wait_ge(pv_mm, NT * (u + 1))
                    if not early:
                        dve.wait_ge(ot_mm, u)
                    dve.tensor_copy(osb[:], ps[0:VW, 4 + slot, :]).then_inc(o_evac, 1)

                def finish_o(u, slot, early):
                    dve.wait_ge(ot_mm, u + 1)
                    dve.reciprocal(rl[:], OT[:, :, HD:HD + 65:64]).then_inc(rl_done, 1)
                    dve.wait_ge(rl_done, u + 1)
                    if not early:
                        dve.wait_ge(o_dma[slot], 8 * (u - slot))
                    for h in range(2):
                        mul = dve.tensor_tensor(ofin[:, slot, :, h], OT[:, :, 64 * h:64 * h + HD],
                                                rl[:, :, h:h + 1].to_broadcast([P, TPB, HD]), ALU.mult)
                    mul.then_inc(o_fin, 1)

                for c in range(C):
                    if c:
                        dve.wait_ge(tp, 2 * c)
                    pack_k(0, 0, c)
                    for h in range(2):
                        k_out(0, h, c, 2 * c + h)
                pack_q(0, 0, 0)
                for h in range(2):
                    q_out(0, h, 2 * C + h)
                pack_k(0, 1, 0)
                pack_q(0, 0, 1)

                def body(it, first, last):
                    for r in range(B):
                        final = last and r == 1
                        for c in range(C):
                            u = C * (B * it + r) + c
                            group = 2 * C + 2 + 4 * u if not final else 2 * C + 2 + 4 * (NU - C) + 2 * c
                            start = first and r == 0 and c == 0
                            if not start:
                                take_o(u - 1, (c + 1) % 2, first and r == 0 and c == 1)
                            more_q = not (final and c == C - 1)
                            if more_q:
                                q_out((c + 1) % 2, 0, group)
                            if not start:
                                finish_o(u - 1, (c + 1) % 2, first and r == 0 and c <= 2)
                            if more_q:
                                q_out((c + 1) % 2, 1, group + 1)
                            if not (final and c >= C - 2):
                                if c < C - 2:
                                    pack_q(it, r, c + 2)
                                else:
                                    pack_q(it + r, 1 - r, c + 2 - C)
                            if not final:
                                for h in range(2):
                                    k_out(1 - r, h, c, group + 2 + h)
                                if c < C - 1:
                                    pack_k(it + r, 1 - r, c + 1)
                                elif not (last and r == 0):
                                    pack_k(it + 1, r, 0)
                iterate(dve, PAIRS, body)
                take_o(NU - 1, 1, False)
                finish_o(NU - 1, 1, False)

            @block.tensor
            def _(pe):
                def turn(pack, h, t, mark):
                    mm = pe.transpose(TP[:, t * P:(t + 1) * P], f32(pack[:, t, h, 0:PKW]), ident[:])
                    if mark:
                        mm.then_inc(tp, 1)

                def scores(r, c, kt, u):
                    if kt == 0:
                        pe.wait_ge(qT_done, 2 * (u + 1))
                    if c == 0 and kt % TPB == 0:
                        pe.wait_ge(kT_done, 2 * u + 2 * (kt // TPB + 1))
                    j = kt % 2
                    for h in range(2):
                        mm = pe.matmul(ps[:, 2 * j + h, :], kT[:, r, h, kt * P:(kt + 1) * P], qT[:, c % 2, h],
                                       start=True, stop=True)
                    mm.then_inc(s_mm, 1)

                for c in range(C):
                    pe.wait_ge(k_pack, c + 1)
                    if c == 0:
                        pe.wait_ge(rows_done, 3)
                    for h in range(2):
                        wait(pe, kT_done, 2 * c + h)
                        for t in range(TPB):
                            turn(kpack, h, t, t == TPB - 1)
                pe.wait_ge(q_pack, 1)
                for h in range(2):
                    if h == 0:
                        pe.wait_ge(kT_done, 2 * C)
                    else:
                        pe.wait_ge(qT_done, 1)
                    for t in range(TPB):
                        turn(qpack, h, t, t == TPB - 1)
                for kt in range(2):
                    scores(0, 0, kt, 0)

                def turn_o(u):
                    pe.wait_ge(o_evac, u + 1)
                    if not (isinstance(u, int) and u == 0):
                        pe.wait_ge(o_fin, u)
                    for t in range(TPB):
                        mm = pe.transpose(OT[:, t, 0:VW], osb[:, t * P:(t + 1) * P], ident[0:VW, 0:VW])
                    mm.then_inc(ot_mm, 1)

                def body(it, first, last):
                    for r in range(B):
                        final = last and r == 1
                        for c in range(C):
                            u = C * (B * it + r) + c
                            for kt0 in range(0, NT, 2):
                                steps = (kt0, kt0 + 1)
                                pe.wait_ge(exp_done, NT * u + kt0 + 2)
                                for kt in steps:
                                    if kt + 2 < NT:
                                        scores(r, c, kt + 2, u)
                                    elif c + 1 < C:
                                        scores(r, c + 1, kt + 2 - NT, u + 1)
                                    elif not final:
                                        scores(1 - r, 0, kt + 2 - NT, u + 1)
                                for kt in steps:
                                    group, t = divmod(kt, TPB)
                                    if group < 2:
                                        if not (final and c == C - 1):
                                            if t == 0:
                                                if group == 0:
                                                    pe.wait_ge(q_pack, u + 2)
                                                    pe.wait_ge(kT_done, 2 * C + 2 * u if not final else 2 * C + 2 * (NU - C))
                                                pe.wait_ge(qT_done, 2 + 2 * u + group)
                                            turn(qpack, group, t, t == TPB - 1)
                                    elif not final:
                                        if t == 0:
                                            if group == 2:
                                                pe.wait_ge(k_pack, u + C + 1)
                                                pe.wait_ge(qT_done, 4 + 2 * u)
                                            else:
                                                pe.wait_ge(kT_done, 2 * C + 2 * u + 1)
                                        turn(kpack, group - 2, t, t == TPB - 1)
                                if kt0 == 2 and not (first and r == 0 and c == 0):
                                    turn_o(u - 1)
                                if kt0 == 0:
                                    if c == 0:
                                        pe.wait_ge(v_done, 4 * (B * it + r) + 4)
                                    if not (first and r == 0 and c < 2):
                                        pe.wait_ge(o_evac, u - 1)
                                O = ps[:, 4 + c % 2, :]
                                for kt in steps:
                                    j = kt % 4
                                    pe.matmul(O[0:64], vp[:, r, kt, 0:64], prob[:, j, 0:BLK], start=kt == 0, stop=kt == NT - 1)
                                    pe.matmul(O[64:VW], vp[:, r, kt, 64:VW], prob[:, j, BLK:2 * BLK], start=kt == 0,
                                              stop=kt == NT - 1).then_inc(pv_mm, 1)
                iterate(pe, PAIRS, body)
                turn_o(NU - 1)


def proj_phase(nc, ctx, sb, ps, o_s, xT, wp, x1_s, ident, mod, gate_b):
    with ExitStack() as st:
        def sem(name):
            return ctx.enter_context(nc.semaphore("c_" + name))

        ob = sb(st, "ob", [P, B, TPB, DP])
        xb = sb(st, "cxb", [KR, B, KC, BLK])
        wp_raw = sb(st, "wp_raw", [KR, KC, DP])
        wp_hi = sb(st, "wp_hi", [KR, KC, DP], F32R)
        wp_lo = sb(st, "wp_lo", [KR, KC, DP], F32R)
        o_hi = sb(st, "o_hi", [KR, B, KC, BLK], F32R)
        o_lo = sb(st, "o_lo", [KR, B, KC, BLK], F32R)
        gated = sb(st, "gated", [KR, 2, BLK])
        wp_ld = sem("wp_ld")
        o_ld = [sem(f"o_ld{j}") for j in range(B)]
        x_ld = [sem(f"x_ld{j}") for j in range(B)]
        pad_done, whi_done, wlo_done = sem("pad_done"), sem("whi_done"), sem("wlo_done")
        tp, hi_done, lo_done = sem("tp"), sem("hi_done"), sem("lo_done")
        proj_mm, gate_done, x1_done = sem("proj_mm"), sem("gate_done"), sem("x1_done")
        x1_dma = [sem(f"x1_dma{j}") for j in range(B)]
        with nc.Block() as block:
            @block.sync
            def _(sp):
                sp.dma_start(wp_raw[:], wp).then_inc(wp_ld, 16)
                sp.wait_ge(pad_done, 1)

                def load_o(it, r):
                    sp.dma_start(ob[:, r, :, 0:D], o_s[bass.ds(r * NT + TPB * it, TPB)]
                                 .rearrange("t p c -> p t c")).then_inc(o_ld[r], 16)

                def load_x(it, r):
                    sp.dma_start(xb[:, r], xT[:, :, bass.ds(r * N + BLK * it, BLK)]).then_inc(x_ld[r], 16)

                for r in range(B):
                    load_o(0, r)
                    load_x(0, r)

                def body(it, first, last):
                    for r in range(B):
                        i = B * it + r
                        if not last:
                            sp.wait_ge(tp, KC * (i + 1))
                            load_o(it + 1, r)
                        sp.wait_ge(x1_done, KC * (i + 1))
                        sp.dma_start(x1_s[:, :, bass.ds(r * N + BLK * it, BLK)], xb[:, r]).then_inc(x1_dma[r], 16)
                        if not last:
                            sp.wait_ge(x1_dma[r], 16 * (it + 1))
                            load_x(it + 1, r)
                iterate(sp, NIT, body)
                for r in range(B):
                    sp.wait_ge(x1_dma[r], 16 * NIT)

            @block.scalar
            def _(act):
                act.wait_ge(wp_ld, 16)
                act.activation(wp_hi[:], wp_raw[:], ACT.Copy).then_inc(whi_done, 1)

                def turn_hi(i, r, k):
                    act.wait_ge(tp, KC * i + k + 1)
                    act.activation(o_hi[:, r, k], ps[0:KR, (r + k) % 2, :], ACT.Copy).then_inc(hi_done, 1)

                for k in range(KC):
                    turn_hi(0, 0, k)

                def body(it, first, last):
                    for r in range(B):
                        i = B * it + r
                        for m in range(KC):
                            j = (KC * r + m) % 2
                            act.wait_ge(proj_mm, KC * i + m + 1)
                            if not (first and r == 0 and m < 2):
                                act.wait_ge(x1_done, KC * i + m - 1)
                            act.activation(gated[:, j], ps[0:KR, 2 + j, :], ACT.Identity, bias=gate_b[:, 0, m, r:r + 1],
                                           scale=mod[:, GATE_MSA, m, r:r + 1]).then_inc(gate_done, 1)
                            if not (last and r == 1):
                                turn_hi(i + 1, 1 - r, m)
                iterate(act, NIT, body)

            @block.vector
            def _(dve):
                dve.memset(ob[:, :, :, D:DP], 0.0).then_inc(pad_done, 1)
                dve.wait_ge(whi_done, 1)
                dve.tensor_tensor(wp_lo[:], wp_raw[:], f32(wp_hi[:]), ALU.subtract).then_inc(wlo_done, 1)

                def turn_lo(i, r, k):
                    dve.wait_ge(hi_done, KC * i + k + 1)
                    dve.tensor_tensor(o_lo[:, r, k], ps[0:KR, (r + k) % 2, :], f32(o_hi[:, r, k]),
                                      ALU.subtract).then_inc(lo_done, 1)

                for k in range(KC):
                    turn_lo(0, 0, k)

                def body(it, first, last):
                    for r in range(B):
                        i = B * it + r
                        for m in range(KC):
                            j = (KC * r + m) % 2
                            dve.wait_ge(gate_done, KC * i + m + 1)
                            if m == 0:
                                dve.wait_ge(x_ld[r], 16 * (it + 1))
                            dve.tensor_tensor(xb[:, r, m], xb[:, r, m], gated[:, j], ALU.add).then_inc(x1_done, 1)
                            if not (last and r == 1):
                                turn_lo(i + 1, 1 - r, m)
                iterate(dve, NIT, body)

            @block.tensor
            def _(pe):
                def turn(it, i, r, k, early):
                    if k == 0:
                        pe.wait_ge(o_ld[r], 16 * (it + 1))
                    if not (early and k < 2):
                        pe.wait_ge(lo_done, KC * i + k - 1)
                    for t in range(TPB):
                        mm = pe.transpose(ps[0:KR, (r + k) % 2, t * P:(t + 1) * P],
                                          ob[:, r, t, k * KR:(k + 1) * KR], ident[:])
                    mm.then_inc(tp, 1)

                for k in range(KC):
                    turn(0, 0, 0, k, True)
                pe.wait_ge(wlo_done, 1)

                def body(it, first, last):
                    for r in range(B):
                        i = B * it + r
                        pe.wait_ge(lo_done, KC * (i + 1))
                        for m in range(KC):
                            j = (KC * r + m) % 2
                            if not (first and r == 0 and m < 2):
                                pe.wait_ge(gate_done, KC * i + m - 1)
                            for k in range(KC):
                                for n, (w, a) in enumerate(((wp_hi, o_hi), (wp_lo, o_hi), (wp_hi, o_lo))):
                                    mm = pe.matmul(ps[0:KR, 2 + j, :], w[:, k, m * KR:(m + 1) * KR], a[:, r, k],
                                                   start=k == 0 and n == 0, stop=k == KC - 1 and n == 2)
                            mm.then_inc(proj_mm, 1)
                            if not (last and r == 1):
                                turn(it + r, i + 1, 1 - r, m, False)
                iterate(pe, NIT, body)


def mlp_phase(nc, ctx, sb, ps, x1_s, w1, outT, ones, mod, gate_b, gain, f1b_t, w2_hi, w2_lo):
    K_SQ, K_SS, K_REC, K_H = 3, 8, 9, 12
    with ExitStack() as st:
        def sem(name):
            return ctx.enter_context(nc.semaphore("d_" + name))

        x1 = sb(st, "x1", [KR, B, KC, BLK])
        tmp = sb(st, "dtmp", [KR, KC, BLK])
        rb = sb(st, "drb", [KR, BLK])
        h_hi = sb(st, "dh_hi", [KR, B, KC, BLK], F32R)
        h_lo = sb(st, "dh_lo", [KR, B, KC, BLK], F32R)
        w1_raw = sb(st, "w1_raw", [KR, 2, KC, P])
        w1_hi = sb(st, "w1_hi", [KR, 2, KC, P], F32R)
        w1_lo = sb(st, "w1_lo", [KR, 2, KC, P], F32R)
        act32 = sb(st, "act32", [P, 2, BLK])
        a_hi = sb(st, "a_hi", [P, 2, BLK], F32R)
        a_lo = sb(st, "a_lo", [P, 2, BLK], F32R)
        gated = sb(st, "dgated", [KR, 2, BLK])

        x_ld = [sem(f"x_ld{j}") for j in range(B)]
        w1_ld = [sem(f"w1_ld{j}") for j in range(2)]
        w1hi_done, w1lo_done = sem("w1hi_done"), sem("w1lo_done")
        sq_done, sqhi_done, sqlo_done, ss_done = sem("sq_done"), sem("sqhi_done"), sem("sqlo_done"), sem("ss_done")
        nrm_done, r_max, r_rec, r_done, xr_done = sem("nrm_done"), sem("r_max"), sem("r_rec"), sem("r_done"), sem("xr_done")
        aff_done, hhi_done, hlo_done = sem("aff_done"), sem("hhi_done"), sem("hlo_done")
        fc1_mm, gelu_done, alo_done, fc2_mm = sem("fc1_mm"), sem("gelu_done"), sem("alo_done"), sem("fc2_mm")
        gate_done, out_done = sem("gate_done"), sem("out_done")
        out_dma = [sem(f"out_dma{j}") for j in range(B)]
        NB = B * NIT
        RB = ps[0:KR, 7, :]

        with nc.Block() as block:
            @block.sync
            def _(sp):
                def load_w1(k, slot, count):
                    wait(sp, w1lo_done, count - 1)
                    wait(sp, w1hi_done, count - 1)
                    sp.dma_start(w1_raw[:, slot], w1[k]).then_inc(w1_ld[slot], 16)

                sp.dma_start(x1[:, 0], x1_s[:, :, 0:BLK]).then_inc(x_ld[0], 16)
                load_w1(0, 0, 0)
                load_w1(1, 1, 0)
                sp.dma_start(x1[:, 1], x1_s[:, :, N:N + BLK]).then_inc(x_ld[1], 16)

                def body(it, first, last):
                    for r in range(B):
                        i = B * it + r
                        for k in range(FC):
                            if not (last and r == 1 and k + 2 >= FC):
                                load_w1((k + 2) % FC, k % 2, FC * i + k + 2)
                            if k == 1 and not (first and r == 0) and not (last and r == 1):
                                sp.wait_ge(out_dma[1 - r], 16 * (it + r))
                                sp.dma_start(x1[:, 1 - r], x1_s[:, :, bass.ds((1 - r) * N + BLK * (it + r), BLK)]
                                             ).then_inc(x_ld[1 - r], 16)
                iterate(sp, NIT, body)
                for r in range(B):
                    sp.wait_ge(out_dma[r], 16 * NIT)

            def act_square(act, it, i, r, m):
                if m == 0:
                    act.wait_ge(x_ld[r], 16 * (it + 1))
                    wait(act, hlo_done, KC * i)
                    wait(act, fc1_mm, FC * (i - 1))
                act.activation(tmp[:, m], x1[:, r, m], ACT.Square).then_inc(sq_done, 1)
                act.activation(h_hi[:, r, m], x1[:, r, m], ACT.Square).then_inc(sqhi_done, 1)

            def act_norm(act, i):
                act.wait_ge(ss_done, i + 1)
                wait(act, xr_done, KC * i)
                act.activation(rb[:], RB, ACT.Sqrt).then_inc(nrm_done, 1)

            def act_h(act, i, r, m):
                act.wait_ge(xr_done, KC * i + m + 1)
                act.activation(tmp[:, m], tmp[:, m], ACT.Identity, bias=mod[:, SHIFT_MLP, m, r:r + 1],
                               scale=mod[:, SCALE_MLP, m, r:r + 1]).then_inc(aff_done, 1)
                act.wait_ge(aff_done, KC * i + m + 1)
                act.activation(h_hi[:, r, m], tmp[:, m], ACT.Copy).then_inc(hhi_done, 1)

            @block.scalar
            def _(act):
                def split_w1(slot, count, it, fours, k):
                    act.wait_ge(w1_ld[slot], 16 * fours)
                    wait(act, fc1_mm, count - 1)
                    act.activation(w1_hi[:, slot], w1_raw[:, slot], ACT.Copy).then_inc(w1hi_done, 1)

                for m in range(KC):
                    act_square(act, 0, 0, 0, m)
                split_w1(0, 0, 0, 1, 0)
                split_w1(1, 1, 0, 1, 1)
                act_norm(act, 0)
                for m in range(KC):
                    act_h(act, 0, 0, m)

                def gelu(i, k, early):
                    j, slot = FC * i + k, k % 2
                    act.wait_ge(fc1_mm, j + 1)
                    if not early:
                        act.wait_ge(alo_done, j - 1)
                    act.activation(act32[:, slot], ps[:, 5 + slot, :], ACT.Gelu_apprx_tanh, bias=f1b_t[:, k:k + 1])
                    if not early:
                        act.wait_ge(fc2_mm, j - 1)
                    act.activation(a_hi[:, slot], ps[:, 5 + slot, :], ACT.Gelu_apprx_tanh,
                                   bias=f1b_t[:, k:k + 1]).then_inc(gelu_done, 1)

                def gates(i, r, early):
                    act.wait_ge(fc2_mm, FC * (i + 1))
                    for m in range(KC):
                        n = KC * i + m
                        if not (early and m < 2):
                            act.wait_ge(out_done, n - 1)
                        act.activation(gated[:, (r + m) % 2], ps[0:KR, m, :], ACT.Identity,
                                       bias=gate_b[:, 1, m, r:r + 1], scale=mod[:, GATE_MLP, m, r:r + 1]).then_inc(gate_done, 1)

                def body(it, first, last):
                    for r in range(B):
                        i = B * it + r
                        more = not (last and r == 1)
                        for k in range(FC):
                            gelu(i, k, first and r == 0 and k < 2)
                            if k == 0 and not (first and r == 0):
                                gates(i - 1, 1 - r, first and r == 1)
                            if k == 1 and not (first and r == 0):
                                act.wait_ge(out_done, KC * i)
                                act.dma_start(outT[:, :, bass.ds((1 - r) * N + BLK * (it + r - 1), BLK)],
                                              x1[:, 1 - r]).then_inc(out_dma[1 - r], 16)
                            if more or k + 2 < FC:
                                j = FC * i + k + 2
                                split_w1(k % 2, j, it, FC // 2 * i + k // 2 + 2, k)
                            if more:
                                if K_SQ <= k < K_SQ + KC:
                                    act_square(act, it + r, i + 1, 1 - r, k - K_SQ)
                                if k == K_SS:
                                    act_norm(act, i + 1)
                                if K_H <= k < K_H + KC:
                                    act_h(act, i + 1, 1 - r, k - K_H)
                iterate(act, NIT, body)
                gates(NB - 1, 1, False)
                act.wait_ge(out_done, KC * NB)
                act.dma_start(outT[:, :, 2 * N - BLK:2 * N], x1[:, 1]).then_inc(out_dma[1], 16)

            @block.vector
            def _(dve):
                def square_lo(i, r, m):
                    dve.wait_ge(sqhi_done, KC * i + m + 1)
                    dve.tensor_tensor(h_lo[:, r, m], tmp[:, m], f32(h_hi[:, r, m]), ALU.subtract).then_inc(sqlo_done, 1)

                def reciprocal(i, part):
                    half = slice(part * BLK // 2, (part + 1) * BLK // 2)
                    if part == 0:
                        dve.wait_ge(nrm_done, i + 1)
                        dve.tensor_scalar(rb[:], rb[:], EPS, None, ALU.max).then_inc(r_max, 1)
                        dve.wait_ge(r_max, i + 1)
                    dve.reciprocal(rb[:, half], rb[:, half]).then_inc(r_rec, 1)
                    if part == 1:
                        dve.wait_ge(r_rec, 2 * i + 2)
                        dve.tensor_scalar(rb[:], rb[:], float(D) ** 0.5, gain[0:KR, 1:2], ALU.mult, ALU.mult).then_inc(r_done, 1)

                def normed(i, r, m):
                    if m == 0:
                        dve.wait_ge(r_done, i + 1)
                    dve.tensor_tensor(tmp[:, m], x1[:, r, m], rb[:], ALU.mult).then_inc(xr_done, 1)

                def h_low(i, r, m):
                    dve.wait_ge(hhi_done, KC * i + m + 1)
                    dve.tensor_tensor(h_lo[:, r, m], tmp[:, m], f32(h_hi[:, r, m]), ALU.subtract).then_inc(hlo_done, 1)

                def split_w1(slot, count):
                    dve.wait_ge(w1hi_done, count + 1)
                    dve.tensor_tensor(w1_lo[:, slot], w1_raw[:, slot], f32(w1_hi[:, slot]), ALU.subtract).then_inc(w1lo_done, 1)

                for m in range(KC):
                    square_lo(0, 0, m)
                split_w1(0, 0)
                split_w1(1, 1)
                reciprocal(0, 0)
                reciprocal(0, 1)
                for m in range(KC):
                    normed(0, 0, m)
                for m in range(KC):
                    h_low(0, 0, m)

                def add_x1(i, r):
                    for m in range(KC):
                        dve.wait_ge(gate_done, KC * i + m + 1)
                        dve.tensor_tensor(x1[:, r, m], x1[:, r, m], gated[:, (r + m) % 2], ALU.add).then_inc(out_done, 1)

                def body(it, first, last):
                    for r in range(B):
                        i = B * it + r
                        more = not (last and r == 1)
                        for k in range(FC):
                            j, slot = FC * i + k, k % 2
                            dve.wait_ge(gelu_done, j + 1)
                            dve.tensor_tensor(a_lo[:, slot], act32[:, slot], f32(a_hi[:, slot]), ALU.subtract).then_inc(alo_done, 1)
                            if k == 0 and not (first and r == 0):
                                add_x1(i - 1, 1 - r)
                            if more or k + 2 < FC:
                                split_w1(slot, j + 2)
                            if more:
                                if K_SQ <= k < K_SQ + KC:
                                    square_lo(i + 1, 1 - r, k - K_SQ)
                                if k in (K_REC, K_REC + 1):
                                    reciprocal(i + 1, k - K_REC)
                                if K_REC + 2 <= k < K_REC + 2 + KC:
                                    normed(i + 1, 1 - r, k - K_REC - 2)
                                if K_H <= k < K_H + KC:
                                    h_low(i + 1, 1 - r, k - K_H)
                iterate(dve, NIT, body)
                add_x1(NB - 1, 1)

            @block.tensor
            def _(pe):
                def sum_squares(i, r):
                    pe.wait_ge(sqlo_done, KC * (i + 1))
                    wait(pe, nrm_done, i)
                    for k in range(KC):
                        for n, part in enumerate((h_hi, h_lo)):
                            mm = pe.matmul(RB, ones[0:KR, 0:KR], part[:, r, k], start=k == 0 and n == 0,
                                           stop=k == KC - 1 and n == 1)
                    mm.then_inc(ss_done, 1)

                def fc1(i, r, k, early):
                    j, slot = FC * i + k, k % 2
                    if k == 0:
                        pe.wait_ge(hlo_done, KC * (i + 1))
                    pe.wait_ge(w1lo_done, j + 1)
                    if not early:
                        pe.wait_ge(gelu_done, j - 1)
                    for c in range(KC):
                        for n, (w, a) in enumerate(((w1_hi, h_hi), (w1_lo, h_hi), (w1_hi, h_lo))):
                            mm = pe.matmul(ps[:, 5 + slot, :], w[:, slot, c], a[:, r, c], start=c == 0 and n == 0,
                                           stop=c == KC - 1 and n == 2)
                    mm.then_inc(fc1_mm, 1)

                sum_squares(0, 0)
                fc1(0, 0, 0, True)

                def body(it, first, last):
                    for r in range(B):
                        i = B * it + r
                        more = not (last and r == 1)
                        for k in range(FC):
                            j, slot = FC * i + k, k % 2
                            if k + 1 < FC:
                                fc1(i, r, k + 1, first and r == 0 and k == 0)
                            elif more:
                                fc1(i + 1, 1 - r, 0, False)
                            if k == K_SS and more:
                                sum_squares(i + 1, 1 - r)
                            pe.wait_ge(alo_done, j + 1)
                            for m in range(KC):
                                if k == 0 and not (first and r == 0):
                                    pe.wait_ge(gate_done, KC * (i - 1) + m + 1)
                                for n, (w, a) in enumerate(((w2_hi, a_hi), (w2_lo, a_hi), (w2_hi, a_lo))):
                                    mm = pe.matmul(ps[0:KR, m, :], w[:, k, m * KR:(m + 1) * KR], a[:, slot],
                                                   start=k == 0 and n == 0, stop=k == FC - 1 and n == 2)
                            mm.then_inc(fc2_mm, 1)
                iterate(pe, NIT, body)


def rows(a, cols):
    out = np.zeros((DP, cols), np.float32)
    out[:D] = a
    return np.ascontiguousarray(out.reshape(KC, KR, cols).transpose(1, 0, 2))


def columns(a):
    out = np.zeros(a.shape[:-1] + (DP,), np.float32)
    out[..., :D] = a
    return out


def by_pair(a):
    return a.reshape((3, PAIRS, 2 * HD) + a.shape[1:]).swapaxes(0, 1).reshape(a.shape)


def kernel(x, cond_1152, L0_cond_g1, L0_cond_g2, L0_cond_qkv_w, L0_cond_qkv_b, L0_cond_qg, L0_cond_kg, L0_cond_proj_w,
           L0_cond_proj_b, L0_cond_fc1_w, L0_cond_fc1_b, L0_cond_fc2_w, L0_cond_fc2_b, L0_cond_ada_w, L0_cond_ada_b):
    import concourse.bacc as bacc
    from concourse.bass_utils import run_bass_kernel_spmd

    n = np.asarray
    ada = columns(n(L0_cond_ada_w).reshape(6, D, D).transpose(0, 2, 1))
    arrays = {
        "xT": rows(n(x).reshape(B * N, D).T, B * N),
        "cT": rows(n(cond_1152).T, B),
        "ada": np.ascontiguousarray(np.stack([rows(a, DP) for a in ada], axis=1)),
        "adab": np.ascontiguousarray(columns(n(L0_cond_ada_b).reshape(6, D)).reshape(6 * KC, KR).T),
        "wqkv": rows(by_pair(n(L0_cond_qkv_w)).T, 3 * D),
        "qkvb": np.ascontiguousarray(by_pair(n(L0_cond_qkv_b))),
        "wp": rows(columns(n(L0_cond_proj_w).T), DP),
        "pb": np.ascontiguousarray(columns(n(L0_cond_proj_b)).reshape(KC, KR).T),
        "w1": np.ascontiguousarray(rows(n(L0_cond_fc1_w).T, F).reshape(KR, KC, FC, P).transpose(2, 0, 1, 3)),
        "f1b": np.ascontiguousarray(n(L0_cond_fc1_b).reshape(FC, P).T),
        "w2": np.ascontiguousarray(columns(n(L0_cond_fc2_w).T).reshape(FC, P, DP).transpose(1, 0, 2)),
        "f2b": np.ascontiguousarray(columns(n(L0_cond_fc2_b)).reshape(KC, KR).T),
        "g1": n(L0_cond_g1), "g2": n(L0_cond_g2), "qg": n(L0_cond_qg), "kg": n(L0_cond_kg),
    }
    nc = bacc.Bacc("TRN2", target_bir_lowering=False, num_devices=1)
    ap = {k: nc.dram_tensor(k, a.shape, F32, kind="ExternalInput").ap() for k, a in arrays.items()}
    outT = nc.dram_tensor("outT", (KR, KC, B * N), F32, kind="ExternalOutput").ap()
    build(nc, ap["xT"], ap["cT"], ap["ada"], ap["adab"], ap["wqkv"], ap["qkvb"], ap["wp"], ap["pb"], ap["w1"], ap["f1b"],
          ap["w2"], ap["f2b"], [ap["g1"], ap["g2"], ap["qg"], ap["kg"]], outT)
    out = run_bass_kernel_spmd(nc, [arrays], core_ids=[0]).results[0]["outT"]
    return np.ascontiguousarray(out.transpose(1, 0, 2).reshape(DP, B * N)[:D].T).reshape(B, N, D)
```

```python
from contextlib import ExitStack

import concourse.bass as bass
import numpy as np
from concourse import mybir

F32 = mybir.dt.float32
F32R = mybir.dt.float32r
ACT = mybir.ActivationFunctionType
ALU = mybir.AluOpType
AX = mybir.AxisListType

P = 128
B, N, D = 2, 2048, 576
H, HD = 16, 36
F = 4 * D
KF = D // P
TL = D - KF * P
KC = KF + 1
DP = KC * P
BLK = 512
NIT = N // BLK
TPB = BLK // P
NT = N // P
FC = F // P
PAIRS = H // 2
PW = 3 * 2 * HD
QK = 2 * 2 * HD
SW = PW + 4
PKW = 3 * HD + 2
PKS = 112
VW = 64 + HD + 1
EPS = 1e-12
MAX_FREE = 60.0
SHIFT_MSA, SCALE_MSA, GATE_MSA, SHIFT_MLP, SCALE_MLP, GATE_MLP = range(6)


def wait(eng, sem, value):
    if isinstance(value, int) and value <= 0:
        return
    eng.wait_ge(sem, value)


def iterate(eng, count, body):
    body(0, True, False)
    with eng.Fori(1, count - 1) as it:
        body(it, False, False)
    body(count - 1, False, True)


def passes(k, w_hi, w_lo, a_hi, a_lo):
    return ((w_hi, a_hi), (w_lo, a_hi), (w_hi, a_lo)) if k < KF else ((w_hi, a_hi), (w_lo, a_hi))


def low(eng, hi, lo, full, k):
    if k < KF:
        return eng.tensor_tensor(lo[:, k], full, f32(hi[:, k]), ALU.subtract)
    return eng.tensor_tensor(hi[TL:P, k], full[TL:P], f32(hi[TL:P, k]), ALU.subtract)


def lows(eng, hi, lo, full):
    eng.tensor_tensor(lo, full[:, 0:KF], f32(hi[:, 0:KF]), ALU.subtract)
    return low(eng, hi, lo, full[:, KF], KF)


def f32(ap):
    return ap.bitcast(F32)


def build(nc, xT, cT, ada, adab, wqkv, qkvb, wp, pb, w1, f1b, w2, f2b, gains, outT):
    qkv_s = nc.dram_tensor("qkv_scratch", (B * NT, P, PAIRS * SW), F32, kind="Internal").ap()
    o_s = nc.dram_tensor("o_scratch", (B * NT, P, D), F32, kind="Internal").ap()
    x1_s = nc.dram_tensor("x1_scratch", (P, KC, B * N), F32, kind="Internal").ap()
    with ExitStack() as ctx:
        ps = ctx.enter_context(nc.psum_tensor("ps", [P, 8, 512], F32))

        def sb(stack, name, shape, dt=F32):
            return stack.enter_context(nc.sbuf_tensor(name, shape, dt))

        ident = sb(ctx, "ident", [P, P])
        ones = sb(ctx, "ones", [P, P], F32R)
        mod = sb(ctx, "mod", [P, 6, KC, B])
        gate_b = sb(ctx, "gate_b", [P, 2, KC, B])
        gain = sb(ctx, "gain", [P, 4])
        qscale = sb(ctx, "qscale", [P, 1])
        bound = sb(ctx, "bound", [P, 1])
        unbounded = sb(ctx, "unbounded", [P, 1], mybir.dt.int32)
        pb_t = sb(ctx, "pb_t", [P, KC])
        f2b_t = sb(ctx, "f2b_t", [P, KC])
        f1b_t = sb(ctx, "f1b_t", [P, FC])

        qkv_phase(nc, ctx, sb, ps, xT, cT, ada, adab, wqkv, qkvb, pb, f1b, f2b, gains, qkv_s,
                  ident, ones, mod, gate_b, gain, qscale, bound, unbounded, pb_t, f2b_t, f1b_t)
        w2_hi = sb(ctx, "w2_hi", [P, FC, DP], F32R)
        w2_lo = sb(ctx, "w2_lo", [P, FC, KF * P], F32R)
        attention_phase(nc, ctx, sb, ps, qkv_s, o_s, w2, ident, unbounded, w2_hi, w2_lo)
        proj_phase(nc, ctx, sb, ps, o_s, xT, wp, x1_s, ident, mod, gate_b)
        mlp_phase(nc, ctx, sb, ps, x1_s, w1, outT, ones, mod, gate_b, gain, f1b_t, w2_hi, w2_lo)


def qkv_phase(nc, ctx, sb, ps, xT, cT, ada, adab, wqkv, qkvb, pb, f1b, f2b, gains, qkv_s,
              ident, ones, mod, gate_b, gain, qscale, bound, unbounded, pb_t, f2b_t, f1b_t):
    PIECE = 2 * PW
    NP = PAIRS // 2
    with ExitStack() as st:
        def sem(name):
            return ctx.enter_context(nc.semaphore("a_" + name))

        aw = sb(st, "aw", [P, 2, KC, DP])
        adab_t = sb(st, "adab_t", [P, 6 * KC])
        c_t = sb(st, "c_t", [P, KC, B])
        c_e = sb(st, "c_e", [P, KC, B])
        c_s = sb(st, "c_s", [P, KC, B])
        ones32 = sb(st, "ones32", [P, P])
        w_raw = sb(st, "w_raw", [P, KC, PIECE])
        w_hi = sb(st, "w_hi", [P, KC, NP * PIECE], F32R)
        w_lo = sb(st, "w_lo", [P, KC, NP * PIECE], F32R)
        bias = sb(st, "bias", [P, NP * PIECE])
        xb = sb(st, "xb", [P, 2, KC, BLK])
        tmp = sb(st, "tmp", [P, KC, BLK])
        rb = sb(st, "rb", [P, BLK])
        h_hi = sb(st, "h_hi", [P, 2, KC, BLK], F32R)
        h_lo = sb(st, "h_lo", [P, 2, KF, BLK], F32R)
        stage = sb(st, "stage", [P, 2, PAIRS, SW])
        sqb = sb(st, "sqb", [P, PAIRS, QK])
        ssb = sb(st, "ssb", [P, PAIRS, 4])
        rt = sb(st, "rt", [P, PAIRS, 4])

        c_ld, small_ld, gain_ld, late_ld = sem("c_ld"), sem("small_ld"), sem("gain_ld"), sem("late_ld")
        aw_ld = [sem(f"aw_ld{j}") for j in range(2)]
        w_ld, bias_ld = sem("w_ld"), sem("bias_ld")
        x_ld = [sem(f"x_ld{j}") for j in range(2)]
        setup, ident_done, ones_done = sem("setup"), sem("ident_done"), sem("ones_done")
        c_exp, c_one, c_rec, c_silu = sem("c_exp"), sem("c_one"), sem("c_rec"), sem("c_silu")
        mod_mm, mod_add, mod_one, mod_done = sem("mod_mm"), sem("mod_add"), sem("mod_one"), sem("mod_done")
        gain_a, gain_c, gain_d = sem("gain_a"), sem("gain_c"), sem("gain_d")
        tanh_done = sem("tanh_done")
        whi_done, wlo_done = sem("whi_done"), sem("wlo_done")
        sq_done, sqlo_done, ss_done, nrm_done = sem("sq_done"), sem("sqlo_done"), sem("ss_done"), sem("nrm_done")
        r_max, r_rec, r_done, xr_done = sem("r_max"), sem("r_rec"), sem("r_done"), sem("xr_done")
        aff_done, hhi_done, hlo_done = sem("aff_done"), sem("hhi_done"), sem("hlo_done")
        qkv_mm, evac_done, sqt_done, red_done = sem("qkv_mm"), sem("evac_done"), sem("sqt_done"), sem("red_done")
        rt_done, t_max, t_rec, t_scl, scale_done = sem("rt_done"), sem("t_max"), sem("t_rec"), sem("t_scl"), sem("scale_done")
        st_dma = [sem(f"st_dma{j}") for j in range(2)]

        MODB, RB = ps[:, 5, :], ps[:, 4, :]

        with nc.Block() as block:
            @block.sync
            def _(sp):
                sp.dma_start(c_t[:], cT).then_inc(c_ld, 16)
                sp.dma_start(adab_t[:], adab).then_inc(small_ld, 16)
                for s in range(2):
                    sp.dma_start(aw[:, s], ada[:, s]).then_inc(aw_ld[s], 16)
                    sp.dma_start(xb[:, s], xT[:, :, s * N:s * N + BLK]).then_inc(x_ld[s], 16)
                for j in range(4):
                    sp.dma_start(gain[:, j:j + 1], gains[j].partition_broadcast(P)).then_inc(gain_ld, 16)
                for q in range(NP):
                    if q >= 1:
                        sp.wait_ge(whi_done, q)
                        sp.wait_ge(wlo_done, q)
                    sp.dma_start(w_raw[:], wqkv[:, :, q * PIECE:(q + 1) * PIECE]).then_inc(w_ld, 16)
                sp.dma_start(bias[:], qkvb.partition_broadcast(P)).then_inc(bias_ld, 16)
                sp.dma_start(pb_t[:], pb).then_inc(late_ld, 16)
                sp.dma_start(f2b_t[:], f2b).then_inc(late_ld, 16)
                sp.dma_start(f1b_t[:], f1b).then_inc(late_ld, 16)
                for s in range(2, 4):
                    sp.wait_ge(mod_mm, s - 1)
                    sp.dma_start(aw[:, s % 2], ada[:, s]).then_inc(aw_ld[s % 2], 16)

                def body(it, first, last):
                    for r in range(B):
                        if not last:
                            sp.wait_ge(xr_done, B * it + r + 1)
                            sp.dma_start(xb[:, r], xT[:, :, bass.ds(r * N + BLK * it + BLK, BLK)]).then_inc(x_ld[r], 16)
                        for t in range(TPB):
                            tt = TPB * (B * it + r) + t
                            sp.wait_ge(scale_done, tt + 1)
                            sp.dma_start(qkv_s[bass.ds(r * NT + TPB * it + t, 1)].rearrange("a p c -> (a p) c"),
                                         stage[:, t % 2].rearrange("p a c -> p (a c)")).then_inc(st_dma[t % 2], 16)
                iterate(sp, NIT, body)
                for s in range(4, 6):
                    sp.wait_ge(mod_mm, s - 1)
                    sp.dma_start(aw[:, s % 2], ada[:, s]).then_inc(aw_ld[s % 2], 16)
                for j in range(2):
                    sp.wait_ge(st_dma[j], 16 * B * N // P // 2)

            @block.gpsimd
            def _(pool):
                pool.memset(ident[:], 0.0).then_inc(setup, 1)
                pool.wait_ge(setup, 1)
                pool.affine_select(out=ident[:], in_=ident[:], compare_op=ALU.not_equal, fill=1.0, base=0,
                                   pattern=[[-1, P]], channel_multiplier=1).then_inc(ident_done, 1)

            def prep_act(act, i, r, part):
                if part == 0:
                    act.wait_ge(x_ld[r], 16 * (i // B + 1) if isinstance(i, int) else 8 * (i - r) + 16)
                    wait(act, hlo_done, i)
                    act.activation(tmp[:], xb[:, r], ACT.Square).then_inc(sq_done, 1)
                    wait(act, qkv_mm, 2 * TPB * (i - 1))
                    act.activation(h_hi[:, r], xb[:, r], ACT.Square).then_inc(sq_done, 1)
                elif part == 1:
                    act.wait_ge(ss_done, i + 1)
                    wait(act, xr_done, i)
                    act.activation(rb[:], RB, ACT.Sqrt).then_inc(nrm_done, 1)
                else:
                    act.wait_ge(xr_done, i + 1)
                    if part == 3:
                        act.wait_ge(mod_one, 1)
                    for m in range(KC):
                        act.activation(tmp[:, m], tmp[:, m], ACT.Identity, bias=mod[:, SHIFT_MSA, m, r:r + 1],
                                       scale=mod[:, SCALE_MSA, m, r:r + 1]).then_inc(aff_done, 1)
                    act.wait_ge(aff_done, KC * (i + 1))
                    act.activation(h_hi[:, r], tmp[:], ACT.Copy).then_inc(hhi_done, 1)

            def prep_dve(dve, i, r, part):
                if part == 0:
                    dve.wait_ge(sq_done, 2 * (i + 1))
                    lows(dve, h_hi[:, r], h_lo[:, r], tmp).then_inc(sqlo_done, 1)
                elif part == 1:
                    dve.wait_ge(nrm_done, i + 1)
                    dve.tensor_scalar(rb[:], rb[:], EPS, None, ALU.max).then_inc(r_max, 1)
                    dve.wait_ge(r_max, i + 1)
                    dve.reciprocal(rb[:], rb[:]).then_inc(r_rec, 1)
                    dve.wait_ge(r_rec, i + 1)
                    dve.tensor_scalar(rb[:], rb[:], float(D) ** 0.5, gain[:, 0:1], ALU.mult,
                                      ALU.mult).then_inc(r_done, 1)
                    dve.wait_ge(r_done, i + 1)
                    dve.tensor_tensor(tmp[:], xb[:, r], rb[:].unsqueeze(1).to_broadcast([P, KC, BLK]),
                                      ALU.mult).then_inc(xr_done, 1)
                else:
                    dve.wait_ge(hhi_done, i + 1)
                    lows(dve, h_hi[:, r], h_lo[:, r], tmp).then_inc(hlo_done, 1)

            @block.scalar
            def _(act):
                act.wait_ge(c_ld, 16)
                act.activation(c_e[:], c_t[:], ACT.Exp, scale=-1.0).then_inc(c_exp, 1)
                prep_act(act, 0, 0, 0)
                for q in range(NP):
                    act.wait_ge(w_ld, 16 * (q + 1))
                    act.activation(w_hi[:, :, q * PIECE:(q + 1) * PIECE], w_raw[:], ACT.Copy).then_inc(whi_done, 1)
                    if q == 0:
                        prep_act(act, 0, 0, 1)
                    if q == 1:
                        prep_act(act, 0, 0, 3)

                def tile(i, t):
                    tt = TPB * i + t
                    act.wait_ge(evac_done, 2 * tt + 2)
                    wait(act, red_done, tt)
                    act.activation(sqb[:], stage[:, t % 2, :, 0:QK], ACT.Square).then_inc(sqt_done, 1)
                    act.wait_ge(red_done, tt + 1)
                    act.activation(rt[:], ssb[:], ACT.Sqrt).then_inc(rt_done, 1)

                def body(it, first, last):
                    for r in range(B):
                        i = B * it + r
                        more = not (last and r == 1)
                        if more:
                            prep_act(act, i + 1, 1 - r, 0)
                        tile(i, 0)
                        if more:
                            prep_act(act, i + 1, 1 - r, 1)
                        tile(i, 1)
                        if more:
                            prep_act(act, i + 1, 1 - r, 2)
                        tile(i, 2)
                        tile(i, 3)
                iterate(act, NIT, body)
                act.wait_ge(mod_add, 2)
                for g in (GATE_MSA, GATE_MLP):
                    act.activation(mod[:, g], mod[:, g], ACT.Tanh).then_inc(tanh_done, 1)

            @block.vector
            def _(dve):
                dve.memset(ones32[:], 1.0).then_inc(ones_done, 1)
                dve.wait_ge(ones_done, 1)
                dve.tensor_copy(ones[:], ones32[:]).then_inc(ones_done, 1)
                dve.wait_ge(c_exp, 1)
                dve.tensor_scalar(c_e[:], c_e[:], 1.0, None, ALU.add).then_inc(c_one, 1)
                dve.wait_ge(c_one, 1)
                dve.reciprocal(c_e[:], c_e[:]).then_inc(c_rec, 1)
                dve.wait_ge(c_rec, 1)
                dve.tensor_tensor(c_s[:], c_t[:], c_e[:], ALU.mult).then_inc(c_silu, 1)
                prep_dve(dve, 0, 0, 0)
                dve.wait_ge(gain_ld, 64)
                dve.tensor_scalar(qscale[:], gain[:, 2:3], gain[:, 3:4], float(HD) ** 0.5, ALU.mult,
                                  ALU.mult).then_inc(gain_a, 1)
                dve.wait_ge(gain_a, 1)
                dve.tensor_scalar(bound[:], qscale[:], -1.0, qscale[:, 0:1], ALU.mult, ALU.max).then_inc(gain_c, 1)
                dve.wait_ge(gain_c, 1)
                dve.tensor_scalar(bound[:], bound[:], MAX_FREE, None, ALU.is_gt).then_inc(gain_d, 1)
                dve.wait_ge(gain_d, 1)
                dve.tensor_copy(unbounded[:], bound[:])
                dve.memset(stage[:, :, :, PW:SW], 0.0)

                def modulation(lo, hi, n):
                    dve.wait_ge(small_ld, 16)
                    dve.wait_ge(mod_mm, hi)
                    dve.tensor_tensor(mod[:, lo:hi].rearrange("p s m b -> p (s m) b"),
                                      MODB[:, lo * KC * B:hi * KC * B].rearrange("p (s b) -> p s b", b=B),
                                      adab_t[:, lo * KC:hi * KC].unsqueeze(2).to_broadcast([P, (hi - lo) * KC, B]),
                                      ALU.add).then_inc(mod_add, 1)
                    dve.wait_ge(mod_add, n)
                    s = SCALE_MSA if n == 1 else SCALE_MLP
                    dve.tensor_scalar(mod[:, s], mod[:, s], 1.0, None, ALU.add).then_inc(mod_one, 1)

                for q in range(NP):
                    dve.wait_ge(whi_done, q + 1)
                    cols = slice(q * PIECE, (q + 1) * PIECE)
                    dve.tensor_tensor(w_lo[:, :, cols], w_raw[:], f32(w_hi[:, :, cols]), ALU.subtract).then_inc(wlo_done, 1)
                    if q == 0:
                        prep_dve(dve, 0, 0, 1)
                        modulation(0, 2, 1)
                    if q == 1:
                        prep_dve(dve, 0, 0, 2)
                dve.wait_ge(bias_ld, 16)

                def scale(tt, t):
                    dve.wait_ge(rt_done, tt + 1)
                    dve.tensor_scalar(rt[:], rt[:], EPS, None, ALU.max).then_inc(t_max, 1)
                    dve.wait_ge(t_max, tt + 1)
                    dve.reciprocal(rt[:], rt[:]).then_inc(t_rec, 1)
                    dve.wait_ge(t_rec, tt + 1)
                    dve.tensor_scalar(rt[:, :, 0:2], rt[:, :, 0:2], qscale[:, 0:1], None, ALU.mult).then_inc(t_scl, 1)
                    dve.wait_ge(t_scl, tt + 1)
                    qk = stage[:, t % 2, :, 0:QK].rearrange("p a (h d) -> p a h d", d=HD)
                    dve.tensor_tensor(qk, qk, rt[:].unsqueeze(3).to_broadcast([P, PAIRS, 4, HD]),
                                      ALU.mult).then_inc(scale_done, 1)

                def tile(it, i, r, t, first):
                    tt = TPB * i + t
                    for h in range(2):
                        dve.wait_ge(qkv_mm, 2 * tt + h + 1)
                        if not (first and r == 0 and t < 2):
                            dve.wait_ge(st_dma[t % 2], 16 * (2 * i + t // 2))
                        dve.tensor_tensor(stage[:, t % 2, 4 * h:4 * h + 4, 0:PW].rearrange("p (n a) c -> p n a c", a=2),
                                          ps[:, 2 * h:2 * h + 2, 0:PIECE].rearrange("p n (a c) -> p n a c", a=2),
                                          bias[:, 2 * h * PIECE:(2 * h + 2) * PIECE].rearrange("p (n a c) -> p n a c",
                                                                                               n=2, a=2),
                                          ALU.add).then_inc(evac_done, 1)
                    if not (first and r == 0 and t == 0):
                        scale(tt - 1, t + 1)
                    dve.wait_ge(sqt_done, tt + 1)
                    dve.tensor_reduce(ssb[:], sqb[:].rearrange("p a (h d) -> p a h d", d=HD), AX.X, ALU.add).then_inc(red_done, 1)

                def body(it, first, last):
                    for r in range(B):
                        i = B * it + r
                        more = not (last and r == 1)
                        if more:
                            prep_dve(dve, i + 1, 1 - r, 0)
                        for t in range(TPB):
                            tile(it, i, r, t, first)
                            if more and t in (1, 2):
                                prep_dve(dve, i + 1, 1 - r, t)
                iterate(dve, NIT, body)
                scale(B * N // P - 1, 1)
                modulation(2, 6, 2)
                dve.wait_ge(late_ld, 48)
                dve.wait_ge(tanh_done, 2)
                for j, (g, b_t) in enumerate(((GATE_MSA, pb_t), (GATE_MLP, f2b_t))):
                    dve.tensor_tensor(gate_b[:, j], mod[:, g], b_t[:].unsqueeze(2).to_broadcast([P, KC, B]),
                                      ALU.mult).then_inc(mod_done, 1)

            @block.tensor
            def _(pe):
                def modulate(s):
                    pe.wait_ge(aw_ld[s % 2], 16 * (s // 2 + 1))
                    for m in range(KC):
                        col = (s * KC + m) * B
                        for k in range(KC):
                            rows = slice(0, P if k < KF else TL)
                            mm = pe.matmul(MODB[:, col:col + B], aw[rows, s % 2, k, m * P:(m + 1) * P], c_s[rows, k],
                                           start=k == 0, stop=k == KC - 1)
                    mm.then_inc(mod_mm, 1)

                def sum_squares(i, r):
                    pe.wait_ge(sqlo_done, i + 1)
                    wait(pe, nrm_done, i)
                    for k in range(KC):
                        for part in (h_hi, h_lo)[:2 if k < KF else 1]:
                            mm = pe.matmul(RB, ones[:], part[:, r, k], start=k == 0 and part is h_hi, stop=k == KF)
                    mm.then_inc(ss_done, 1)

                pe.wait_ge(c_silu, 1)
                modulate(0)
                pe.wait_ge(ones_done, 2)
                sum_squares(0, 0)
                modulate(1)

                def tile(i, r, t, first):
                    tt = TPB * i + t
                    cols = slice(t * P, (t + 1) * P)
                    for h in range(2):
                        if first and r == 0 and t == 0:
                            pe.wait_ge(wlo_done, 2 * h + 2)
                        if not (first and r == 0 and t == 0):
                            pe.wait_ge(evac_done, 2 * tt + h - 1)
                        for k in range(KC):
                            for n, (w, a) in enumerate(passes(k, w_hi, w_lo, h_hi, h_lo)):
                                for q in (2 * h, 2 * h + 1):
                                    mm = pe.matmul(ps[:, q, 0:PIECE], a[:, r, k, cols], w[:, k, q * PIECE:(q + 1) * PIECE],
                                                   start=k == 0 and n == 0, stop=k == KF and n == 1)
                        mm.then_inc(qkv_mm, 1)

                def body(it, first, last):
                    for r in range(B):
                        i = B * it + r
                        pe.wait_ge(hlo_done, i + 1)
                        for t in range(TPB):
                            tile(i, r, t, first)
                            if t == 0 and not (last and r == 1):
                                sum_squares(i + 1, 1 - r)
                iterate(pe, NIT, body)
                for s in range(2, 6):
                    modulate(s)


def attention_phase(nc, ctx, sb, ps, qkv_s, o_s, w2, ident, unbounded, w2_hi, w2_lo):
    C = NIT
    with ExitStack() as st:
        def sem(name):
            return ctx.enter_context(nc.semaphore("b_" + name))

        pair = sb(st, "pair", [P, B, NT, SW])
        kT = sb(st, "kT", [PKW, B, 2, N], F32R)
        qT = sb(st, "qT", [PKW, 2, 2, BLK], F32R)
        vp = sb(st, "vp", [P, B, NT, VW])
        prob = sb(st, "prob", [P, 4, 2 * BLK])
        qpack = sb(st, "qpack", [P, TPB, 2, PKS], F32R)
        kpack = sb(st, "kpack", [P, TPB, 2, PKS], F32R)
        osb = sb(st, "osb", [VW, BLK])
        rl = sb(st, "rl", [P, TPB, 2])
        ofin = sb(st, "ofin", [P, 2, TPB, 2, HD])
        w2_raw = sb(st, "w2_raw", [P, 2, D])
        cst = sb(st, "cst", [P, TPB, 2, 2])
        mx_hi = sb(st, "mx_hi", [P, 1], F32R)
        mx = sb(st, "mx", [P, 4])

        pair_ld = [sem(f"pair_ld{j}") for j in range(B)]
        w2_ld = [sem(f"w2_ld{j}") for j in range(2)]
        vzero, cst_done, rows_done = sem("vzero"), sem("cst_done"), sem("rows_done")
        q_hi, q_pack, k_hi, k_pack = sem("q_hi"), sem("q_pack"), sem("k_hi"), sem("k_pack")
        tp, qT_done, kT_done, v_done = sem("tp"), sem("qT_done"), sem("kT_done"), sem("v_done")
        s_mm, exp_done, pv_mm = sem("s_mm"), sem("exp_done"), sem("pv_mm")
        o_evac, ot_mm, rl_done, o_fin = sem("o_evac"), sem("ot_mm"), sem("rl_done"), sem("o_fin")
        o_dma = [sem(f"o_dma{j}") for j in range(2)]
        w2hi_done, w2lo_done = sem("w2hi_done"), sem("w2lo_done")

        TP, OT = ps[0:PKW, 6, :], ps[:, 7, :].rearrange("p (t c) -> p t c", t=TPB)
        NU = B * PAIRS * C

        m_ld, m_st = sem("m_ld"), sem("m_st")
        m_kt, m_kx, m_q, m_qt, m_qx = sem("m_kt"), sem("m_kx"), sem("m_q"), sem("m_qt"), sem("m_qx")
        m_s, m_max, m_neg, m_hi, m_lo, m_out = sem("m_s"), sem("m_max"), sem("m_neg"), sem("m_hi"), sem("m_lo"), sem("m_out")
        kx = prob[0:HD, 0:2].rearrange("p a b -> p (a b)")
        qt_tile = prob[:, 2, 0:2 * HD]
        qx = osb[0:HD, 0:P]
        SC = ps[:, 0:4, :].rearrange("p a b -> p (a b)")
        QX = ps[0:2 * HD, 6, 0:P]

        def row_maxima_sync(sp):
            def load(it, r):
                sp.dma_start(pair[:, 0], qkv_s[r * NT:(r + 1) * NT, :, bass.ds(SW * it, SW)]
                             .rearrange("t p c -> p t c")).then_inc(m_ld, 16)

            def store(it, r):
                n = it + PAIRS * r
                sp.wait_ge(m_out, 2 * NT * n + 2 * NT)
                sp.dma_start(qkv_s[r * NT:(r + 1) * NT, :, bass.ds(SW * it + PW, SW - PW)]
                             .rearrange("t p c -> p t c"), pair[:, 0, :, PW:SW]).then_inc(m_st, 16)
                sp.wait_ge(m_st, 16 * n + 16)
            for r in range(B):
                load(0, r)
                with sp.Fori(0, PAIRS - 1) as it:
                    store(it, r)
                    load(it + 1, r)
                store(PAIRS - 1, r)

        def row_maxima_tensor(pe):
            for r in range(B):
                with pe.Fori(0, PAIRS) as it:
                    n = it + PAIRS * r
                    pe.wait_ge(m_ld, 16 * n + 16)
                    for h in range(2):
                        pe.wait_ge(m_max, NT * (2 * n + h) + 1)
                        for t in range(NT):
                            mm = pe.transpose(SC[0:2 * HD, t * P:(t + 1) * P], pair[:, 0, t, (2 + h) * HD:(4 + h) * HD], ident[:])
                        mm.then_inc(m_kt, 1)
                        with pe.Fori(0, NT) as qt:
                            j = NT * (2 * n + h) + qt
                            pe.wait_ge(m_q, j + 1)
                            pe.transpose(QX, qt_tile, ident[:]).then_inc(m_qt, 1)
                            pe.wait_ge(m_qx, j + 1)
                            pe.wait_ge(m_kx, 2 * n + h + 1)
                            pe.wait_ge(m_max, j + 1)
                            for b in range(4):
                                mm = pe.matmul(ps[:, b, :], qx, kx[:, b * BLK:(b + 1) * BLK], start=True, stop=True)
                            mm.then_inc(m_s, 1)

        def row_maxima_vector(dve):
            dve.memset(mx[:], 0.0).then_inc(m_max, 1)
            for r in range(B):
                with dve.Fori(0, PAIRS) as it:
                    n = it + PAIRS * r
                    for h in range(2):
                        dve.wait_ge(m_kt, 2 * n + h + 1)
                        dve.tensor_copy(kx, SC[0:HD]).then_inc(m_kx, 1)
                        with dve.Fori(0, NT) as qt:
                            j = NT * (2 * n + h) + qt
                            dve.tensor_copy(qt_tile, pair[:, 0, bass.ds(qt, 1), h * HD:(2 + h) * HD]
                                            .rearrange("p a c -> p (a c)")).then_inc(m_q, 1)
                            dve.wait_ge(m_qt, j + 1)
                            dve.tensor_copy(qx, QX[0:HD]).then_inc(m_qx, 1)
                            dve.wait_ge(m_s, j + 1)
                            dve.tensor_reduce(mx[:, 0:1], SC, AX.X, ALU.max).then_inc(m_max, 1)
                            dve.wait_ge(m_max, j + 2)
                            dve.tensor_scalar(mx[:, 1:2], mx[:, 0:1], -1.0, None, ALU.mult).then_inc(m_neg, 1)
                            dve.wait_ge(m_neg, j + 1)
                            dve.tensor_copy(mx_hi[:], mx[:, 1:2]).then_inc(m_hi, 1)
                            dve.wait_ge(m_hi, j + 1)
                            dve.tensor_copy(mx[:, 2:3], f32(mx_hi[:]))
                            dve.tensor_tensor(mx[:, 3:4], mx[:, 1:2], f32(mx_hi[:]), ALU.subtract).then_inc(m_lo, 1)
                            dve.wait_ge(m_lo, j + 1)
                            dve.tensor_copy(pair[:, 0, bass.ds(qt, 1), PW + 2 * h:PW + 2 * h + 2]
                                            .rearrange("p a c -> p (a c)"), mx[:, 2:4]).then_inc(m_out, 1)

        with nc.Block() as block:
            @block.sync
            def _(sp):
                def load(it, r):
                    sp.dma_start(pair[:, r], qkv_s[r * NT:(r + 1) * NT, :, bass.ds(SW * it, SW)]
                                 .rearrange("t p c -> p t c")).then_inc(pair_ld[r], 16)

                def store(it, r, c):
                    u = C * (B * it + r) + c
                    sp.wait_ge(o_fin, u + 1)
                    sp.dma_start(o_s[r * NT + TPB * c:r * NT + TPB * (c + 1), :, bass.ds(2 * HD * it, 2 * HD)]
                                 .rearrange("t p c -> p t c"),
                                 ofin[:, c % 2].rearrange("p t h d -> p t (h d)")).then_inc(o_dma[c % 2], 16)

                with sp.If(sp.value_load(unbounded[0:1, 0:1], min_val=0, max_val=1) > 0):
                    row_maxima_sync(sp)
                load(0, 0)
                load(0, 1)

                def body(it, first, last):
                    for r in range(B):
                        g = B * it + r
                        for c in range(C):
                            if c == 2 and not last:
                                sp.wait_ge(q_pack, 4 * g + 4)
                                sp.wait_ge(v_done, 4 * g + 4)
                                load(it + 1, r)
                            store(it, r, c)
                iterate(sp, PAIRS, body)
                for j in range(2):
                    sp.wait_ge(o_dma[j], 16 * NU // 2)

            @block.gpsimd
            def _(pool):
                pool.memset(vp[:], 0.0).then_inc(vzero, 1)
                pool.wait_ge(vzero, 1)
                for r in range(B):
                    for h in range(2):
                        pool.memset(vp[:, r, :, 64 * h + HD:64 * h + HD + 1], 1.0).then_inc(vzero, 1)
                pool.wait_ge(vzero, 5)
                for k in range(2):
                    pool.dma_start(w2_raw[:, k], w2[:, k]).then_inc(w2_ld[k], 16)

                def take_v(it, r, first):
                    g = B * it + r
                    pool.wait_ge(pair_ld[r], 16 * (it + 1))
                    if not first:
                        pool.wait_ge(pv_mm, NT * C * (g - 1))
                    for h in range(2):
                        c = QK + h * HD
                        for half in (slice(0, NT // 2), slice(NT // 2, NT)):
                            pool.tensor_scalar(vp[:, r, half, 64 * h:64 * h + HD], pair[:, r, half, c:c + HD], 1.0, None,
                                               ALU.mult).then_inc(v_done, 1)

                take_v(0, 0, True)
                take_v(0, 1, True)
                for k in range(FC):
                    pool.wait_ge(w2_ld[k % 2], 16 * (k // 2 + 1))
                    pool.tensor_scalar(w2_hi[:, k, 0:D], w2_raw[:, k % 2], 1.0, None, ALU.mult).then_inc(w2hi_done, 1)
                    pool.wait_ge(w2hi_done, k + 1)
                    pool.tensor_tensor(w2_lo[:, k], w2_raw[:, k % 2, 0:KF * P], f32(w2_hi[:, k, 0:KF * P]), ALU.subtract)
                    pool.tensor_tensor(w2_hi[:, k, D:DP], w2_raw[:, k % 2, KF * P:D], f32(w2_hi[:, k, KF * P:D]),
                                       ALU.subtract).then_inc(w2lo_done, 1)
                    if k + 2 < FC:
                        pool.wait_ge(w2lo_done, k + 1)
                        pool.dma_start(w2_raw[:, k % 2], w2[:, k + 2]).then_inc(w2_ld[k % 2], 16)
                for it in range(1, PAIRS):
                    for r in range(B):
                        take_v(it, r, False)

            @block.scalar
            def _(act):
                def body(it, first, last):
                    for r in range(B):
                        for c in range(C):
                            for kt in range(NT):
                                s = NT * (C * (B * it + r) + c) + kt
                                act.wait_ge(s_mm, s + 1)
                                if not (first and r == 0 and c == 0 and kt < 4):
                                    act.wait_ge(pv_mm, s - 3)
                                j = kt % 2
                                act.activation(prob[:, kt % 4], ps[:, 2 * j:2 * j + 2, :].rearrange("p a b -> p (a b)"),
                                               ACT.Exp).then_inc(exp_done, 1)
                iterate(act, PAIRS, body)

            @block.vector
            def _(dve):
                dve.memset(cst[:], 1.0).then_inc(cst_done, 1)
                dve.wait_ge(cst_done, 1)
                dve.tensor_copy(kpack[:, :, :, 3 * HD:PKW], cst[:]).then_inc(rows_done, 1)

                def pack_q(it, r, c):
                    n = C * (B * it + r) + c
                    dve.wait_ge(pair_ld[r], 16 * (it + 1))
                    src = pair[:, r, TPB * c:TPB * (c + 1), 0:2 * HD].rearrange("p t (h d) -> p t h d", d=HD)
                    dve.tensor_copy(qpack[:, :, :, 0:HD], src).then_inc(q_hi, 1)
                    dve.tensor_copy(qpack[:, :, :, HD:2 * HD], src)
                    dve.tensor_copy(qpack[:, :, :, 3 * HD:PKW],
                                    pair[:, r, TPB * c:TPB * (c + 1), PW:SW].rearrange("p t (h d) -> p t h d", d=2))
                    dve.wait_ge(q_hi, n + 1)
                    dve.tensor_tensor(qpack[:, :, :, 2 * HD:3 * HD], src, f32(qpack[:, :, :, 0:HD]), ALU.subtract).then_inc(q_pack, 1)

                def pack_k(it, r, c):
                    n = C * (B * it + r) + c
                    dve.wait_ge(pair_ld[r], 16 * (it + 1))
                    src = pair[:, r, TPB * c:TPB * (c + 1), 2 * HD:4 * HD].rearrange("p t (h d) -> p t h d", d=HD)
                    dve.tensor_copy(kpack[:, :, :, 0:HD], src).then_inc(k_hi, 1)
                    dve.tensor_copy(kpack[:, :, :, 2 * HD:3 * HD], src)
                    dve.wait_ge(k_hi, n + 1)
                    dve.tensor_tensor(kpack[:, :, :, HD:2 * HD], src, f32(kpack[:, :, :, 0:HD]), ALU.subtract).then_inc(k_pack, 1)

                def q_out(slot, h, group):
                    dve.wait_ge(tp, group + 1)
                    dve.tensor_copy(qT[:, slot, h], TP).then_inc(qT_done, 1)

                def k_out(r, h, c, group):
                    dve.wait_ge(tp, group + 1)
                    dve.tensor_copy(kT[:, r, h, BLK * c:BLK * (c + 1)], TP).then_inc(kT_done, 1)

                def take_o(u, slot, early):
                    dve.wait_ge(pv_mm, NT * (u + 1))
                    if not early:
                        dve.wait_ge(ot_mm, u)
                    dve.tensor_copy(osb[:], ps[0:VW, 4 + slot, :]).then_inc(o_evac, 1)

                def finish_o(u, slot, early):
                    dve.wait_ge(ot_mm, u + 1)
                    dve.reciprocal(rl[:], OT[:, :, HD:HD + 65:64]).then_inc(rl_done, 1)
                    dve.wait_ge(rl_done, u + 1)
                    if not early:
                        dve.wait_ge(o_dma[slot], 8 * (u - slot))
                    for h in range(2):
                        mul = dve.tensor_tensor(ofin[:, slot, :, h], OT[:, :, 64 * h:64 * h + HD],
                                                rl[:, :, h:h + 1].to_broadcast([P, TPB, HD]), ALU.mult)
                    mul.then_inc(o_fin, 1)

                with dve.If(dve.value_load(unbounded[0:1, 0:1], min_val=0, max_val=1) > 0):
                    row_maxima_vector(dve)
                for c in range(C):
                    if c:
                        dve.wait_ge(tp, 2 * c)
                    pack_k(0, 0, c)
                    for h in range(2):
                        k_out(0, h, c, 2 * c + h)
                pack_q(0, 0, 0)
                for h in range(2):
                    q_out(0, h, 2 * C + h)
                pack_k(0, 1, 0)
                pack_q(0, 0, 1)

                def body(it, first, last):
                    for r in range(B):
                        final = last and r == 1
                        for c in range(C):
                            u = C * (B * it + r) + c
                            group = 2 * C + 2 + 4 * u if not final else 2 * C + 2 + 4 * (NU - C) + 2 * c
                            start = first and r == 0 and c == 0
                            if not start:
                                take_o(u - 1, (c + 1) % 2, first and r == 0 and c == 1)
                            more_q = not (final and c == C - 1)
                            if more_q:
                                q_out((c + 1) % 2, 0, group)
                            if not start:
                                finish_o(u - 1, (c + 1) % 2, first and r == 0 and c <= 2)
                            if more_q:
                                q_out((c + 1) % 2, 1, group + 1)
                            if not (final and c >= C - 2):
                                if c < C - 2:
                                    pack_q(it, r, c + 2)
                                else:
                                    pack_q(it + r, 1 - r, c + 2 - C)
                            if not final:
                                for h in range(2):
                                    k_out(1 - r, h, c, group + 2 + h)
                                if c < C - 1:
                                    pack_k(it + r, 1 - r, c + 1)
                                elif not (last and r == 0):
                                    pack_k(it + 1, r, 0)
                iterate(dve, PAIRS, body)
                take_o(NU - 1, 1, False)
                finish_o(NU - 1, 1, False)

            @block.tensor
            def _(pe):
                def turn(pack, h, t, mark):
                    mm = pe.transpose(TP[:, t * P:(t + 1) * P], f32(pack[:, t, h, 0:PKW]), ident[:])
                    if mark:
                        mm.then_inc(tp, 1)

                def scores(r, c, kt, u):
                    if kt == 0:
                        pe.wait_ge(qT_done, 2 * (u + 1))
                    if c == 0 and kt % TPB == 0:
                        pe.wait_ge(kT_done, 2 * u + 2 * (kt // TPB + 1))
                    j = kt % 2
                    for h in range(2):
                        mm = pe.matmul(ps[:, 2 * j + h, :], kT[:, r, h, kt * P:(kt + 1) * P], qT[:, c % 2, h],
                                       start=True, stop=True)
                    mm.then_inc(s_mm, 1)

                with pe.If(pe.value_load(unbounded[0:1, 0:1], min_val=0, max_val=1) > 0):
                    row_maxima_tensor(pe)
                for c in range(C):
                    pe.wait_ge(k_pack, c + 1)
                    if c == 0:
                        pe.wait_ge(rows_done, 1)
                    for h in range(2):
                        wait(pe, kT_done, 2 * c + h)
                        for t in range(TPB):
                            turn(kpack, h, t, t == TPB - 1)
                pe.wait_ge(q_pack, 1)
                for h in range(2):
                    if h == 0:
                        pe.wait_ge(kT_done, 2 * C)
                    else:
                        pe.wait_ge(qT_done, 1)
                    for t in range(TPB):
                        turn(qpack, h, t, t == TPB - 1)
                for kt in range(2):
                    scores(0, 0, kt, 0)

                def turn_o(u):
                    pe.wait_ge(o_evac, u + 1)
                    if not (isinstance(u, int) and u == 0):
                        pe.wait_ge(o_fin, u)
                    for t in range(TPB):
                        mm = pe.transpose(OT[:, t, 0:VW], osb[:, t * P:(t + 1) * P], ident[0:VW, 0:VW])
                    mm.then_inc(ot_mm, 1)

                def body(it, first, last):
                    for r in range(B):
                        final = last and r == 1
                        for c in range(C):
                            u = C * (B * it + r) + c
                            for kt0 in range(0, NT, 2):
                                steps = (kt0, kt0 + 1)
                                pe.wait_ge(exp_done, NT * u + kt0 + 2)
                                for kt in steps:
                                    if kt + 2 < NT:
                                        scores(r, c, kt + 2, u)
                                    elif c + 1 < C:
                                        scores(r, c + 1, kt + 2 - NT, u + 1)
                                    elif not final:
                                        scores(1 - r, 0, kt + 2 - NT, u + 1)
                                for kt in steps:
                                    group, t = divmod(kt, TPB)
                                    if group < 2:
                                        if not (final and c == C - 1):
                                            if t == 0:
                                                if group == 0:
                                                    pe.wait_ge(q_pack, u + 2)
                                                    pe.wait_ge(kT_done, 2 * C + 2 * u if not final else 2 * C + 2 * (NU - C))
                                                pe.wait_ge(qT_done, 2 + 2 * u + group)
                                            turn(qpack, group, t, t == TPB - 1)
                                    elif not final:
                                        if t == 0:
                                            if group == 2:
                                                pe.wait_ge(k_pack, u + C + 1)
                                                pe.wait_ge(qT_done, 4 + 2 * u)
                                            else:
                                                pe.wait_ge(kT_done, 2 * C + 2 * u + 1)
                                        turn(kpack, group - 2, t, t == TPB - 1)
                                if kt0 == 2 and not (first and r == 0 and c == 0):
                                    turn_o(u - 1)
                                if kt0 == 0:
                                    if c == 0:
                                        pe.wait_ge(v_done, 4 * (B * it + r) + 4)
                                    if not (first and r == 0 and c < 2):
                                        pe.wait_ge(o_evac, u - 1)
                                O = ps[:, 4 + c % 2, :]
                                for kt in steps:
                                    j = kt % 4
                                    pe.matmul(O[0:64], vp[:, r, kt, 0:64], prob[:, j, 0:BLK], start=kt == 0, stop=kt == NT - 1)
                                    pe.matmul(O[64:VW], vp[:, r, kt, 64:VW], prob[:, j, BLK:2 * BLK], start=kt == 0,
                                              stop=kt == NT - 1).then_inc(pv_mm, 1)
                iterate(pe, PAIRS, body)
                turn_o(NU - 1)


def proj_phase(nc, ctx, sb, ps, o_s, xT, wp, x1_s, ident, mod, gate_b):
    with ExitStack() as st:
        def sem(name):
            return ctx.enter_context(nc.semaphore("c_" + name))

        ob = sb(st, "ob", [P, B, TPB, DP])
        xb = sb(st, "cxb", [P, B, KC, BLK])
        wp_raw = sb(st, "wp_raw", [P, KC, DP])
        wp_hi = sb(st, "wp_hi", [P, KC, DP], F32R)
        wp_lo = sb(st, "wp_lo", [P, KC, DP], F32R)
        o_hi = sb(st, "o_hi", [P, B, KC, BLK], F32R)
        o_lo = sb(st, "o_lo", [P, B, KF, BLK], F32R)
        gated = sb(st, "gated", [P, 2, BLK])
        wp_ld = sem("wp_ld")
        o_ld = [sem(f"o_ld{j}") for j in range(B)]
        x_ld = [sem(f"x_ld{j}") for j in range(B)]
        whi_done, wlo_done = sem("whi_done"), sem("wlo_done")
        tp, hi_done, lo_done = sem("tp"), sem("hi_done"), sem("lo_done")
        proj_mm, gate_done, x1_done = sem("proj_mm"), sem("gate_done"), sem("x1_done")
        x1_dma = [sem(f"x1_dma{j}") for j in range(B)]
        with nc.Block() as block:
            @block.sync
            def _(sp):
                sp.dma_start(wp_raw[:], wp).then_inc(wp_ld, 16)

                def load_o(it, r):
                    tiles = o_s[bass.ds(r * NT + TPB * it, TPB)].rearrange("t p c -> p t c")
                    sp.dma_start(ob[:, r, :, 0:D], tiles).then_inc(o_ld[r], 16)
                    sp.dma_start(ob[:, r, :, D:DP], tiles[:, :, KF * P:D]).then_inc(o_ld[r], 16)

                def load_x(it, r):
                    sp.dma_start(xb[:, r], xT[:, :, bass.ds(r * N + BLK * it, BLK)]).then_inc(x_ld[r], 16)

                for r in range(B):
                    load_o(0, r)
                    load_x(0, r)

                def body(it, first, last):
                    for r in range(B):
                        i = B * it + r
                        if not last:
                            sp.wait_ge(tp, KC * (i + 1))
                            load_o(it + 1, r)
                        sp.wait_ge(x1_done, KC * (i + 1))
                        sp.dma_start(x1_s[:, :, bass.ds(r * N + BLK * it, BLK)], xb[:, r]).then_inc(x1_dma[r], 16)
                        if not last:
                            sp.wait_ge(x1_dma[r], 16 * (it + 1))
                            load_x(it + 1, r)
                iterate(sp, NIT, body)
                for r in range(B):
                    sp.wait_ge(x1_dma[r], 16 * NIT)

            @block.scalar
            def _(act):
                act.wait_ge(wp_ld, 16)
                act.activation(wp_hi[:], wp_raw[:], ACT.Copy).then_inc(whi_done, 1)

                def turn_hi(i, r, k):
                    act.wait_ge(tp, KC * i + k + 1)
                    act.activation(o_hi[:, r, k], ps[:, (r + k) % 2, :], ACT.Copy).then_inc(hi_done, 1)

                for k in range(KC):
                    turn_hi(0, 0, k)

                def body(it, first, last):
                    for r in range(B):
                        i = B * it + r
                        for m in range(KC):
                            j = (KC * r + m) % 2
                            act.wait_ge(proj_mm, KC * i + m + 1)
                            if not (first and r == 0 and m < 2):
                                act.wait_ge(x1_done, KC * i + m - 1)
                            act.activation(gated[:, j], ps[:, 2 + j, :], ACT.Identity, bias=gate_b[:, 0, m, r:r + 1],
                                           scale=mod[:, GATE_MSA, m, r:r + 1]).then_inc(gate_done, 1)
                            if not (last and r == 1):
                                turn_hi(i + 1, 1 - r, m)
                iterate(act, NIT, body)

            @block.vector
            def _(dve):
                dve.wait_ge(whi_done, 1)
                dve.tensor_tensor(wp_lo[:], wp_raw[:], f32(wp_hi[:]), ALU.subtract).then_inc(wlo_done, 1)

                def turn_lo(i, r, k):
                    dve.wait_ge(hi_done, KC * i + k + 1)
                    low(dve, o_hi[:, r], o_lo[:, r], ps[:, (r + k) % 2, :], k).then_inc(lo_done, 1)

                for k in range(KC):
                    turn_lo(0, 0, k)

                def body(it, first, last):
                    for r in range(B):
                        i = B * it + r
                        for m in range(KC):
                            j = (KC * r + m) % 2
                            dve.wait_ge(gate_done, KC * i + m + 1)
                            if m == 0:
                                dve.wait_ge(x_ld[r], 16 * (it + 1))
                            dve.tensor_tensor(xb[:, r, m], xb[:, r, m], gated[:, j], ALU.add).then_inc(x1_done, 1)
                            if not (last and r == 1):
                                turn_lo(i + 1, 1 - r, m)
                iterate(dve, NIT, body)

            @block.tensor
            def _(pe):
                def turn(it, i, r, k, early):
                    if k == 0:
                        pe.wait_ge(o_ld[r], 32 * (it + 1))
                    if not (early and k < 2):
                        pe.wait_ge(lo_done, KC * i + k - 1)
                    for t in range(TPB):
                        mm = pe.transpose(ps[:, (r + k) % 2, t * P:(t + 1) * P], ob[:, r, t, k * P:(k + 1) * P], ident[:])
                    mm.then_inc(tp, 1)

                for k in range(KC):
                    turn(0, 0, 0, k, True)
                pe.wait_ge(wlo_done, 1)

                def body(it, first, last):
                    for r in range(B):
                        i = B * it + r
                        pe.wait_ge(lo_done, KC * (i + 1))
                        for m in range(KC):
                            j = (KC * r + m) % 2
                            if not (first and r == 0 and m < 2):
                                pe.wait_ge(gate_done, KC * i + m - 1)
                            for k in range(KC):
                                for n, (w, a) in enumerate(passes(k, wp_hi, wp_lo, o_hi, o_lo)):
                                    mm = pe.matmul(ps[:, 2 + j, :], w[:, k, m * P:(m + 1) * P], a[:, r, k],
                                                   start=k == 0 and n == 0, stop=k == KF and n == 1)
                            mm.then_inc(proj_mm, 1)
                            if not (last and r == 1):
                                turn(it + r, i + 1, 1 - r, m, False)
                iterate(pe, NIT, body)


def mlp_phase(nc, ctx, sb, ps, x1_s, w1, outT, ones, mod, gate_b, gain, f1b_t, w2_hi, w2_lo):
    K_SQ, K_SS, K_REC, K_H = 3, 8, 9, 12
    with ExitStack() as st:
        def sem(name):
            return ctx.enter_context(nc.semaphore("d_" + name))

        x1 = sb(st, "x1", [P, B, KC, BLK])
        tmp = sb(st, "dtmp", [P, KC, BLK])
        rb = sb(st, "drb", [P, BLK])
        h_hi = sb(st, "dh_hi", [P, B, KC, BLK], F32R)
        h_lo = sb(st, "dh_lo", [P, B, KF, BLK], F32R)
        w1_raw = sb(st, "w1_raw", [P, 2, KC, P])
        w1_hi = sb(st, "w1_hi", [P, 2, KC, P], F32R)
        w1_lo = sb(st, "w1_lo", [P, 2, KC, P], F32R)
        act32 = sb(st, "act32", [P, 2, BLK])
        a_hi = sb(st, "a_hi", [P, 2, BLK], F32R)
        a_lo = sb(st, "a_lo", [P, 2, BLK], F32R)
        gated = sb(st, "dgated", [P, 2, BLK])
        tail = sb(st, "tail", [TL, BLK])

        x_ld = [sem(f"x_ld{j}") for j in range(B)]
        w1_ld = [sem(f"w1_ld{j}") for j in range(2)]
        w1hi_done, w1lo_done = sem("w1hi_done"), sem("w1lo_done")
        sq_done, sqhi_done, sqlo_done, ss_done = sem("sq_done"), sem("sqhi_done"), sem("sqlo_done"), sem("ss_done")
        nrm_done, r_max, r_rec, r_done, xr_done = sem("nrm_done"), sem("r_max"), sem("r_rec"), sem("r_done"), sem("xr_done")
        aff_done, hhi_done, hlo_done = sem("aff_done"), sem("hhi_done"), sem("hlo_done")
        fc1_mm, gelu_done, alo_done, fc2_mm = sem("fc1_mm"), sem("gelu_done"), sem("alo_done"), sem("fc2_mm")
        gate_done, tail_done, out_done = sem("gate_done"), sem("tail_done"), sem("out_done")
        out_dma = [sem(f"out_dma{j}") for j in range(B)]
        NB = B * NIT
        RB = ps[:, 7, :]

        with nc.Block() as block:
            @block.sync
            def _(sp):
                def load_w1(k, slot, count):
                    wait(sp, w1lo_done, count - 1)
                    wait(sp, w1hi_done, count - 1)
                    sp.dma_start(w1_raw[:, slot], w1[k]).then_inc(w1_ld[slot], 16)

                sp.dma_start(x1[:, 0], x1_s[:, :, 0:BLK]).then_inc(x_ld[0], 16)
                load_w1(0, 0, 0)
                load_w1(1, 1, 0)
                sp.dma_start(x1[:, 1], x1_s[:, :, N:N + BLK]).then_inc(x_ld[1], 16)

                def body(it, first, last):
                    for r in range(B):
                        i = B * it + r
                        for k in range(FC):
                            if not (last and r == 1 and k + 2 >= FC):
                                load_w1((k + 2) % FC, k % 2, FC * i + k + 2)
                            if k == 1 and not (first and r == 0) and not (last and r == 1):
                                sp.wait_ge(out_dma[1 - r], 16 * (it + r))
                                sp.dma_start(x1[:, 1 - r], x1_s[:, :, bass.ds((1 - r) * N + BLK * (it + r), BLK)]
                                             ).then_inc(x_ld[1 - r], 16)
                iterate(sp, NIT, body)
                for r in range(B):
                    sp.wait_ge(out_dma[r], 16 * NIT)

            def act_square(act, it, i, r, m):
                if m == 0:
                    act.wait_ge(x_ld[r], 16 * (it + 1))
                    wait(act, hlo_done, KC * i)
                    wait(act, fc1_mm, FC * (i - 1))
                act.activation(tmp[:, m], x1[:, r, m], ACT.Square).then_inc(sq_done, 1)
                act.activation(h_hi[:, r, m], x1[:, r, m], ACT.Square).then_inc(sqhi_done, 1)

            def act_norm(act, i):
                act.wait_ge(ss_done, i + 1)
                wait(act, xr_done, KC * i)
                act.activation(rb[:], RB, ACT.Sqrt).then_inc(nrm_done, 1)

            def act_h(act, i, r, m):
                act.wait_ge(xr_done, KC * i + m + 1)
                act.activation(tmp[:, m], tmp[:, m], ACT.Identity, bias=mod[:, SHIFT_MLP, m, r:r + 1],
                               scale=mod[:, SCALE_MLP, m, r:r + 1]).then_inc(aff_done, 1)
                act.wait_ge(aff_done, KC * i + m + 1)
                act.activation(h_hi[:, r, m], tmp[:, m], ACT.Copy).then_inc(hhi_done, 1)

            @block.scalar
            def _(act):
                def split_w1(slot, count, it, fours, k):
                    act.wait_ge(w1_ld[slot], 16 * fours)
                    wait(act, fc1_mm, count - 1)
                    act.activation(w1_hi[:, slot], w1_raw[:, slot], ACT.Copy).then_inc(w1hi_done, 1)

                for m in range(KC):
                    act_square(act, 0, 0, 0, m)
                split_w1(0, 0, 0, 1, 0)
                split_w1(1, 1, 0, 1, 1)
                act_norm(act, 0)
                for m in range(KC):
                    act_h(act, 0, 0, m)

                def gelu(i, k, early):
                    j, slot = FC * i + k, k % 2
                    act.wait_ge(fc1_mm, j + 1)
                    if not early:
                        act.wait_ge(alo_done, j - 1)
                    act.activation(act32[:, slot], ps[:, 5 + slot, :], ACT.Gelu_apprx_tanh, bias=f1b_t[:, k:k + 1])
                    if not early:
                        act.wait_ge(fc2_mm, j - 1)
                    act.activation(a_hi[:, slot], ps[:, 5 + slot, :], ACT.Gelu_apprx_tanh,
                                   bias=f1b_t[:, k:k + 1]).then_inc(gelu_done, 1)

                def gates(i, r, early):
                    act.wait_ge(fc2_mm, FC * (i + 1))
                    for m in range(KC):
                        n = KC * i + m
                        if not (early and m < 2):
                            act.wait_ge(out_done, n - 1)
                        act.activation(gated[:, (r + m) % 2], ps[:, m, :], ACT.Identity,
                                       bias=gate_b[:, 1, m, r:r + 1], scale=mod[:, GATE_MLP, m, r:r + 1]).then_inc(gate_done, 1)

                def body(it, first, last):
                    for r in range(B):
                        i = B * it + r
                        more = not (last and r == 1)
                        for k in range(FC):
                            gelu(i, k, first and r == 0 and k < 2)
                            if k == 0 and not (first and r == 0):
                                gates(i - 1, 1 - r, first and r == 1)
                            if k == 1 and not (first and r == 0):
                                act.wait_ge(out_done, KC * i)
                                act.dma_start(outT[:, :, bass.ds((1 - r) * N + BLK * (it + r - 1), BLK)],
                                              x1[:, 1 - r]).then_inc(out_dma[1 - r], 16)
                            if more or k + 2 < FC:
                                j = FC * i + k + 2
                                split_w1(k % 2, j, it, FC // 2 * i + k // 2 + 2, k)
                            if more:
                                if K_SQ <= k < K_SQ + KC:
                                    act_square(act, it + r, i + 1, 1 - r, k - K_SQ)
                                if k == K_SS:
                                    act_norm(act, i + 1)
                                if K_H <= k < K_H + KC:
                                    act_h(act, i + 1, 1 - r, k - K_H)
                iterate(act, NIT, body)
                gates(NB - 1, 1, False)
                act.wait_ge(out_done, KC * NB)
                act.dma_start(outT[:, :, 2 * N - BLK:2 * N], x1[:, 1]).then_inc(out_dma[1], 16)

            @block.vector
            def _(dve):
                def square_lo(i, r, m):
                    dve.wait_ge(sqhi_done, KC * i + m + 1)
                    low(dve, h_hi[:, r], h_lo[:, r], tmp[:, m], m).then_inc(sqlo_done, 1)

                def reciprocal(i, part):
                    half = slice(part * BLK // 2, (part + 1) * BLK // 2)
                    if part == 0:
                        dve.wait_ge(nrm_done, i + 1)
                        dve.tensor_scalar(rb[:], rb[:], EPS, None, ALU.max).then_inc(r_max, 1)
                        dve.wait_ge(r_max, i + 1)
                    dve.reciprocal(rb[:, half], rb[:, half]).then_inc(r_rec, 1)
                    if part == 1:
                        dve.wait_ge(r_rec, 2 * i + 2)
                        dve.tensor_scalar(rb[:], rb[:], float(D) ** 0.5, gain[:, 1:2], ALU.mult, ALU.mult).then_inc(r_done, 1)

                def normed(i, r, m):
                    if m == 0:
                        dve.wait_ge(r_done, i + 1)
                    dve.tensor_tensor(tmp[:, m], x1[:, r, m], rb[:], ALU.mult).then_inc(xr_done, 1)

                def h_low(i, r, m):
                    dve.wait_ge(hhi_done, KC * i + m + 1)
                    low(dve, h_hi[:, r], h_lo[:, r], tmp[:, m], m).then_inc(hlo_done, 1)

                def split_w1(slot, count):
                    dve.wait_ge(w1hi_done, count + 1)
                    dve.tensor_tensor(w1_lo[:, slot], w1_raw[:, slot], f32(w1_hi[:, slot]), ALU.subtract).then_inc(w1lo_done, 1)

                for m in range(KC):
                    square_lo(0, 0, m)
                split_w1(0, 0)
                split_w1(1, 1)
                reciprocal(0, 0)
                reciprocal(0, 1)
                for m in range(KC):
                    normed(0, 0, m)
                for m in range(KC):
                    h_low(0, 0, m)

                def add_x1(i, r):
                    for m in range(KF):
                        dve.wait_ge(gate_done, KC * i + m + 1)
                        dve.tensor_tensor(x1[:, r, m], x1[:, r, m], gated[:, (r + m) % 2], ALU.add).then_inc(out_done, 1)
                    dve.wait_ge(gate_done, KC * (i + 1))
                    dve.tensor_copy(tail[:], gated[TL:P, r]).then_inc(tail_done, 1)
                    dve.tensor_tensor(x1[0:TL, r, KF], x1[0:TL, r, KF], gated[0:TL, r], ALU.add).then_inc(tail_done, 1)
                    dve.wait_ge(tail_done, 2 * i + 2)
                    dve.tensor_tensor(x1[0:TL, r, KF], x1[0:TL, r, KF], tail[:], ALU.add).then_inc(out_done, 1)

                def body(it, first, last):
                    for r in range(B):
                        i = B * it + r
                        more = not (last and r == 1)
                        for k in range(FC):
                            j, slot = FC * i + k, k % 2
                            dve.wait_ge(gelu_done, j + 1)
                            dve.tensor_tensor(a_lo[:, slot], act32[:, slot], f32(a_hi[:, slot]), ALU.subtract).then_inc(alo_done, 1)
                            if k == 0 and not (first and r == 0):
                                add_x1(i - 1, 1 - r)
                            if more or k + 2 < FC:
                                split_w1(slot, j + 2)
                            if more:
                                if K_SQ <= k < K_SQ + KC:
                                    square_lo(i + 1, 1 - r, k - K_SQ)
                                if k in (K_REC, K_REC + 1):
                                    reciprocal(i + 1, k - K_REC)
                                if K_REC + 2 <= k < K_REC + 2 + KC:
                                    normed(i + 1, 1 - r, k - K_REC - 2)
                                if K_H <= k < K_H + KC:
                                    h_low(i + 1, 1 - r, k - K_H)
                iterate(dve, NIT, body)
                add_x1(NB - 1, 1)

            @block.tensor
            def _(pe):
                def sum_squares(i, r):
                    pe.wait_ge(sqlo_done, KC * (i + 1))
                    wait(pe, nrm_done, i)
                    for k in range(KC):
                        for part in (h_hi, h_lo)[:2 if k < KF else 1]:
                            mm = pe.matmul(RB, ones[:], part[:, r, k], start=k == 0 and part is h_hi, stop=k == KF)
                    mm.then_inc(ss_done, 1)

                def fc1(i, r, k, early):
                    j, slot = FC * i + k, k % 2
                    if k == 0:
                        pe.wait_ge(hlo_done, KC * (i + 1))
                    pe.wait_ge(w1lo_done, j + 1)
                    if not early:
                        pe.wait_ge(gelu_done, j - 1)
                    for c in range(KC):
                        for n, (w, a) in enumerate(passes(c, w1_hi, w1_lo, h_hi, h_lo)):
                            mm = pe.matmul(ps[:, 5 + slot, :], w[:, slot, c], a[:, r, c], start=c == 0 and n == 0,
                                           stop=c == KF and n == 1)
                    mm.then_inc(fc1_mm, 1)

                sum_squares(0, 0)
                fc1(0, 0, 0, True)

                def body(it, first, last):
                    for r in range(B):
                        i = B * it + r
                        more = not (last and r == 1)
                        for k in range(FC):
                            j, slot = FC * i + k, k % 2
                            if k + 1 < FC:
                                fc1(i, r, k + 1, first and r == 0 and k == 0)
                            elif more:
                                fc1(i + 1, 1 - r, 0, False)
                            if k == K_SS and more:
                                sum_squares(i + 1, 1 - r)
                            pe.wait_ge(alo_done, j + 1)
                            for m in range(KC):
                                if k == 0 and not (first and r == 0):
                                    pe.wait_ge(gate_done, KC * (i - 1) + m + 1)
                                parts = ((w2_hi, a_hi), (w2_lo, a_hi), (w2_hi, a_lo)) if m < KF else (
                                    (w2_hi, a_hi), (w2_hi, a_lo))
                                for n, (w, a) in enumerate(parts):
                                    mm = pe.matmul(ps[:, m, :], w[:, k, m * P:(m + 1) * P], a[:, slot],
                                                   start=k == 0 and n == 0, stop=k == FC - 1 and n == len(parts) - 1)
                            mm.then_inc(fc2_mm, 1)
                iterate(pe, NIT, body)


def columns(a):
    return np.concatenate([a, a[..., KF * P:]], axis=-1)


def rows(a):
    a = columns(a.swapaxes(0, -1)).swapaxes(0, -1)
    return np.ascontiguousarray(a.reshape((KC, P) + a.shape[1:]).swapaxes(0, 1))


def by_pair(a):
    return a.reshape((3, PAIRS, 2 * HD) + a.shape[1:]).swapaxes(0, 1).reshape(a.shape)


def kernel(x, cond_1152, L0_cond_g1, L0_cond_g2, L0_cond_qkv_w, L0_cond_qkv_b, L0_cond_qg, L0_cond_kg, L0_cond_proj_w,
           L0_cond_proj_b, L0_cond_fc1_w, L0_cond_fc1_b, L0_cond_fc2_w, L0_cond_fc2_b, L0_cond_ada_w, L0_cond_ada_b):
    import concourse.bacc as bacc
    from concourse.bass_utils import run_bass_kernel_spmd

    n = np.asarray
    ada = columns(n(L0_cond_ada_w).reshape(6, D, D).transpose(2, 0, 1))
    f2b = rows(n(L0_cond_fc2_b))
    f2b[TL:, KF] = 0
    arrays = {
        "xT": rows(n(x).reshape(B * N, D).T),
        "cT": rows(n(cond_1152).T),
        "ada": np.ascontiguousarray(rows(ada).swapaxes(1, 2)),
        "adab": np.ascontiguousarray(rows(n(L0_cond_ada_b).reshape(6, D).T).swapaxes(1, 2).reshape(P, 6 * KC)),
        "wqkv": rows(by_pair(n(L0_cond_qkv_w)).T),
        "qkvb": np.ascontiguousarray(by_pair(n(L0_cond_qkv_b))),
        "wp": rows(columns(n(L0_cond_proj_w).T)),
        "pb": rows(n(L0_cond_proj_b)),
        "w1": np.ascontiguousarray(rows(n(L0_cond_fc1_w).T).reshape(P, KC, FC, P).transpose(2, 0, 1, 3)),
        "f1b": np.ascontiguousarray(n(L0_cond_fc1_b).reshape(FC, P).T),
        "w2": np.ascontiguousarray(n(L0_cond_fc2_w).T.reshape(FC, P, D).transpose(1, 0, 2)),
        "f2b": f2b,
        "g1": n(L0_cond_g1), "g2": n(L0_cond_g2), "qg": n(L0_cond_qg), "kg": n(L0_cond_kg),
    }
    nc = bacc.Bacc("TRN2", target_bir_lowering=False, num_devices=1)
    ap = {k: nc.dram_tensor(k, a.shape, F32, kind="ExternalInput").ap() for k, a in arrays.items()}
    outT = nc.dram_tensor("outT", (P, KC, B * N), F32, kind="ExternalOutput").ap()
    build(nc, ap["xT"], ap["cT"], ap["ada"], ap["adab"], ap["wqkv"], ap["qkvb"], ap["wp"], ap["pb"], ap["w1"], ap["f1b"],
          ap["w2"], ap["f2b"], [ap["g1"], ap["g2"], ap["qg"], ap["kg"]], outT)
    out = run_bass_kernel_spmd(nc, [arrays], core_ids=[0]).results[0]["outT"]
    return np.ascontiguousarray(out.transpose(1, 0, 2).reshape(DP, B * N)[:D].T).reshape(B, N, D)
```

```python
from contextlib import ExitStack

import concourse.bass as bass
import numpy as np
from concourse import mybir

F32 = mybir.dt.float32
F32R = mybir.dt.float32r
ACT = mybir.ActivationFunctionType
ALU = mybir.AluOpType
AX = mybir.AxisListType

P = 128
B, N, D = 2, 2048, 576
H, HD = 16, 36
F = 4 * D
KF = D // P
TL = D - KF * P
KC = KF + 1
DP = KC * P
BLK = 512
NIT = N // BLK
TPB = BLK // P
NT = N // P
FC = F // P
PAIRS = H // 2
PW = 3 * 2 * HD
QK = 2 * 2 * HD
SW = PW + 4
PKW = 3 * HD + 2
PKS = 112
VW = 64 + HD + 1
EPS = 1e-12
MAX_FREE = 60.0
SHIFT_MSA, SCALE_MSA, GATE_MSA, SHIFT_MLP, SCALE_MLP, GATE_MLP = range(6)


def wait(eng, sem, value):
    if isinstance(value, int) and value <= 0:
        return
    eng.wait_ge(sem, value)


def iterate(eng, count, body):
    body(0, True, False)
    with eng.Fori(1, count - 1) as it:
        body(it, False, False)
    body(count - 1, False, True)


def passes(k, w_hi, w_lo, a_hi, a_lo):
    return ((w_hi, a_hi), (w_lo, a_hi), (w_hi, a_lo)) if k < KF else ((w_hi, a_hi), (w_lo, a_hi))


def low(eng, hi, lo, full, k):
    if k < KF:
        return eng.tensor_tensor(lo[:, k], full, f32(hi[:, k]), ALU.subtract)
    return eng.tensor_tensor(hi[TL:P, k], full[TL:P], f32(hi[TL:P, k]), ALU.subtract)


def lows(eng, hi, lo, full):
    eng.tensor_tensor(lo, full[:, 0:KF], f32(hi[:, 0:KF]), ALU.subtract)
    return low(eng, hi, lo, full[:, KF], KF)


def f32(ap):
    return ap.bitcast(F32)


def build(nc, xT, cT, ada, adan, adab, wqkv, qkvb, wp, pb, w1, f1b, w2, f2b, gains, outT):
    qkv_s = nc.dram_tensor("qkv_scratch", (B * NT, P, PAIRS * SW), F32, kind="Internal").ap()
    o_s = nc.dram_tensor("o_scratch", (B * NT, P, D), F32, kind="Internal").ap()
    x1_s = nc.dram_tensor("x1_scratch", (P, KC, B * N), F32, kind="Internal").ap()
    with ExitStack() as ctx:
        ps = ctx.enter_context(nc.psum_tensor("ps", [P, 8, 512], F32))

        def sb(stack, name, shape, dt=F32):
            return stack.enter_context(nc.sbuf_tensor(name, shape, dt))

        ident = sb(ctx, "ident", [P, P])
        ones = sb(ctx, "ones", [P, P], F32R)
        mod = sb(ctx, "mod", [P, 6, KC, B])
        gate_b = sb(ctx, "gate_b", [P, 2, KC, B])
        gain = sb(ctx, "gain", [P, 4])
        qscale = sb(ctx, "qscale", [P, 1])
        bound = sb(ctx, "bound", [P, 1])
        unbounded = sb(ctx, "unbounded", [P, 1], mybir.dt.int32)
        pb_t = sb(ctx, "pb_t", [P, KC])
        f2b_t = sb(ctx, "f2b_t", [P, KC])
        f1b_t = sb(ctx, "f1b_t", [P, FC])

        qkv_phase(nc, ctx, sb, ps, xT, cT, ada, adan, adab, wqkv, qkvb, pb, f1b, f2b, gains, qkv_s,
                  ident, ones, mod, gate_b, gain, qscale, bound, unbounded, pb_t, f2b_t, f1b_t)
        w2_hi = sb(ctx, "w2_hi", [P, FC, DP], F32R)
        w2_lo = sb(ctx, "w2_lo", [P, FC, KF * P], F32R)
        attention_phase(nc, ctx, sb, ps, qkv_s, o_s, w2, ident, unbounded, w2_hi, w2_lo)
        proj_phase(nc, ctx, sb, ps, o_s, xT, wp, x1_s, ident, mod, gate_b)
        mlp_phase(nc, ctx, sb, ps, x1_s, w1, outT, ones, mod, gate_b, gain, f1b_t, w2_hi, w2_lo)


def qkv_phase(nc, ctx, sb, ps, xT, cT, ada, adan, adab, wqkv, qkvb, pb, f1b, f2b, gains, qkv_s,
              ident, ones, mod, gate_b, gain, qscale, bound, unbounded, pb_t, f2b_t, f1b_t):
    PIECE = 2 * PW
    NP = PAIRS // 2
    with ExitStack() as st:
        def sem(name):
            return ctx.enter_context(nc.semaphore("a_" + name))

        aw = sb(st, "aw", [P, 2, KC * DP])
        adab_t = sb(st, "adab_t", [P, 6 * KC])
        c_t = sb(st, "c_t", [P, KC, B])
        c_e = sb(st, "c_e", [P, KC, B])
        c_s = sb(st, "c_s", [P, KC, B])
        c_b = sb(st, "c_b", [P, B, D])
        dots = sb(st, "dots", [P, B, KC])
        ones32 = sb(st, "ones32", [P, P])
        warm = sb(st, "warm", [P, 1])
        w_raw = sb(st, "w_raw", [P, KC, PIECE])
        w_hi = sb(st, "w_hi", [P, KC, NP * PIECE], F32R)
        w_lo = sb(st, "w_lo", [P, KC, NP * PIECE], F32R)
        bias = sb(st, "bias", [P, NP * PIECE])
        xb = sb(st, "xb", [P, 2, KC, BLK])
        tmp = sb(st, "tmp", [P, KC, BLK])
        rb = sb(st, "rb", [P, BLK])
        h_hi = sb(st, "h_hi", [P, 2, KC, BLK], F32R)
        h_lo = sb(st, "h_lo", [P, 2, KF, BLK], F32R)
        stage = sb(st, "stage", [P, 2, PAIRS, SW])
        sqb = sb(st, "sqb", [P, PAIRS, QK])
        ssb = sb(st, "ssb", [P, PAIRS, 4])
        rt = sb(st, "rt", [P, PAIRS, 4])

        aw01 = aw[:].rearrange("p s (k c) -> p s k c", k=KC)
        awn = aw[:, 1, 0:KC * D].rearrange("p (m c) -> p m c", m=KC)
        prod = w_raw[:].rearrange("p k c -> p (k c)")[:, 0:D]
        raw = [w_raw[:],
               stage[:].rearrange("p s a c -> p (s a c)")[:, 0:KC * PIECE].rearrange("p (k c) -> p k c", k=KC),
               aw[:, 0, 0:KC * PIECE].rearrange("p (k c) -> p k c", k=KC), w_raw[:]]

        c_ld, small_ld, gain_ld, late_ld = sem("c_ld"), sem("small_ld"), sem("gain_ld"), sem("late_ld")
        aw_ld = [sem(f"aw_ld{j}") for j in range(2)]
        w_ld = [sem(f"w_ld{j}") for j in range(NP)]
        bias_ld, awn_ld = sem("bias_ld"), sem("awn_ld")
        x_ld = [sem(f"x_ld{j}") for j in range(2)]
        setup, ident_done, ones_done = sem("setup"), sem("ident_done"), sem("ones_done")
        c_exp, c_one, c_rec, c_silu = sem("c_exp"), sem("c_one"), sem("c_rec"), sem("c_silu")
        cb_mm, cb_done = sem("cb_mm"), sem("cb_done")
        mod_mm, mod_add, mod_one, mod_done = sem("mod_mm"), sem("mod_add"), sem("mod_one"), sem("mod_done")
        dot_done, modn_add, modn_one = sem("dot_done"), sem("modn_add"), sem("modn_one")
        gain_a, gain_c, gain_d = sem("gain_a"), sem("gain_c"), sem("gain_d")
        tanh_done = sem("tanh_done")
        whi_done, wlo_done, wlo_last = sem("whi_done"), sem("wlo_done"), sem("wlo_last")
        sq0_done, xr0_done, hhi0_done = sem("sq0_done"), sem("xr0_done"), sem("hhi0_done")
        sq_done, sqlo_done, ss_done, nrm_done = sem("sq_done"), sem("sqlo_done"), sem("ss_done"), sem("nrm_done")
        r_max, r_rec, r_done, xr_done = sem("r_max"), sem("r_rec"), sem("r_done"), sem("xr_done")
        aff_done, hhi_done, hlo_done = sem("aff_done"), sem("hhi_done"), sem("hlo_done")
        qkv_mm, evac_done, sqt_done, red_done = sem("qkv_mm"), sem("evac_done"), sem("sqt_done"), sem("red_done")
        rt_done, t_max, t_rec, t_scl, scale_done = sem("rt_done"), sem("t_max"), sem("t_rec"), sem("t_scl"), sem("scale_done")
        st_dma = [sem(f"st_dma{j}") for j in range(2)]

        RB, MOD0 = ps[:, 4, :], ps[:, 5, 0:KC * B].rearrange("p (m b) -> p m b", b=B)
        MOD1 = [ps[:, m if m < KF else 6, 0:B] for m in range(KC)]
        CT = RB[:, 0:P].rearrange("p (b c) -> p b c", b=B)

        with nc.Block() as block:
            @block.sync
            def _(sp):
                def load_w(q):
                    sp.dma_start(raw[q], wqkv[:, :, q * PIECE:(q + 1) * PIECE]).then_inc(w_ld[q], 16)

                sp.dma_start(c_t[:], cT).then_inc(c_ld, 16)
                sp.dma_start(adab_t[:], adab).then_inc(small_ld, 16)
                for s in range(2):
                    sp.dma_start(aw01[:, s], ada[:, s]).then_inc(aw_ld[s], 16)
                sp.dma_start(xb[:, 0], xT[:, :, 0:BLK]).then_inc(x_ld[0], 16)
                for j in range(4):
                    sp.dma_start(gain[:, j:j + 1], gains[j].partition_broadcast(P)).then_inc(gain_ld, 16)
                load_w(0)
                load_w(1)
                sp.wait_ge(mod_mm, 1)
                load_w(2)
                sp.dma_start(xb[:, 1], xT[:, :, N:N + BLK]).then_inc(x_ld[1], 16)
                sp.dma_start(bias[:], qkvb.partition_broadcast(P)).then_inc(bias_ld, 16)
                sp.wait_ge(whi_done, 1)
                sp.wait_ge(wlo_done, 1)
                load_w(3)
                sp.wait_ge(mod_mm, 1 + KC)
                sp.dma_start(awn, adan[0]).then_inc(awn_ld, 16)
                sp.dma_start(pb_t[:], pb).then_inc(late_ld, 16)
                sp.dma_start(f2b_t[:], f2b).then_inc(late_ld, 16)
                sp.dma_start(f1b_t[:], f1b).then_inc(late_ld, 16)

                def body(it, first, last):
                    for r in range(B):
                        if not last:
                            sp.wait_ge(xr_done, B * it + r + 1)
                            sp.dma_start(xb[:, r], xT[:, :, bass.ds(r * N + BLK * it + BLK, BLK)]).then_inc(x_ld[r], 16)
                        for t in range(TPB):
                            tt = TPB * (B * it + r) + t
                            if r == 1 and t == TPB - 1 and not last:
                                sp.wait_ge(modn_add, B * it + B)
                                sp.dma_start(awn, adan[bass.ds(it + 1, 1)].rearrange("a p m c -> (a p) m c")
                                             ).then_inc(awn_ld, 16)
                            sp.wait_ge(scale_done, tt + 1)
                            sp.dma_start(qkv_s[bass.ds(r * NT + TPB * it + t, 1)].rearrange("a p c -> (a p) c"),
                                         stage[:, t % 2].rearrange("p a c -> p (a c)")).then_inc(st_dma[t % 2], 16)
                iterate(sp, NIT, body)
                for j in range(2):
                    sp.wait_ge(st_dma[j], 16 * B * N // P // 2)

            @block.gpsimd
            def _(pool):
                pool.memset(ident[:], 0.0).then_inc(setup, 1)
                pool.wait_ge(setup, 1)
                pool.affine_select(out=ident[:], in_=ident[:], compare_op=ALU.not_equal, fill=1.0, base=0,
                                   pattern=[[-1, P]], channel_multiplier=1).then_inc(ident_done, 1)
                for q in range(NP - 1):
                    pool.wait_ge(whi_done, q + 1)
                    cols = slice(q * PIECE, (q + 1) * PIECE)
                    pool.tensor_tensor(w_lo[:, :, cols], raw[q], f32(w_hi[:, :, cols]), ALU.subtract).then_inc(wlo_done, 1)

            def norm_act(act, i):
                act.wait_ge(ss_done, i + 1)
                wait(act, xr_done, i)
                act.activation(rb[:], RB, ACT.Sqrt).then_inc(nrm_done, 1)

            def affine(act, r, m):
                act.activation(tmp[:, m], tmp[:, m], ACT.Identity, bias=mod[:, SHIFT_MSA, m, r:r + 1],
                               scale=mod[:, SCALE_MSA, m, r:r + 1]).then_inc(aff_done, 1)

            def prep_act(act, i, r, part):
                if part == 0:
                    act.wait_ge(x_ld[r], 16 * (i // B + 1) if isinstance(i, int) else 8 * (i - r) + 16)
                    act.wait_ge(hlo_done, i)
                    act.activation(tmp[:], xb[:, r], ACT.Square).then_inc(sq_done, 1)
                    wait(act, qkv_mm, 2 * TPB * (i - 1))
                    act.activation(h_hi[:, r], xb[:, r], ACT.Square).then_inc(sq_done, 1)
                elif part == 1:
                    norm_act(act, i)
                elif part == 2:
                    act.wait_ge(xr_done, i + 1)
                    for m in range(KC):
                        affine(act, r, m)
                else:
                    act.wait_ge(aff_done, KC * (i + 1))
                    act.activation(h_hi[:, r], tmp[:], ACT.Copy).then_inc(hhi_done, 1)

            def reciprocal(dve, i):
                dve.wait_ge(nrm_done, i + 1)
                dve.tensor_scalar(rb[:], rb[:], EPS, None, ALU.max).then_inc(r_max, 1)
                dve.wait_ge(r_max, i + 1)
                dve.reciprocal(rb[:], rb[:]).then_inc(r_rec, 1)
                dve.wait_ge(r_rec, i + 1)
                dve.tensor_scalar(rb[:], rb[:], float(D) ** 0.5, gain[:, 0:1], ALU.mult, ALU.mult).then_inc(r_done, 1)

            def prep_dve(dve, i, r, part):
                if part == 0:
                    dve.wait_ge(sq_done, 2 * i)
                    lows(dve, h_hi[:, r], h_lo[:, r], tmp).then_inc(sqlo_done, 1)
                elif part == 1:
                    reciprocal(dve, i)
                elif part == 2:
                    dve.wait_ge(r_done, i + 1)
                    dve.tensor_tensor(tmp[:], xb[:, r], rb[:].unsqueeze(1).to_broadcast([P, KC, BLK]),
                                      ALU.mult).then_inc(xr_done, 1)
                else:
                    dve.wait_ge(hhi_done, i)
                    lows(dve, h_hi[:, r], h_lo[:, r], tmp).then_inc(hlo_done, 1)

            @block.scalar
            def _(act):
                def split_w(q):
                    act.wait_ge(w_ld[q], 16)
                    act.activation(w_hi[:, :, q * PIECE:(q + 1) * PIECE], raw[q], ACT.Copy).then_inc(whi_done, 1)

                act.wait_ge(c_ld, 16)
                act.activation(c_e[:], c_t[:], ACT.Exp, scale=-1.0).then_inc(c_exp, 1)
                act.wait_ge(c_silu, 1)
                act.activation(warm[:], c_e[:, 0, 0:1], ACT.Sqrt)
                act.wait_ge(cb_mm, 1)
                for b in range(B):
                    act.activation(c_b[:, b, 0:KF * P], ps[:, 6 + b, :], ACT.Copy).then_inc(cb_done, 1)
                act.activation(c_b[:, :, KF * P:D], CT, ACT.Copy).then_inc(cb_done, 1)
                act.wait_ge(x_ld[0], 16)
                for m in range(KC):
                    act.activation(tmp[:, m], xb[:, 0, m], ACT.Square).then_inc(sq0_done, 1)
                    act.activation(h_hi[:, 0, m], xb[:, 0, m], ACT.Square).then_inc(sq0_done, 1)
                split_w(0)
                norm_act(act, 0)
                split_w(1)
                for m in range(KC):
                    act.wait_ge(xr0_done, m + 1) if m < KF else act.wait_ge(xr_done, 1)
                    act.wait_ge(mod_one, m + 1)
                    affine(act, 0, m)
                    act.wait_ge(aff_done, m + 1)
                    act.activation(h_hi[:, 0, m], tmp[:, m], ACT.Copy).then_inc(hhi0_done, 1)
                split_w(2)
                split_w(3)

                def tile(i, t):
                    tt = TPB * i + t
                    act.wait_ge(evac_done, 2 * tt + 2)
                    wait(act, red_done, tt)
                    act.activation(sqb[:], stage[:, t % 2, :, 0:QK], ACT.Square).then_inc(sqt_done, 1)
                    act.wait_ge(red_done, tt + 1)
                    act.activation(rt[:], ssb[:], ACT.Sqrt).then_inc(rt_done, 1)

                def body(it, first, last):
                    for r in range(B):
                        i = B * it + r
                        for t in range(TPB):
                            if not (last and r == 1):
                                prep_act(act, i + 1, 1 - r, t)
                            tile(i, t)
                iterate(act, NIT, body)
                act.wait_ge(modn_add, 2 * NIT)
                for g in (GATE_MSA, GATE_MLP):
                    act.activation(mod[:, g], mod[:, g], ACT.Tanh).then_inc(tanh_done, 1)

            @block.vector
            def _(dve):
                dve.memset(ones32[:], 1.0).then_inc(ones_done, 1)
                dve.wait_ge(ones_done, 1)
                dve.tensor_copy(ones[:], ones32[:]).then_inc(ones_done, 1)
                dve.wait_ge(c_exp, 1)
                dve.tensor_scalar(c_e[:], c_e[:], 1.0, None, ALU.add).then_inc(c_one, 1)
                dve.wait_ge(c_one, 1)
                dve.reciprocal(c_e[:], c_e[:]).then_inc(c_rec, 1)
                dve.wait_ge(c_rec, 1)
                dve.tensor_tensor(c_s[:], c_t[:], c_e[:], ALU.mult).then_inc(c_silu, 1)
                for m in range(KC):
                    dve.wait_ge(sq0_done, 2 * m + 2)
                    mm = low(dve, h_hi[:, 0], h_lo[:, 0], tmp[:, m], m)
                mm.then_inc(sqlo_done, 1)
                dve.wait_ge(gain_ld, 64)
                dve.tensor_scalar(qscale[:], gain[:, 2:3], gain[:, 3:4], float(HD) ** 0.5, ALU.mult,
                                  ALU.mult).then_inc(gain_a, 1)
                dve.wait_ge(gain_a, 1)
                dve.tensor_scalar(bound[:], qscale[:], -1.0, qscale[:, 0:1], ALU.mult, ALU.max).then_inc(gain_c, 1)
                dve.wait_ge(gain_c, 1)
                dve.tensor_scalar(bound[:], bound[:], MAX_FREE, None, ALU.is_gt).then_inc(gain_d, 1)
                dve.wait_ge(gain_d, 1)
                dve.tensor_copy(unbounded[:], bound[:])
                reciprocal(dve, 0)
                dve.wait_ge(r_done, 1)
                dve.wait_ge(small_ld, 16)
                dve.wait_ge(mod_mm, 1)
                dve.tensor_tensor(mod[:, SHIFT_MSA], MOD0, adab_t[:, 0:KC].unsqueeze(2).to_broadcast([P, KC, B]), ALU.add)
                for m in range(KC):
                    dve.tensor_tensor(tmp[:, m], xb[:, 0, m], rb[:], ALU.mult).then_inc(xr0_done if m < KF else xr_done, 1)
                    dve.wait_ge(mod_mm, m + 2)
                    dve.tensor_scalar(mod[:, SCALE_MSA, m], MOD1[m], adab_t[:, KC + m:KC + m + 1], None,
                                      ALU.add).then_inc(mod_add, 1)
                    dve.wait_ge(mod_add, m + 1)
                    dve.tensor_scalar(mod[:, SCALE_MSA, m], mod[:, SCALE_MSA, m], 1.0, None, ALU.add).then_inc(mod_one, 1)
                for m in range(KC):
                    dve.wait_ge(hhi0_done, m + 1)
                    mm = low(dve, h_hi[:, 0], h_lo[:, 0], tmp[:, m], m)
                mm.then_inc(hlo_done, 1)
                dve.wait_ge(wlo_done, 2)
                dve.memset(stage[:, :, :, PW:SW], 0.0)
                dve.wait_ge(whi_done, NP)
                cols = slice((NP - 1) * PIECE, NP * PIECE)
                dve.tensor_tensor(w_lo[:, :, cols], raw[NP - 1], f32(w_hi[:, :, cols]), ALU.subtract).then_inc(wlo_last, 1)
                dve.wait_ge(bias_ld, 16)
                dve.wait_ge(cb_done, 3)

                def scale(tt, t):
                    dve.wait_ge(rt_done, tt + 1)
                    dve.tensor_scalar(rt[:], rt[:], EPS, None, ALU.max).then_inc(t_max, 1)
                    dve.wait_ge(t_max, tt + 1)
                    dve.reciprocal(rt[:], rt[:]).then_inc(t_rec, 1)
                    dve.wait_ge(t_rec, tt + 1)
                    dve.tensor_scalar(rt[:, :, 0:2], rt[:, :, 0:2], qscale[:, 0:1], None, ALU.mult).then_inc(t_scl, 1)
                    dve.wait_ge(t_scl, tt + 1)
                    qk = stage[:, t % 2, :, 0:QK].rearrange("p a (h d) -> p a h d", d=HD)
                    dve.tensor_tensor(qk, qk, rt[:].unsqueeze(3).to_broadcast([P, PAIRS, 4, HD]),
                                      ALU.mult).then_inc(scale_done, 1)

                def evac(tt, i, t, h, early):
                    dve.wait_ge(qkv_mm, 2 * tt + h + 1)
                    if not early:
                        dve.wait_ge(st_dma[t % 2], 16 * (2 * i + t // 2))
                    dve.tensor_tensor(stage[:, t % 2, 4 * h:4 * h + 4, 0:PW].rearrange("p (n a) c -> p n a c", a=2),
                                      ps[:, 2 * h:2 * h + 2, 0:PIECE].rearrange("p n (a c) -> p n a c", a=2),
                                      bias[:, 2 * h * PIECE:(2 * h + 2) * PIECE].rearrange("p (n a c) -> p n a c",
                                                                                           n=2, a=2),
                                      ALU.add).then_inc(evac_done, 1)

                def dot(it, i, r, m):
                    if m == 0 and r == 0:
                        dve.wait_ge(awn_ld, 16 * (it + 1))
                    if m == 0:
                        wait(dve, modn_add, i - 1)
                    wait(dve, dot_done, KC * i + m)
                    dve.tensor_tensor_reduce(prod, awn[:, m], c_b[:, r], 1.0, 0.0, ALU.mult, ALU.add,
                                             dots[:, r, m:m + 1]).then_inc(dot_done, 1)
                    if m == KC - 1:
                        dve.wait_ge(dot_done, KC * (i + 1))
                        out = mod[:, 2 + it, :, r] if isinstance(it, int) else (
                            mod[:, bass.ds(it + 2, 1), :, r].rearrange("p a m -> p (a m)"))
                        dve.tensor_tensor(out, dots[:, r], adab_t[:, bass.ds(KC * it + 2 * KC, KC)],
                                          ALU.add).then_inc(modn_add, 1)

                DOTS = ((0,), (), (1, 2), (3, 4))

                def body(it, first, last):
                    for r in range(B):
                        i = B * it + r
                        more = not (last and r == 1)
                        for t in range(TPB):
                            tt, early = TPB * i + t, first and r == 0 and t < 2
                            evac(tt, i, t, 0, early)
                            if not (first and r == 0 and t == 0):
                                scale(tt - 1, t + 1)
                            if more and t >= 1:
                                prep_dve(dve, i + 1, 1 - r, t)
                            evac(tt, i, t, 1, early)
                            if more and t == 0:
                                prep_dve(dve, i + 1, 1 - r, 0)
                            dve.wait_ge(sqt_done, tt + 1)
                            dve.tensor_reduce(ssb[:], sqb[:].rearrange("p a (h d) -> p a h d", d=HD), AX.X,
                                              ALU.add).then_inc(red_done, 1)
                            for m in DOTS[t]:
                                dot(it, i, r, m)
                iterate(dve, NIT, body)
                scale(B * N // P - 1, 1)
                dve.tensor_scalar(mod[:, SCALE_MLP], mod[:, SCALE_MLP], 1.0, None, ALU.add).then_inc(modn_one, 1)
                dve.wait_ge(late_ld, 48)
                dve.wait_ge(tanh_done, 2)
                for j, (g, b_t) in enumerate(((GATE_MSA, pb_t), (GATE_MLP, f2b_t))):
                    dve.tensor_tensor(gate_b[:, j], mod[:, g], b_t[:].unsqueeze(2).to_broadcast([P, KC, B]),
                                      ALU.mult).then_inc(mod_done, 1)

            @block.tensor
            def _(pe):
                def modulate(s, m):
                    out = MOD1[m] if s else MOD0[:, m]
                    for k in range(KC):
                        rows = slice(0, P if k < KF else TL)
                        mm = pe.matmul(out, aw01[rows, s, k, m * P:(m + 1) * P], c_s[rows, k],
                                       start=k == 0, stop=k == KC - 1)
                    return mm

                def sum_squares(i, r):
                    pe.wait_ge(sqlo_done, i + 1)
                    wait(pe, nrm_done, i)
                    for k in range(KC):
                        for part in (h_hi, h_lo)[:2 if k < KF else 1]:
                            mm = pe.matmul(RB, ones[:], part[:, r, k], start=k == 0 and part is h_hi, stop=k == KF)
                    mm.then_inc(ss_done, 1)

                pe.wait_ge(c_silu, 1)
                pe.wait_ge(ident_done, 1)
                for b in range(B):
                    for k in range(KC):
                        rows = slice(0, P if k < KF else TL)
                        out = ps[:, 6 + b, k * P:(k + 1) * P] if k < KF else CT[:, b]
                        mm = pe.matmul(out, c_s[rows, k, b:b + 1].to_broadcast([P if k < KF else TL, P]),
                                       ident[rows, rows], start=True, stop=True)
                mm.then_inc(cb_mm, 1)
                pe.wait_ge(aw_ld[0], 16)
                for m in range(KC):
                    mm = modulate(0, m)
                mm.then_inc(mod_mm, 1)
                pe.wait_ge(aw_ld[1], 16)
                for m in range(KC):
                    if m == 1:
                        pe.wait_ge(ones_done, 2)
                        sum_squares(0, 0)
                    modulate(1, m).then_inc(mod_mm, 1)

                def tile(i, r, t, first, last):
                    tt = TPB * i + t
                    cols = slice(t * P, (t + 1) * P)
                    for h in range(2):
                        if first and r == 0 and t == 0:
                            pe.wait_ge(wlo_done, h + 2)
                            if h == 1:
                                pe.wait_ge(wlo_last, 1)
                        else:
                            pe.wait_ge(evac_done, 2 * tt + h - 1)
                        for k in range(KC):
                            for n, (w, a) in enumerate(passes(k, w_hi, w_lo, h_hi, h_lo)):
                                for q in (2 * h, 2 * h + 1):
                                    mm = pe.matmul(ps[:, q, 0:PIECE], a[:, r, k, cols], w[:, k, q * PIECE:(q + 1) * PIECE],
                                                   start=k == 0 and n == 0, stop=k == KF and n == 1)
                        mm.then_inc(qkv_mm, 1)
                        if t == 1 and h == 0 and not (last and r == 1):
                            sum_squares(i + 1, 1 - r)

                def body(it, first, last):
                    for r in range(B):
                        i = B * it + r
                        pe.wait_ge(hlo_done, i + 1)
                        for t in range(TPB):
                            tile(i, r, t, first, last)
                iterate(pe, NIT, body)


def attention_phase(nc, ctx, sb, ps, qkv_s, o_s, w2, ident, unbounded, w2_hi, w2_lo):
    C = NIT
    with ExitStack() as st:
        def sem(name):
            return ctx.enter_context(nc.semaphore("b_" + name))

        pair = sb(st, "pair", [P, B, NT, SW])
        kT = sb(st, "kT", [PKW, B, 2, N], F32R)
        qT = sb(st, "qT", [PKW, 2, 2, BLK], F32R)
        vp = sb(st, "vp", [P, B, NT, VW])
        prob = sb(st, "prob", [P, 4, 2 * BLK])
        qpack = sb(st, "qpack", [P, TPB, 2, PKS], F32R)
        kpack = sb(st, "kpack", [P, TPB, 2, PKS], F32R)
        osb = sb(st, "osb", [VW, BLK])
        rl = sb(st, "rl", [P, TPB, 2])
        ofin = sb(st, "ofin", [P, 2, TPB, 2, HD])
        w2_raw = sb(st, "w2_raw", [P, 2, D])
        cst = sb(st, "cst", [P, TPB, 2, 2])
        mx_hi = sb(st, "mx_hi", [P, 1], F32R)
        mx = sb(st, "mx", [P, 4])

        pair_ld = [sem(f"pair_ld{j}") for j in range(B)]
        w2_ld = [sem(f"w2_ld{j}") for j in range(2)]
        vzero, cst_done, rows_done = sem("vzero"), sem("cst_done"), sem("rows_done")
        q_hi, q_pack, k_hi, k_pack = sem("q_hi"), sem("q_pack"), sem("k_hi"), sem("k_pack")
        tp, qT_done, kT_done, v_done = sem("tp"), sem("qT_done"), sem("kT_done"), sem("v_done")
        s_mm, exp_done, pv_mm = sem("s_mm"), sem("exp_done"), sem("pv_mm")
        o_evac, ot_mm, rl_done, o_fin = sem("o_evac"), sem("ot_mm"), sem("rl_done"), sem("o_fin")
        o_dma = [sem(f"o_dma{j}") for j in range(2)]
        w2hi_done, w2lo_done = sem("w2hi_done"), sem("w2lo_done")

        TP, OT = ps[0:PKW, 6, :], ps[:, 7, :].rearrange("p (t c) -> p t c", t=TPB)
        NU = B * PAIRS * C

        m_ld, m_st = sem("m_ld"), sem("m_st")
        m_kt, m_kx, m_q, m_qt, m_qx = sem("m_kt"), sem("m_kx"), sem("m_q"), sem("m_qt"), sem("m_qx")
        m_s, m_max, m_neg, m_hi, m_lo, m_out = sem("m_s"), sem("m_max"), sem("m_neg"), sem("m_hi"), sem("m_lo"), sem("m_out")
        kx = prob[0:HD, 0:2].rearrange("p a b -> p (a b)")
        qt_tile = prob[:, 2, 0:2 * HD]
        qx = osb[0:HD, 0:P]
        SC = ps[:, 0:4, :].rearrange("p a b -> p (a b)")
        QX = ps[0:2 * HD, 6, 0:P]

        def row_maxima_sync(sp):
            def load(it, r):
                sp.dma_start(pair[:, 0], qkv_s[r * NT:(r + 1) * NT, :, bass.ds(SW * it, SW)]
                             .rearrange("t p c -> p t c")).then_inc(m_ld, 16)

            def store(it, r):
                n = it + PAIRS * r
                sp.wait_ge(m_out, 2 * NT * n + 2 * NT)
                sp.dma_start(qkv_s[r * NT:(r + 1) * NT, :, bass.ds(SW * it + PW, SW - PW)]
                             .rearrange("t p c -> p t c"), pair[:, 0, :, PW:SW]).then_inc(m_st, 16)
                sp.wait_ge(m_st, 16 * n + 16)
            for r in range(B):
                load(0, r)
                with sp.Fori(0, PAIRS - 1) as it:
                    store(it, r)
                    load(it + 1, r)
                store(PAIRS - 1, r)

        def row_maxima_tensor(pe):
            for r in range(B):
                with pe.Fori(0, PAIRS) as it:
                    n = it + PAIRS * r
                    pe.wait_ge(m_ld, 16 * n + 16)
                    for h in range(2):
                        pe.wait_ge(m_max, NT * (2 * n + h) + 1)
                        for t in range(NT):
                            mm = pe.transpose(SC[0:2 * HD, t * P:(t + 1) * P], pair[:, 0, t, (2 + h) * HD:(4 + h) * HD], ident[:])
                        mm.then_inc(m_kt, 1)
                        with pe.Fori(0, NT) as qt:
                            j = NT * (2 * n + h) + qt
                            pe.wait_ge(m_q, j + 1)
                            pe.transpose(QX, qt_tile, ident[:]).then_inc(m_qt, 1)
                            pe.wait_ge(m_qx, j + 1)
                            pe.wait_ge(m_kx, 2 * n + h + 1)
                            pe.wait_ge(m_max, j + 1)
                            for b in range(4):
                                mm = pe.matmul(ps[:, b, :], qx, kx[:, b * BLK:(b + 1) * BLK], start=True, stop=True)
                            mm.then_inc(m_s, 1)

        def row_maxima_vector(dve):
            dve.memset(mx[:], 0.0).then_inc(m_max, 1)
            for r in range(B):
                with dve.Fori(0, PAIRS) as it:
                    n = it + PAIRS * r
                    for h in range(2):
                        dve.wait_ge(m_kt, 2 * n + h + 1)
                        dve.tensor_copy(kx, SC[0:HD]).then_inc(m_kx, 1)
                        with dve.Fori(0, NT) as qt:
                            j = NT * (2 * n + h) + qt
                            dve.tensor_copy(qt_tile, pair[:, 0, bass.ds(qt, 1), h * HD:(2 + h) * HD]
                                            .rearrange("p a c -> p (a c)")).then_inc(m_q, 1)
                            dve.wait_ge(m_qt, j + 1)
                            dve.tensor_copy(qx, QX[0:HD]).then_inc(m_qx, 1)
                            dve.wait_ge(m_s, j + 1)
                            dve.tensor_reduce(mx[:, 0:1], SC, AX.X, ALU.max).then_inc(m_max, 1)
                            dve.wait_ge(m_max, j + 2)
                            dve.tensor_scalar(mx[:, 1:2], mx[:, 0:1], -1.0, None, ALU.mult).then_inc(m_neg, 1)
                            dve.wait_ge(m_neg, j + 1)
                            dve.tensor_copy(mx_hi[:], mx[:, 1:2]).then_inc(m_hi, 1)
                            dve.wait_ge(m_hi, j + 1)
                            dve.tensor_copy(mx[:, 2:3], f32(mx_hi[:]))
                            dve.tensor_tensor(mx[:, 3:4], mx[:, 1:2], f32(mx_hi[:]), ALU.subtract).then_inc(m_lo, 1)
                            dve.wait_ge(m_lo, j + 1)
                            dve.tensor_copy(pair[:, 0, bass.ds(qt, 1), PW + 2 * h:PW + 2 * h + 2]
                                            .rearrange("p a c -> p (a c)"), mx[:, 2:4]).then_inc(m_out, 1)

        with nc.Block() as block:
            @block.sync
            def _(sp):
                def load(it, r):
                    sp.dma_start(pair[:, r], qkv_s[r * NT:(r + 1) * NT, :, bass.ds(SW * it, SW)]
                                 .rearrange("t p c -> p t c")).then_inc(pair_ld[r], 16)

                def store(it, r, c):
                    u = C * (B * it + r) + c
                    sp.wait_ge(o_fin, u + 1)
                    sp.dma_start(o_s[r * NT + TPB * c:r * NT + TPB * (c + 1), :, bass.ds(2 * HD * it, 2 * HD)]
                                 .rearrange("t p c -> p t c"),
                                 ofin[:, c % 2].rearrange("p t h d -> p t (h d)")).then_inc(o_dma[c % 2], 16)

                with sp.If(sp.value_load(unbounded[0:1, 0:1], min_val=0, max_val=1) > 0):
                    row_maxima_sync(sp)
                load(0, 0)
                load(0, 1)

                def body(it, first, last):
                    for r in range(B):
                        g = B * it + r
                        for c in range(C):
                            if c == 2 and not last:
                                sp.wait_ge(q_pack, 4 * g + 4)
                                sp.wait_ge(v_done, 4 * g + 4)
                                load(it + 1, r)
                            store(it, r, c)
                iterate(sp, PAIRS, body)
                for j in range(2):
                    sp.wait_ge(o_dma[j], 16 * NU // 2)

            @block.gpsimd
            def _(pool):
                pool.memset(vp[:], 0.0).then_inc(vzero, 1)
                pool.wait_ge(vzero, 1)
                for r in range(B):
                    for h in range(2):
                        pool.memset(vp[:, r, :, 64 * h + HD:64 * h + HD + 1], 1.0).then_inc(vzero, 1)
                pool.wait_ge(vzero, 5)
                for k in range(2):
                    pool.dma_start(w2_raw[:, k], w2[:, k]).then_inc(w2_ld[k], 16)

                def take_v(it, r, first):
                    g = B * it + r
                    pool.wait_ge(pair_ld[r], 16 * (it + 1))
                    if not first:
                        pool.wait_ge(pv_mm, NT * C * (g - 1))
                    for h in range(2):
                        c = QK + h * HD
                        for half in (slice(0, NT // 2), slice(NT // 2, NT)):
                            pool.tensor_scalar(vp[:, r, half, 64 * h:64 * h + HD], pair[:, r, half, c:c + HD], 1.0, None,
                                               ALU.mult).then_inc(v_done, 1)

                take_v(0, 0, True)
                take_v(0, 1, True)
                for k in range(FC):
                    pool.wait_ge(w2_ld[k % 2], 16 * (k // 2 + 1))
                    pool.tensor_scalar(w2_hi[:, k, 0:D], w2_raw[:, k % 2], 1.0, None, ALU.mult).then_inc(w2hi_done, 1)
                    pool.wait_ge(w2hi_done, k + 1)
                    pool.tensor_tensor(w2_lo[:, k], w2_raw[:, k % 2, 0:KF * P], f32(w2_hi[:, k, 0:KF * P]), ALU.subtract)
                    pool.tensor_tensor(w2_hi[:, k, D:DP], w2_raw[:, k % 2, KF * P:D], f32(w2_hi[:, k, KF * P:D]),
                                       ALU.subtract).then_inc(w2lo_done, 1)
                    if k + 2 < FC:
                        pool.wait_ge(w2lo_done, k + 1)
                        pool.dma_start(w2_raw[:, k % 2], w2[:, k + 2]).then_inc(w2_ld[k % 2], 16)
                for it in range(1, PAIRS):
                    for r in range(B):
                        take_v(it, r, False)

            @block.scalar
            def _(act):
                def body(it, first, last):
                    for r in range(B):
                        for c in range(C):
                            for kt in range(NT):
                                s = NT * (C * (B * it + r) + c) + kt
                                act.wait_ge(s_mm, s + 1)
                                if not (first and r == 0 and c == 0 and kt < 4):
                                    act.wait_ge(pv_mm, s - 3)
                                j = kt % 2
                                act.activation(prob[:, kt % 4], ps[:, 2 * j:2 * j + 2, :].rearrange("p a b -> p (a b)"),
                                               ACT.Exp).then_inc(exp_done, 1)
                iterate(act, PAIRS, body)

            @block.vector
            def _(dve):
                dve.memset(cst[:], 1.0).then_inc(cst_done, 1)
                dve.wait_ge(cst_done, 1)
                dve.tensor_copy(kpack[:, :, :, 3 * HD:PKW], cst[:]).then_inc(rows_done, 1)

                def pack_q(it, r, c):
                    n = C * (B * it + r) + c
                    dve.wait_ge(pair_ld[r], 16 * (it + 1))
                    src = pair[:, r, TPB * c:TPB * (c + 1), 0:2 * HD].rearrange("p t (h d) -> p t h d", d=HD)
                    dve.tensor_copy(qpack[:, :, :, 0:HD], src).then_inc(q_hi, 1)
                    dve.tensor_copy(qpack[:, :, :, HD:2 * HD], src)
                    dve.tensor_copy(qpack[:, :, :, 3 * HD:PKW],
                                    pair[:, r, TPB * c:TPB * (c + 1), PW:SW].rearrange("p t (h d) -> p t h d", d=2))
                    dve.wait_ge(q_hi, n + 1)
                    dve.tensor_tensor(qpack[:, :, :, 2 * HD:3 * HD], src, f32(qpack[:, :, :, 0:HD]), ALU.subtract).then_inc(q_pack, 1)

                def pack_k(it, r, c):
                    n = C * (B * it + r) + c
                    dve.wait_ge(pair_ld[r], 16 * (it + 1))
                    src = pair[:, r, TPB * c:TPB * (c + 1), 2 * HD:4 * HD].rearrange("p t (h d) -> p t h d", d=HD)
                    dve.tensor_copy(kpack[:, :, :, 0:HD], src).then_inc(k_hi, 1)
                    dve.tensor_copy(kpack[:, :, :, 2 * HD:3 * HD], src)
                    dve.wait_ge(k_hi, n + 1)
                    dve.tensor_tensor(kpack[:, :, :, HD:2 * HD], src, f32(kpack[:, :, :, 0:HD]), ALU.subtract).then_inc(k_pack, 1)

                def q_out(slot, h, group):
                    dve.wait_ge(tp, group + 1)
                    dve.tensor_copy(qT[:, slot, h], TP).then_inc(qT_done, 1)

                def k_out(r, h, c, group):
                    dve.wait_ge(tp, group + 1)
                    dve.tensor_copy(kT[:, r, h, BLK * c:BLK * (c + 1)], TP).then_inc(kT_done, 1)

                def take_o(u, slot, early):
                    dve.wait_ge(pv_mm, NT * (u + 1))
                    if not early:
                        dve.wait_ge(ot_mm, u)
                    dve.tensor_copy(osb[:], ps[0:VW, 4 + slot, :]).then_inc(o_evac, 1)

                def finish_o(u, slot, early):
                    dve.wait_ge(ot_mm, u + 1)
                    dve.reciprocal(rl[:], OT[:, :, HD:HD + 65:64]).then_inc(rl_done, 1)
                    dve.wait_ge(rl_done, u + 1)
                    if not early:
                        dve.wait_ge(o_dma[slot], 8 * (u - slot))
                    for h in range(2):
                        mul = dve.tensor_tensor(ofin[:, slot, :, h], OT[:, :, 64 * h:64 * h + HD],
                                                rl[:, :, h:h + 1].to_broadcast([P, TPB, HD]), ALU.mult)
                    mul.then_inc(o_fin, 1)

                with dve.If(dve.value_load(unbounded[0:1, 0:1], min_val=0, max_val=1) > 0):
                    row_maxima_vector(dve)
                for c in range(C):
                    if c:
                        dve.wait_ge(tp, 2 * c)
                    pack_k(0, 0, c)
                    for h in range(2):
                        k_out(0, h, c, 2 * c + h)
                pack_q(0, 0, 0)
                for h in range(2):
                    q_out(0, h, 2 * C + h)
                pack_k(0, 1, 0)
                pack_q(0, 0, 1)

                def body(it, first, last):
                    for r in range(B):
                        final = last and r == 1
                        for c in range(C):
                            u = C * (B * it + r) + c
                            group = 2 * C + 2 + 4 * u if not final else 2 * C + 2 + 4 * (NU - C) + 2 * c
                            start = first and r == 0 and c == 0
                            if not start:
                                take_o(u - 1, (c + 1) % 2, first and r == 0 and c == 1)
                            more_q = not (final and c == C - 1)
                            if more_q:
                                q_out((c + 1) % 2, 0, group)
                            if not start:
                                finish_o(u - 1, (c + 1) % 2, first and r == 0 and c <= 2)
                            if more_q:
                                q_out((c + 1) % 2, 1, group + 1)
                            if not (final and c >= C - 2):
                                if c < C - 2:
                                    pack_q(it, r, c + 2)
                                else:
                                    pack_q(it + r, 1 - r, c + 2 - C)
                            if not final:
                                for h in range(2):
                                    k_out(1 - r, h, c, group + 2 + h)
                                if c < C - 1:
                                    pack_k(it + r, 1 - r, c + 1)
                                elif not (last and r == 0):
                                    pack_k(it + 1, r, 0)
                iterate(dve, PAIRS, body)
                take_o(NU - 1, 1, False)
                finish_o(NU - 1, 1, False)

            @block.tensor
            def _(pe):
                def turn(pack, h, t, mark):
                    mm = pe.transpose(TP[:, t * P:(t + 1) * P], f32(pack[:, t, h, 0:PKW]), ident[:])
                    if mark:
                        mm.then_inc(tp, 1)

                def scores(r, c, kt, u):
                    if kt == 0:
                        pe.wait_ge(qT_done, 2 * (u + 1))
                    if c == 0 and kt % TPB == 0:
                        pe.wait_ge(kT_done, 2 * u + 2 * (kt // TPB + 1))
                    j = kt % 2
                    for h in range(2):
                        mm = pe.matmul(ps[:, 2 * j + h, :], kT[:, r, h, kt * P:(kt + 1) * P], qT[:, c % 2, h],
                                       start=True, stop=True)
                    mm.then_inc(s_mm, 1)

                with pe.If(pe.value_load(unbounded[0:1, 0:1], min_val=0, max_val=1) > 0):
                    row_maxima_tensor(pe)
                for c in range(C):
                    pe.wait_ge(k_pack, c + 1)
                    if c == 0:
                        pe.wait_ge(rows_done, 1)
                    for h in range(2):
                        wait(pe, kT_done, 2 * c + h)
                        for t in range(TPB):
                            turn(kpack, h, t, t == TPB - 1)
                pe.wait_ge(q_pack, 1)
                for h in range(2):
                    if h == 0:
                        pe.wait_ge(kT_done, 2 * C)
                    else:
                        pe.wait_ge(qT_done, 1)
                    for t in range(TPB):
                        turn(qpack, h, t, t == TPB - 1)
                for kt in range(2):
                    scores(0, 0, kt, 0)

                def turn_o(u):
                    pe.wait_ge(o_evac, u + 1)
                    if not (isinstance(u, int) and u == 0):
                        pe.wait_ge(o_fin, u)
                    for t in range(TPB):
                        mm = pe.transpose(OT[:, t, 0:VW], osb[:, t * P:(t + 1) * P], ident[0:VW, 0:VW])
                    mm.then_inc(ot_mm, 1)

                def body(it, first, last):
                    for r in range(B):
                        final = last and r == 1
                        for c in range(C):
                            u = C * (B * it + r) + c
                            for kt0 in range(0, NT, 2):
                                steps = (kt0, kt0 + 1)
                                pe.wait_ge(exp_done, NT * u + kt0 + 2)
                                for kt in steps:
                                    if kt + 2 < NT:
                                        scores(r, c, kt + 2, u)
                                    elif c + 1 < C:
                                        scores(r, c + 1, kt + 2 - NT, u + 1)
                                    elif not final:
                                        scores(1 - r, 0, kt + 2 - NT, u + 1)
                                for kt in steps:
                                    group, t = divmod(kt, TPB)
                                    if group < 2:
                                        if not (final and c == C - 1):
                                            if t == 0:
                                                if group == 0:
                                                    pe.wait_ge(q_pack, u + 2)
                                                    pe.wait_ge(kT_done, 2 * C + 2 * u if not final else 2 * C + 2 * (NU - C))
                                                pe.wait_ge(qT_done, 2 + 2 * u + group)
                                            turn(qpack, group, t, t == TPB - 1)
                                    elif not final:
                                        if t == 0:
                                            if group == 2:
                                                pe.wait_ge(k_pack, u + C + 1)
                                                pe.wait_ge(qT_done, 4 + 2 * u)
                                            else:
                                                pe.wait_ge(kT_done, 2 * C + 2 * u + 1)
                                        turn(kpack, group - 2, t, t == TPB - 1)
                                if kt0 == 2 and not (first and r == 0 and c == 0):
                                    turn_o(u - 1)
                                if kt0 == 0:
                                    if c == 0:
                                        pe.wait_ge(v_done, 4 * (B * it + r) + 4)
                                    if not (first and r == 0 and c < 2):
                                        pe.wait_ge(o_evac, u - 1)
                                O = ps[:, 4 + c % 2, :]
                                for kt in steps:
                                    j = kt % 4
                                    pe.matmul(O[0:64], vp[:, r, kt, 0:64], prob[:, j, 0:BLK], start=kt == 0, stop=kt == NT - 1)
                                    pe.matmul(O[64:VW], vp[:, r, kt, 64:VW], prob[:, j, BLK:2 * BLK], start=kt == 0,
                                              stop=kt == NT - 1).then_inc(pv_mm, 1)
                iterate(pe, PAIRS, body)
                turn_o(NU - 1)


def proj_phase(nc, ctx, sb, ps, o_s, xT, wp, x1_s, ident, mod, gate_b):
    with ExitStack() as st:
        def sem(name):
            return ctx.enter_context(nc.semaphore("c_" + name))

        ob = sb(st, "ob", [P, B, TPB, DP])
        xb = sb(st, "cxb", [P, B, KC, BLK])
        wp_raw = sb(st, "wp_raw", [P, KC, DP])
        wp_hi = sb(st, "wp_hi", [P, KC, DP], F32R)
        wp_lo = sb(st, "wp_lo", [P, KC, DP], F32R)
        o_hi = sb(st, "o_hi", [P, B, KC, BLK], F32R)
        o_lo = sb(st, "o_lo", [P, B, KF, BLK], F32R)
        gated = sb(st, "gated", [P, 2, BLK])
        wp_ld = sem("wp_ld")
        o_ld = [sem(f"o_ld{j}") for j in range(B)]
        x_ld = [sem(f"x_ld{j}") for j in range(B)]
        whi_done, wlo_done = sem("whi_done"), sem("wlo_done")
        tp, hi_done, lo_done = sem("tp"), sem("hi_done"), sem("lo_done")
        proj_mm, gate_done, x1_done = sem("proj_mm"), sem("gate_done"), sem("x1_done")
        x1_dma = [sem(f"x1_dma{j}") for j in range(B)]
        with nc.Block() as block:
            @block.sync
            def _(sp):
                sp.dma_start(wp_raw[:], wp).then_inc(wp_ld, 16)

                def load_o(it, r):
                    tiles = o_s[bass.ds(r * NT + TPB * it, TPB)].rearrange("t p c -> p t c")
                    sp.dma_start(ob[:, r, :, 0:D], tiles).then_inc(o_ld[r], 16)
                    sp.dma_start(ob[:, r, :, D:DP], tiles[:, :, KF * P:D]).then_inc(o_ld[r], 16)

                def load_x(it, r):
                    sp.dma_start(xb[:, r], xT[:, :, bass.ds(r * N + BLK * it, BLK)]).then_inc(x_ld[r], 16)

                for r in range(B):
                    load_o(0, r)
                    load_x(0, r)

                def body(it, first, last):
                    for r in range(B):
                        i = B * it + r
                        if not last:
                            sp.wait_ge(tp, KC * (i + 1))
                            load_o(it + 1, r)
                        sp.wait_ge(x1_done, KC * (i + 1))
                        sp.dma_start(x1_s[:, :, bass.ds(r * N + BLK * it, BLK)], xb[:, r]).then_inc(x1_dma[r], 16)
                        if not last:
                            sp.wait_ge(x1_dma[r], 16 * (it + 1))
                            load_x(it + 1, r)
                iterate(sp, NIT, body)
                for r in range(B):
                    sp.wait_ge(x1_dma[r], 16 * NIT)

            @block.scalar
            def _(act):
                act.wait_ge(wp_ld, 16)
                act.activation(wp_hi[:], wp_raw[:], ACT.Copy).then_inc(whi_done, 1)

                def turn_hi(i, r, k):
                    act.wait_ge(tp, KC * i + k + 1)
                    act.activation(o_hi[:, r, k], ps[:, (r + k) % 2, :], ACT.Copy).then_inc(hi_done, 1)

                for k in range(KC):
                    turn_hi(0, 0, k)

                def body(it, first, last):
                    for r in range(B):
                        i = B * it + r
                        for m in range(KC):
                            j = (KC * r + m) % 2
                            act.wait_ge(proj_mm, KC * i + m + 1)
                            if not (first and r == 0 and m < 2):
                                act.wait_ge(x1_done, KC * i + m - 1)
                            act.activation(gated[:, j], ps[:, 2 + j, :], ACT.Identity, bias=gate_b[:, 0, m, r:r + 1],
                                           scale=mod[:, GATE_MSA, m, r:r + 1]).then_inc(gate_done, 1)
                            if not (last and r == 1):
                                turn_hi(i + 1, 1 - r, m)
                iterate(act, NIT, body)

            @block.vector
            def _(dve):
                dve.wait_ge(whi_done, 1)
                dve.tensor_tensor(wp_lo[:], wp_raw[:], f32(wp_hi[:]), ALU.subtract).then_inc(wlo_done, 1)

                def turn_lo(i, r, k):
                    dve.wait_ge(hi_done, KC * i + k + 1)
                    low(dve, o_hi[:, r], o_lo[:, r], ps[:, (r + k) % 2, :], k).then_inc(lo_done, 1)

                for k in range(KC):
                    turn_lo(0, 0, k)

                def body(it, first, last):
                    for r in range(B):
                        i = B * it + r
                        for m in range(KC):
                            j = (KC * r + m) % 2
                            dve.wait_ge(gate_done, KC * i + m + 1)
                            if m == 0:
                                dve.wait_ge(x_ld[r], 16 * (it + 1))
                            dve.tensor_tensor(xb[:, r, m], xb[:, r, m], gated[:, j], ALU.add).then_inc(x1_done, 1)
                            if not (last and r == 1):
                                turn_lo(i + 1, 1 - r, m)
                iterate(dve, NIT, body)

            @block.tensor
            def _(pe):
                def turn(it, i, r, k, early):
                    if k == 0:
                        pe.wait_ge(o_ld[r], 32 * (it + 1))
                    if not (early and k < 2):
                        pe.wait_ge(lo_done, KC * i + k - 1)
                    for t in range(TPB):
                        mm = pe.transpose(ps[:, (r + k) % 2, t * P:(t + 1) * P], ob[:, r, t, k * P:(k + 1) * P], ident[:])
                    mm.then_inc(tp, 1)

                for k in range(KC):
                    turn(0, 0, 0, k, True)
                pe.wait_ge(wlo_done, 1)

                def body(it, first, last):
                    for r in range(B):
                        i = B * it + r
                        pe.wait_ge(lo_done, KC * (i + 1))
                        for m in range(KC):
                            j = (KC * r + m) % 2
                            if not (first and r == 0 and m < 2):
                                pe.wait_ge(gate_done, KC * i + m - 1)
                            for k in range(KC):
                                for n, (w, a) in enumerate(passes(k, wp_hi, wp_lo, o_hi, o_lo)):
                                    mm = pe.matmul(ps[:, 2 + j, :], w[:, k, m * P:(m + 1) * P], a[:, r, k],
                                                   start=k == 0 and n == 0, stop=k == KF and n == 1)
                            mm.then_inc(proj_mm, 1)
                            if not (last and r == 1):
                                turn(it + r, i + 1, 1 - r, m, False)
                iterate(pe, NIT, body)


def mlp_phase(nc, ctx, sb, ps, x1_s, w1, outT, ones, mod, gate_b, gain, f1b_t, w2_hi, w2_lo):
    K_SQ, K_SS, K_REC, K_H = 3, 8, 9, 12
    with ExitStack() as st:
        def sem(name):
            return ctx.enter_context(nc.semaphore("d_" + name))

        x1 = sb(st, "x1", [P, B, KC, BLK])
        tmp = sb(st, "dtmp", [P, KC, BLK])
        rb = sb(st, "drb", [P, BLK])
        h_hi = sb(st, "dh_hi", [P, B, KC, BLK], F32R)
        h_lo = sb(st, "dh_lo", [P, B, KF, BLK], F32R)
        w1_raw = sb(st, "w1_raw", [P, 2, KC, P])
        w1_hi = sb(st, "w1_hi", [P, 2, KC, P], F32R)
        w1_lo = sb(st, "w1_lo", [P, 2, KC, P], F32R)
        act32 = sb(st, "act32", [P, 2, BLK])
        a_hi = sb(st, "a_hi", [P, 2, BLK], F32R)
        a_lo = sb(st, "a_lo", [P, 2, BLK], F32R)
        gated = sb(st, "dgated", [P, 2, BLK])
        tail = sb(st, "tail", [TL, BLK])

        x_ld = [sem(f"x_ld{j}") for j in range(B)]
        w1_ld = [sem(f"w1_ld{j}") for j in range(2)]
        w1hi_done, w1lo_done = sem("w1hi_done"), sem("w1lo_done")
        sq_done, sqhi_done, sqlo_done, ss_done = sem("sq_done"), sem("sqhi_done"), sem("sqlo_done"), sem("ss_done")
        nrm_done, r_max, r_rec, r_done, xr_done = sem("nrm_done"), sem("r_max"), sem("r_rec"), sem("r_done"), sem("xr_done")
        aff_done, hhi_done, hlo_done = sem("aff_done"), sem("hhi_done"), sem("hlo_done")
        fc1_mm, gelu_done, alo_done, fc2_mm = sem("fc1_mm"), sem("gelu_done"), sem("alo_done"), sem("fc2_mm")
        gate_done, tail_done, out_done = sem("gate_done"), sem("tail_done"), sem("out_done")
        out_dma = [sem(f"out_dma{j}") for j in range(B)]
        NB = B * NIT
        RB = ps[:, 7, :]

        with nc.Block() as block:
            @block.sync
            def _(sp):
                def load_w1(k, slot, count):
                    wait(sp, w1lo_done, count - 1)
                    wait(sp, w1hi_done, count - 1)
                    sp.dma_start(w1_raw[:, slot], w1[k]).then_inc(w1_ld[slot], 16)

                sp.dma_start(x1[:, 0], x1_s[:, :, 0:BLK]).then_inc(x_ld[0], 16)
                load_w1(0, 0, 0)
                load_w1(1, 1, 0)
                sp.dma_start(x1[:, 1], x1_s[:, :, N:N + BLK]).then_inc(x_ld[1], 16)

                def body(it, first, last):
                    for r in range(B):
                        i = B * it + r
                        for k in range(FC):
                            if not (last and r == 1 and k + 2 >= FC):
                                load_w1((k + 2) % FC, k % 2, FC * i + k + 2)
                            if k == 1 and not (first and r == 0) and not (last and r == 1):
                                sp.wait_ge(out_dma[1 - r], 16 * (it + r))
                                sp.dma_start(x1[:, 1 - r], x1_s[:, :, bass.ds((1 - r) * N + BLK * (it + r), BLK)]
                                             ).then_inc(x_ld[1 - r], 16)
                iterate(sp, NIT, body)
                for r in range(B):
                    sp.wait_ge(out_dma[r], 16 * NIT)

            def act_square(act, it, i, r, m):
                if m == 0:
                    act.wait_ge(x_ld[r], 16 * (it + 1))
                    wait(act, hlo_done, KC * i)
                    wait(act, fc1_mm, FC * (i - 1))
                act.activation(tmp[:, m], x1[:, r, m], ACT.Square).then_inc(sq_done, 1)
                act.activation(h_hi[:, r, m], x1[:, r, m], ACT.Square).then_inc(sqhi_done, 1)

            def act_norm(act, i):
                act.wait_ge(ss_done, i + 1)
                wait(act, xr_done, KC * i)
                act.activation(rb[:], RB, ACT.Sqrt).then_inc(nrm_done, 1)

            def act_h(act, i, r, m):
                act.wait_ge(xr_done, KC * i + m + 1)
                act.activation(tmp[:, m], tmp[:, m], ACT.Identity, bias=mod[:, SHIFT_MLP, m, r:r + 1],
                               scale=mod[:, SCALE_MLP, m, r:r + 1]).then_inc(aff_done, 1)
                act.wait_ge(aff_done, KC * i + m + 1)
                act.activation(h_hi[:, r, m], tmp[:, m], ACT.Copy).then_inc(hhi_done, 1)

            @block.scalar
            def _(act):
                def split_w1(slot, count, it, fours, k):
                    act.wait_ge(w1_ld[slot], 16 * fours)
                    wait(act, fc1_mm, count - 1)
                    act.activation(w1_hi[:, slot], w1_raw[:, slot], ACT.Copy).then_inc(w1hi_done, 1)

                for m in range(KC):
                    act_square(act, 0, 0, 0, m)
                split_w1(0, 0, 0, 1, 0)
                split_w1(1, 1, 0, 1, 1)
                act_norm(act, 0)
                for m in range(KC):
                    act_h(act, 0, 0, m)

                def gelu(i, k, early):
                    j, slot = FC * i + k, k % 2
                    act.wait_ge(fc1_mm, j + 1)
                    if not early:
                        act.wait_ge(alo_done, j - 1)
                    act.activation(act32[:, slot], ps[:, 5 + slot, :], ACT.Gelu_apprx_tanh, bias=f1b_t[:, k:k + 1])
                    if not early:
                        act.wait_ge(fc2_mm, j - 1)
                    act.activation(a_hi[:, slot], ps[:, 5 + slot, :], ACT.Gelu_apprx_tanh,
                                   bias=f1b_t[:, k:k + 1]).then_inc(gelu_done, 1)

                def gates(i, r, early):
                    act.wait_ge(fc2_mm, FC * (i + 1))
                    for m in range(KC):
                        n = KC * i + m
                        if not (early and m < 2):
                            act.wait_ge(out_done, n - 1)
                        act.activation(gated[:, (r + m) % 2], ps[:, m, :], ACT.Identity,
                                       bias=gate_b[:, 1, m, r:r + 1], scale=mod[:, GATE_MLP, m, r:r + 1]).then_inc(gate_done, 1)

                def body(it, first, last):
                    for r in range(B):
                        i = B * it + r
                        more = not (last and r == 1)
                        for k in range(FC):
                            gelu(i, k, first and r == 0 and k < 2)
                            if k == 0 and not (first and r == 0):
                                gates(i - 1, 1 - r, first and r == 1)
                            if k == 1 and not (first and r == 0):
                                act.wait_ge(out_done, KC * i)
                                act.dma_start(outT[:, :, bass.ds((1 - r) * N + BLK * (it + r - 1), BLK)],
                                              x1[:, 1 - r]).then_inc(out_dma[1 - r], 16)
                            if more or k + 2 < FC:
                                j = FC * i + k + 2
                                split_w1(k % 2, j, it, FC // 2 * i + k // 2 + 2, k)
                            if more:
                                if K_SQ <= k < K_SQ + KC:
                                    act_square(act, it + r, i + 1, 1 - r, k - K_SQ)
                                if k == K_SS:
                                    act_norm(act, i + 1)
                                if K_H <= k < K_H + KC:
                                    act_h(act, i + 1, 1 - r, k - K_H)
                iterate(act, NIT, body)
                gates(NB - 1, 1, False)
                act.wait_ge(out_done, KC * NB)
                act.dma_start(outT[:, :, 2 * N - BLK:2 * N], x1[:, 1]).then_inc(out_dma[1], 16)

            @block.vector
            def _(dve):
                def square_lo(i, r, m):
                    dve.wait_ge(sqhi_done, KC * i + m + 1)
                    low(dve, h_hi[:, r], h_lo[:, r], tmp[:, m], m).then_inc(sqlo_done, 1)

                def reciprocal(i, part):
                    half = slice(part * BLK // 2, (part + 1) * BLK // 2)
                    if part == 0:
                        dve.wait_ge(nrm_done, i + 1)
                        dve.tensor_scalar(rb[:], rb[:], EPS, None, ALU.max).then_inc(r_max, 1)
                        dve.wait_ge(r_max, i + 1)
                    dve.reciprocal(rb[:, half], rb[:, half]).then_inc(r_rec, 1)
                    if part == 1:
                        dve.wait_ge(r_rec, 2 * i + 2)
                        dve.tensor_scalar(rb[:], rb[:], float(D) ** 0.5, gain[:, 1:2], ALU.mult, ALU.mult).then_inc(r_done, 1)

                def normed(i, r, m):
                    if m == 0:
                        dve.wait_ge(r_done, i + 1)
                    dve.tensor_tensor(tmp[:, m], x1[:, r, m], rb[:], ALU.mult).then_inc(xr_done, 1)

                def h_low(i, r, m):
                    dve.wait_ge(hhi_done, KC * i + m + 1)
                    low(dve, h_hi[:, r], h_lo[:, r], tmp[:, m], m).then_inc(hlo_done, 1)

                def split_w1(slot, count):
                    dve.wait_ge(w1hi_done, count + 1)
                    dve.tensor_tensor(w1_lo[:, slot], w1_raw[:, slot], f32(w1_hi[:, slot]), ALU.subtract).then_inc(w1lo_done, 1)

                for m in range(KC):
                    square_lo(0, 0, m)
                split_w1(0, 0)
                split_w1(1, 1)
                reciprocal(0, 0)
                reciprocal(0, 1)
                for m in range(KC):
                    normed(0, 0, m)
                for m in range(KC):
                    h_low(0, 0, m)

                def add_x1(i, r):
                    for m in range(KF):
                        dve.wait_ge(gate_done, KC * i + m + 1)
                        dve.tensor_tensor(x1[:, r, m], x1[:, r, m], gated[:, (r + m) % 2], ALU.add).then_inc(out_done, 1)
                    dve.wait_ge(gate_done, KC * (i + 1))
                    dve.tensor_copy(tail[:], gated[TL:P, r]).then_inc(tail_done, 1)
                    dve.tensor_tensor(x1[0:TL, r, KF], x1[0:TL, r, KF], gated[0:TL, r], ALU.add).then_inc(tail_done, 1)
                    dve.wait_ge(tail_done, 2 * i + 2)
                    dve.tensor_tensor(x1[0:TL, r, KF], x1[0:TL, r, KF], tail[:], ALU.add).then_inc(out_done, 1)

                def body(it, first, last):
                    for r in range(B):
                        i = B * it + r
                        more = not (last and r == 1)
                        for k in range(FC):
                            j, slot = FC * i + k, k % 2
                            dve.wait_ge(gelu_done, j + 1)
                            dve.tensor_tensor(a_lo[:, slot], act32[:, slot], f32(a_hi[:, slot]), ALU.subtract).then_inc(alo_done, 1)
                            if k == 0 and not (first and r == 0):
                                add_x1(i - 1, 1 - r)
                            if more or k + 2 < FC:
                                split_w1(slot, j + 2)
                            if more:
                                if K_SQ <= k < K_SQ + KC:
                                    square_lo(i + 1, 1 - r, k - K_SQ)
                                if k in (K_REC, K_REC + 1):
                                    reciprocal(i + 1, k - K_REC)
                                if K_REC + 2 <= k < K_REC + 2 + KC:
                                    normed(i + 1, 1 - r, k - K_REC - 2)
                                if K_H <= k < K_H + KC:
                                    h_low(i + 1, 1 - r, k - K_H)
                iterate(dve, NIT, body)
                add_x1(NB - 1, 1)

            @block.tensor
            def _(pe):
                def sum_squares(i, r):
                    pe.wait_ge(sqlo_done, KC * (i + 1))
                    wait(pe, nrm_done, i)
                    for k in range(KC):
                        for part in (h_hi, h_lo)[:2 if k < KF else 1]:
                            mm = pe.matmul(RB, ones[:], part[:, r, k], start=k == 0 and part is h_hi, stop=k == KF)
                    mm.then_inc(ss_done, 1)

                def fc1(i, r, k, early):
                    j, slot = FC * i + k, k % 2
                    if k == 0:
                        pe.wait_ge(hlo_done, KC * (i + 1))
                    pe.wait_ge(w1lo_done, j + 1)
                    if not early:
                        pe.wait_ge(gelu_done, j - 1)
                    for c in range(KC):
                        for n, (w, a) in enumerate(passes(c, w1_hi, w1_lo, h_hi, h_lo)):
                            mm = pe.matmul(ps[:, 5 + slot, :], w[:, slot, c], a[:, r, c], start=c == 0 and n == 0,
                                           stop=c == KF and n == 1)
                    mm.then_inc(fc1_mm, 1)

                sum_squares(0, 0)
                fc1(0, 0, 0, True)

                def body(it, first, last):
                    for r in range(B):
                        i = B * it + r
                        more = not (last and r == 1)
                        for k in range(FC):
                            j, slot = FC * i + k, k % 2
                            if k + 1 < FC:
                                fc1(i, r, k + 1, first and r == 0 and k == 0)
                            elif more:
                                fc1(i + 1, 1 - r, 0, False)
                            if k == K_SS and more:
                                sum_squares(i + 1, 1 - r)
                            pe.wait_ge(alo_done, j + 1)
                            for m in range(KC):
                                if k == 0 and not (first and r == 0):
                                    pe.wait_ge(gate_done, KC * (i - 1) + m + 1)
                                parts = ((w2_hi, a_hi), (w2_lo, a_hi), (w2_hi, a_lo)) if m < KF else (
                                    (w2_hi, a_hi), (w2_hi, a_lo))
                                for n, (w, a) in enumerate(parts):
                                    mm = pe.matmul(ps[:, m, :], w[:, k, m * P:(m + 1) * P], a[:, slot],
                                                   start=k == 0 and n == 0, stop=k == FC - 1 and n == len(parts) - 1)
                            mm.then_inc(fc2_mm, 1)
                iterate(pe, NIT, body)


def columns(a):
    return np.concatenate([a, a[..., KF * P:]], axis=-1)


def rows(a):
    a = columns(a.swapaxes(0, -1)).swapaxes(0, -1)
    return np.ascontiguousarray(a.reshape((KC, P) + a.shape[1:]).swapaxes(0, 1))


def by_pair(a):
    return a.reshape((3, PAIRS, 2 * HD) + a.shape[1:]).swapaxes(0, 1).reshape(a.shape)


def kernel(x, cond_1152, L0_cond_g1, L0_cond_g2, L0_cond_qkv_w, L0_cond_qkv_b, L0_cond_qg, L0_cond_kg, L0_cond_proj_w,
           L0_cond_proj_b, L0_cond_fc1_w, L0_cond_fc1_b, L0_cond_fc2_w, L0_cond_fc2_b, L0_cond_ada_w, L0_cond_ada_b):
    import concourse.bacc as bacc
    from concourse.bass_utils import run_bass_kernel_spmd

    n = np.asarray
    ada = n(L0_cond_ada_w).reshape(6, D, D)
    f2b = rows(n(L0_cond_fc2_b))
    f2b[TL:, KF] = 0
    arrays = {
        "xT": rows(n(x).reshape(B * N, D).T),
        "cT": rows(n(cond_1152).T),
        "ada": np.ascontiguousarray(rows(columns(ada[:2].transpose(2, 0, 1))).swapaxes(1, 2)).reshape(P, 2, KC, DP),
        "adan": np.stack([rows(a) for a in ada[2:]]),
        "adab": np.ascontiguousarray(rows(n(L0_cond_ada_b).reshape(6, D).T).swapaxes(1, 2).reshape(P, 6 * KC)),
        "wqkv": rows(by_pair(n(L0_cond_qkv_w)).T),
        "qkvb": np.ascontiguousarray(by_pair(n(L0_cond_qkv_b))),
        "wp": rows(columns(n(L0_cond_proj_w).T)),
        "pb": rows(n(L0_cond_proj_b)),
        "w1": np.ascontiguousarray(rows(n(L0_cond_fc1_w).T).reshape(P, KC, FC, P).transpose(2, 0, 1, 3)),
        "f1b": np.ascontiguousarray(n(L0_cond_fc1_b).reshape(FC, P).T),
        "w2": np.ascontiguousarray(n(L0_cond_fc2_w).T.reshape(FC, P, D).transpose(1, 0, 2)),
        "f2b": f2b,
        "g1": n(L0_cond_g1), "g2": n(L0_cond_g2), "qg": n(L0_cond_qg), "kg": n(L0_cond_kg),
    }
    nc = bacc.Bacc("TRN2", target_bir_lowering=False, num_devices=1)
    ap = {k: nc.dram_tensor(k, a.shape, F32, kind="ExternalInput").ap() for k, a in arrays.items()}
    outT = nc.dram_tensor("outT", (P, KC, B * N), F32, kind="ExternalOutput").ap()
    build(nc, ap["xT"], ap["cT"], ap["ada"], ap["adan"], ap["adab"], ap["wqkv"], ap["qkvb"], ap["wp"], ap["pb"], ap["w1"], ap["f1b"],
          ap["w2"], ap["f2b"], [ap["g1"], ap["g2"], ap["qg"], ap["kg"]], outT)
    out = run_bass_kernel_spmd(nc, [arrays], core_ids=[0]).results[0]["outT"]
    return np.ascontiguousarray(out.transpose(1, 0, 2).reshape(DP, B * N)[:D].T).reshape(B, N, D)
```
